# Optimizing a Trainium2 kernel written in Bass

```python
import numpy as np
import jax
import jax.numpy as jnp

def _softmax(x, axis=-1):
    return jax.nn.softmax(x, axis=axis)

def _gelu(x):
    return jax.nn.gelu(x, approximate=True)

def _silu(x):
    return jax.nn.silu(x)

def _sigmoid(x):
    return jax.nn.sigmoid(x)

def _layernorm(x, axis=-1, eps=1e-05):
    m = jnp.mean(x, axis=axis, keepdims=True)
    v = jnp.var(x, axis=axis, keepdims=True)
    return (x - m) / jnp.sqrt(v + eps)

def _scatter_add(tgt, idx, src, axis=0):
    return tgt.at[idx].add(src)

def _segment_sum(src, seg, n):
    return jax.ops.segment_sum(src, seg, n)
kernel_name = 'mk_decoder_postln_d1_seqx_r4_0f63d9'

def setup_inputs(seed: int=0):
    np.random.seed(seed)
    _w = jnp.asarray

    def _rec_inputs():
        import jax
        import jax.numpy as jnp
        _rk = jax.random.key(seed)
        x = 2.818e-05 + 1 * jax.random.normal(jax.random.fold_in(_rk, 1), (4, 512, 512), jnp.float32)
        _lenS = 512 - jax.random.randint(jax.random.fold_in(_rk, 7), (4,), 0, max(1, 512 // 4) + 1, jnp.int32)
        _lenS2 = 512 - jax.random.randint(jax.random.fold_in(_rk, 8), (4,), 0, max(1, 512 // 4) + 1, jnp.int32)
        _ctx_1024P = jax.random.normal(jax.random.fold_in(_rk, 11), (4, 16, 256), jnp.float32)
        _ctx_1024c = jax.random.dirichlet(jax.random.fold_in(_rk, 511), 0.3 * jnp.ones((16,), jnp.float32), (4, 512))
        _ctx_1024t = jnp.einsum('bsk,bkd->bsd', _ctx_1024c, _ctx_1024P)
        _ctx_1024t = _ctx_1024t * jax.lax.rsqrt(jnp.mean(jnp.square(_ctx_1024t)) + 1e-12) * 0.953939
        ctx_1024 = 7.22013e-05 + 1.00017 * (_ctx_1024t + 0.3 * jax.random.normal(jax.random.fold_in(_rk, 611), (4, 512, 256), jnp.float32))
        return (x, ctx_1024)
    x, ctx_1024 = _rec_inputs()

    def _L0_attn_setup():
        import math
        import jax, jax.numpy as jnp
        import numpy as np
        EMBED_DIM = 512
        NUM_HEADS = 16
        HEAD_DIM = EMBED_DIM // NUM_HEADS
        CHUNK = 128
        RMS_EPS = 1e-05

        def _build_slopes(n):

            def pow2(n):
                start = 2.0 ** (-2.0 ** (-(math.log2(n) - 3)))
                return [start * start ** i for i in range(n)]
            if math.log2(n).is_integer():
                s = pow2(n)
            else:
                closest = 2 ** math.floor(math.log2(n))
                s = pow2(closest) + pow2(2 * closest)[0::2][:n - closest]
            return jnp.asarray(s, dtype=jnp.float32)

        def _rotary(x_BTHD, offset=0):
            T, D = (x_BTHD.shape[1], x_BTHD.shape[-1])
            freq = (1.0 / 1024.0) ** jnp.linspace(0.0, 1.0, D // 4, dtype=jnp.float32)
            freq = jnp.concatenate([freq, jnp.zeros(D // 4, dtype=jnp.float32)])
            t = jnp.arange(offset, offset + T, dtype=jnp.float32)
            theta = t[:, None] * freq[None, :]
            cos = jnp.cos(theta)[None, :, None, :]
            sin = jnp.sin(theta)[None, :, None, :]
            x1, x2 = jnp.split(x_BTHD.astype(jnp.float32), 2, axis=-1)
            y1 = x1 * cos + x2 * sin
            y2 = -x1 * sin + x2 * cos
            return jnp.concatenate([y1, y2], axis=-1).astype(x_BTHD.dtype)

        def _lightning_attn(q, k, v, slopes):
            B, H, T, D = q.shape
            C = CHUNK
            NC = T // C
            r = jnp.exp(-slopes)
            i = jnp.arange(C, dtype=jnp.float32)
            q_decay = r[:, None] ** (i[None, :] + 1.0)
            k_decay = r[:, None] ** (C - 1.0 - i[None, :])
            diff = i[:, None] - i[None, :]
            mask = diff >= 0
            dmask = jnp.where(mask[None], r[:, None, None] ** jnp.where(mask, diff, 0.0)[None], 0.0)
            r_C = r ** float(C)

            def reshape_chunks(x):
                return x.reshape(B, H, NC, C, D).transpose(2, 0, 1, 3, 4)
            qc, kc, vc = (reshape_chunks(q), reshape_chunks(k), reshape_chunks(v))

            def step(kv, qkv):
                qi, ki, vi = qkv
                inter = jnp.einsum('bhcd,bhde->bhce', qi * q_decay[None, :, :, None], kv)
                scores = jnp.einsum('bhcd,bhsd->bhcs', qi, ki) * dmask[None]
                intra = jnp.einsum('bhcs,bhse->bhce', scores, vi)
                kv_new = r_C[None, :, None, None] * kv + jnp.einsum('bhcd,bhce->bhde', ki * k_decay[None, :, :, None], vi)
                return (kv_new, inter + intra)
            kv0 = jnp.zeros((B, H, D, D), dtype=q.dtype)
            _, out = jax.lax.scan(step, kv0, (qc, kc, vc))
            return out.transpose(1, 2, 0, 3, 4).reshape(B, H, T, D)

        def _rms_norm(x, w):
            var = jnp.mean(jnp.square(x), axis=-1, keepdims=True)
            return x * jax.lax.rsqrt(var + RMS_EPS) * w
        key = jax.random.key(seed)
        ks = jax.random.split(key, 6)
        sc = 1.0 / math.sqrt(EMBED_DIM)
        return {'x': jax.random.normal(ks[0], (4, 1024, EMBED_DIM), dtype=jnp.float32), 'Wq': jax.random.normal(ks[1], (EMBED_DIM, EMBED_DIM), dtype=jnp.float32) * sc, 'Wk': jax.random.normal(ks[2], (EMBED_DIM, EMBED_DIM), dtype=jnp.float32) * sc, 'Wv': jax.random.normal(ks[3], (EMBED_DIM, EMBED_DIM), dtype=jnp.float32) * sc, 'Wo': jax.random.normal(ks[4], (EMBED_DIM, EMBED_DIM), dtype=jnp.float32) * sc, 'rms_w': jnp.ones((EMBED_DIM,), dtype=jnp.float32)}
    _L0_attn_all = _L0_attn_setup()
    _L0_attn_in = {k: v for k, v in _L0_attn_all.items() if k in ('Wq', 'Wk', 'Wv', 'Wo', 'rms_w')}
    del _L0_attn_all

    def _L0_xattn_setup():
        import jax, jax.numpy as jnp
        import numpy as np
        B_, L_, D_MODEL = (4, 512, 256)
        D_STATE, D_CONV, EXPAND = (16, 4, 2)
        D_INNER = EXPAND * D_MODEL
        DT_RANK = (D_MODEL + 15) // 16

        def silu(x):
            return x * jax.nn.sigmoid(x)
        key = jax.random.key(seed)
        ks = jax.random.split(key, 10)
        f32 = jnp.float32
        hidden_states = jax.random.normal(ks[0], (B_, L_, D_MODEL), dtype=f32)
        z = jax.random.normal(ks[1], (B_, D_INNER, L_), dtype=f32)
        in_proj_w = jax.random.normal(ks[2], (D_INNER, D_MODEL), dtype=f32) * 0.02
        conv_w = jax.random.normal(ks[3], (D_INNER, 1, D_CONV), dtype=f32) * 0.1
        conv_b = jax.random.normal(ks[4], (D_INNER,), dtype=f32) * 0.02
        x_proj_w = jax.random.normal(ks[5], (DT_RANK + 2 * D_STATE, D_INNER), dtype=f32) * 0.02
        dt_proj_w = jax.random.uniform(ks[6], (D_INNER, DT_RANK), dtype=f32, minval=-DT_RANK ** (-0.5), maxval=DT_RANK ** (-0.5))
        dt = jnp.exp(jax.random.uniform(ks[7], (D_INNER,), dtype=f32, minval=np.log(0.001), maxval=np.log(0.1)))
        dt_proj_b = jnp.log(jnp.expm1(dt))
        A_log = jnp.log(jnp.broadcast_to(jnp.arange(1, D_STATE + 1, dtype=f32), (D_INNER, D_STATE)))
        D = jnp.ones((D_INNER,), f32)
        return {'hidden_states': hidden_states, 'z': z, 'in_proj_w': in_proj_w, 'conv_w': conv_w, 'conv_b': conv_b, 'x_proj_w': x_proj_w, 'dt_proj_w': dt_proj_w, 'dt_proj_b': dt_proj_b, 'A_log': A_log, 'D': D}
    _L0_xattn_all = _L0_xattn_setup()
    _L0_xattn_in = {k: v for k, v in _L0_xattn_all.items() if k in ('in_proj_w', 'conv_w', 'conv_b', 'x_proj_w', 'dt_proj_w', 'dt_proj_b', 'A_log', 'D')}
    del _L0_xattn_all

    def _L0_ffn_setup():
        import jax, jax.numpy as jnp
        import numpy as np
        TOP_K = 8
        CAPACITY = 256
        key = jax.random.key(seed)
        k1, k2, k3, k4 = jax.random.split(key, 4)
        B, S, H, E, I = (2, 256, 512, 64, 192)
        hidden_states = jax.random.normal(k1, (B, S, H), dtype=jnp.float32)
        router_weight = jax.random.normal(k2, (E, H), dtype=jnp.float32) * 0.02
        gate_up_proj = jax.random.normal(k3, (E, H, 2 * I), dtype=jnp.float32) * 0.02
        down_proj = jax.random.normal(k4, (E, I, H), dtype=jnp.float32) * 0.02
        return {'hidden_states': hidden_states, 'router_weight': router_weight, 'gate_up_proj': gate_up_proj, 'down_proj': down_proj}
    _L0_ffn_all = _L0_ffn_setup()
    _L0_ffn_in = {k: v for k, v in _L0_ffn_all.items() if k in ('router_weight', 'gate_up_proj', 'down_proj')}
    del _L0_ffn_all
    return {'x': x, 'ctx_1024': ctx_1024, 'L0_attn_Wq': _L0_attn_in['Wq'], 'L0_attn_Wk': _L0_attn_in['Wk'], 'L0_attn_Wv': _L0_attn_in['Wv'], 'L0_attn_Wo': _L0_attn_in['Wo'], 'L0_attn_rms_w': _L0_attn_in['rms_w'], 'L0_xattn_in_proj_w': _L0_xattn_in['in_proj_w'], 'L0_xattn_conv_w': _L0_xattn_in['conv_w'], 'L0_xattn_conv_b': _L0_xattn_in['conv_b'], 'L0_xattn_x_proj_w': _L0_xattn_in['x_proj_w'], 'L0_xattn_dt_proj_w': _L0_xattn_in['dt_proj_w'], 'L0_xattn_dt_proj_b': _L0_xattn_in['dt_proj_b'], 'L0_xattn_A_log': _L0_xattn_in['A_log'], 'L0_xattn_D': _L0_xattn_in['D'], 'L0_ffn_router_weight': _L0_ffn_in['router_weight'], 'L0_ffn_gate_up_proj': _L0_ffn_in['gate_up_proj'], 'L0_ffn_down_proj': _L0_ffn_in['down_proj']}

def reference(x, ctx_1024, L0_attn_Wq, L0_attn_Wk, L0_attn_Wv, L0_attn_Wo, L0_attn_rms_w, L0_xattn_in_proj_w, L0_xattn_conv_w, L0_xattn_conv_b, L0_xattn_x_proj_w, L0_xattn_dt_proj_w, L0_xattn_dt_proj_b, L0_xattn_A_log, L0_xattn_D, L0_ffn_router_weight, L0_ffn_gate_up_proj, L0_ffn_down_proj):
    import jax
    import jax.numpy as jnp

    def _L0_attn_ref(x, Wq, Wk, Wv, Wo, rms_w):
        import math
        import jax, jax.numpy as jnp
        import numpy as np
        EMBED_DIM = 512
        NUM_HEADS = 16
        HEAD_DIM = EMBED_DIM // NUM_HEADS
        CHUNK = 128
        RMS_EPS = 1e-05

        def _build_slopes(n):

            def pow2(n):
                start = 2.0 ** (-2.0 ** (-(math.log2(n) - 3)))
                return [start * start ** i for i in range(n)]
            if math.log2(n).is_integer():
                s = pow2(n)
            else:
                closest = 2 ** math.floor(math.log2(n))
                s = pow2(closest) + pow2(2 * closest)[0::2][:n - closest]
            return jnp.asarray(s, dtype=jnp.float32)

        def _rotary(x_BTHD, offset=0):
            T, D = (x_BTHD.shape[1], x_BTHD.shape[-1])
            freq = (1.0 / 1024.0) ** jnp.linspace(0.0, 1.0, D // 4, dtype=jnp.float32)
            freq = jnp.concatenate([freq, jnp.zeros(D // 4, dtype=jnp.float32)])
            t = jnp.arange(offset, offset + T, dtype=jnp.float32)
            theta = t[:, None] * freq[None, :]
            cos = jnp.cos(theta)[None, :, None, :]
            sin = jnp.sin(theta)[None, :, None, :]
            x1, x2 = jnp.split(x_BTHD.astype(jnp.float32), 2, axis=-1)
            y1 = x1 * cos + x2 * sin
            y2 = -x1 * sin + x2 * cos
            return jnp.concatenate([y1, y2], axis=-1).astype(x_BTHD.dtype)

        def _lightning_attn(q, k, v, slopes):
            B, H, T, D = q.shape
            C = CHUNK
            NC = T // C
            r = jnp.exp(-slopes)
            i = jnp.arange(C, dtype=jnp.float32)
            q_decay = r[:, None] ** (i[None, :] + 1.0)
            k_decay = r[:, None] ** (C - 1.0 - i[None, :])
            diff = i[:, None] - i[None, :]
            mask = diff >= 0
            dmask = jnp.where(mask[None], r[:, None, None] ** jnp.where(mask, diff, 0.0)[None], 0.0)
            r_C = r ** float(C)

            def reshape_chunks(x):
                return x.reshape(B, H, NC, C, D).transpose(2, 0, 1, 3, 4)
            qc, kc, vc = (reshape_chunks(q), reshape_chunks(k), reshape_chunks(v))

            def step(kv, qkv):
                qi, ki, vi = qkv
                inter = jnp.einsum('bhcd,bhde->bhce', qi * q_decay[None, :, :, None], kv)
                scores = jnp.einsum('bhcd,bhsd->bhcs', qi, ki) * dmask[None]
                intra = jnp.einsum('bhcs,bhse->bhce', scores, vi)
                kv_new = r_C[None, :, None, None] * kv + jnp.einsum('bhcd,bhce->bhde', ki * k_decay[None, :, :, None], vi)
                return (kv_new, inter + intra)
            kv0 = jnp.zeros((B, H, D, D), dtype=q.dtype)
            _, out = jax.lax.scan(step, kv0, (qc, kc, vc))
            return out.transpose(1, 2, 0, 3, 4).reshape(B, H, T, D)

        def _rms_norm(x, w):
            var = jnp.mean(jnp.square(x), axis=-1, keepdims=True)
            return x * jax.lax.rsqrt(var + RMS_EPS) * w
        B, T, E = x.shape
        H, D = (NUM_HEADS, HEAD_DIM)
        q = (x @ Wq).reshape(B, T, H, D)
        k = (x @ Wk).reshape(B, T, H, D)
        v = (x @ Wv).reshape(B, T, H, D)
        q = _rotary(q)
        k = _rotary(k)
        q, k, v = (t.transpose(0, 2, 1, 3) for t in (q, k, v))
        slopes = _build_slopes(H)
        attn = _lightning_attn(q, k, v, slopes)
        attn = attn.transpose(0, 2, 1, 3).reshape(B, T, E)
        attn = _rms_norm(attn, rms_w)
        return attn @ Wo

    def _L0_xattn_ref(hidden_states, z, in_proj_w, conv_w, conv_b, x_proj_w, dt_proj_w, dt_proj_b, A_log, D):
        import jax, jax.numpy as jnp
        import numpy as np
        B_, L_, D_MODEL = (4, 512, 256)
        D_STATE, D_CONV, EXPAND = (16, 4, 2)
        D_INNER = EXPAND * D_MODEL
        DT_RANK = (D_MODEL + 15) // 16

        def silu(x):
            return x * jax.nn.sigmoid(x)
        Bsz, L, _ = hidden_states.shape
        d_inner, _, d_conv = conv_w.shape
        dt_rank = dt_proj_w.shape[1]
        d_state = A_log.shape[1]
        x = jnp.einsum('bld,ed->bel', hidden_states, in_proj_w)
        xc = jax.lax.conv_general_dilated(x, conv_w, window_strides=(1,), padding=[(d_conv - 1, 0)], feature_group_count=d_inner, dimension_numbers=('NCH', 'OIH', 'NCH'))
        x = silu(xc + conv_b[None, :, None])
        x_dbl = jnp.einsum('bdl,ed->bel', x, x_proj_w)
        dt_low, Bm, Cm = jnp.split(x_dbl, [dt_rank, dt_rank + d_state], axis=1)
        dt = jnp.einsum('brl,dr->bdl', dt_low, dt_proj_w)
        dt = jax.nn.softplus(dt + dt_proj_b[None, :, None])
        A = -jnp.exp(A_log)
        dt_t = jnp.moveaxis(dt, -1, 0)
        B_t = jnp.moveaxis(Bm, -1, 0)
        C_t = jnp.moveaxis(Cm, -1, 0)
        u_t = jnp.moveaxis(x, -1, 0)

        def step(state, inp):
            d, b, c, u = inp
            dA = jnp.exp(d[..., None] * A)
            state = state * dA + (d * u)[..., None] * b[:, None, :]
            y = jnp.einsum('bdn,bn->bd', state, c)
            return (state, y)
        state0 = jnp.zeros((Bsz, d_inner, d_state), x.dtype)
        _, ys = jax.lax.scan(step, state0, (dt_t, B_t, C_t, u_t))
        y = jnp.moveaxis(ys, 0, 2)
        y = y + D[None, :, None] * x
        y = y * silu(z)
        return jnp.swapaxes(y, 1, 2)

    def _L0_ffn_ref(hidden_states, router_weight, gate_up_proj, down_proj):
        import jax, jax.numpy as jnp
        import numpy as np
        TOP_K = 8
        CAPACITY = 256
        B, S, H = hidden_states.shape
        E = router_weight.shape[0]
        K, C = (TOP_K, CAPACITY)
        x = hidden_states.reshape(-1, H)
        logits = x @ router_weight.T
        probs = jax.nn.softmax(logits, axis=-1)
        topw, topi = jax.lax.top_k(probs, K)
        topw = topw / jnp.sum(topw, axis=-1, keepdims=True)
        flat_e = topi.reshape(-1)
        oh = jax.nn.one_hot(flat_e, E, dtype=jnp.int32)
        pos = jnp.take_along_axis(jnp.cumsum(oh, axis=0), flat_e[:, None], axis=1)[:, 0] - 1
        x_rep = jnp.repeat(x, K, axis=0)
        xe = jnp.zeros((E, C, H), x.dtype).at[flat_e, pos].set(x_rep, mode='drop')
        gu = jnp.einsum('ech,ehf->ecf', xe, gate_up_proj)
        g, u = jnp.split(gu, 2, axis=-1)
        h = jax.nn.silu(g) * u
        ye = jnp.einsum('eci,eih->ech', h, down_proj)
        valid = pos < C
        y_flat = jnp.where(valid[:, None], ye[flat_e, jnp.minimum(pos, C - 1)], 0.0)
        y = jnp.sum(y_flat.reshape(-1, K, H) * topw.reshape(-1, K)[..., None], axis=1)
        return y.reshape(B, S, H)
    x = _layernorm(x + _L0_attn_ref(x, L0_attn_Wq, L0_attn_Wk, L0_attn_Wv, L0_attn_Wo, L0_attn_rms_w), axis=-1)
    x = _layernorm(x + _L0_xattn_ref(ctx_1024, x, L0_xattn_in_proj_w, L0_xattn_conv_w, L0_xattn_conv_b, L0_xattn_x_proj_w, L0_xattn_dt_proj_w, L0_xattn_dt_proj_b, L0_xattn_A_log, L0_xattn_D), axis=-1)
    x = _layernorm(x + _L0_ffn_ref(x, L0_ffn_router_weight, L0_ffn_gate_up_proj, L0_ffn_down_proj), axis=-1)
    return x

_drawn_inputs = setup_inputs


def setup_inputs(seed=0):
    import zlib

    import numpy as np

    out = dict(_drawn_inputs(seed))
    spreads = {'L0_attn_rms_w': (1.0, 0.2), 'L0_xattn_D': (1.0, 0.6)}
    factors = {'ctx_1024': 2.907,
     'L0_xattn_in_proj_w': 2.905,
     'L0_xattn_conv_w': 2.962,
     'L0_xattn_conv_b': 8.0,
     'L0_xattn_x_proj_w': 8.0,
     'L0_xattn_dt_proj_w': 8.0,
     'L0_xattn_dt_proj_b': 8.0,
     'L0_xattn_A_log': 8.0,
     'L0_ffn_router_weight': 5.363,
     'L0_ffn_gate_up_proj': 4.851,
     'L0_ffn_down_proj': 4.851}
    for name, (base, spread) in spreads.items():
        noise = np.random.default_rng([zlib.crc32(name.encode()), seed]).standard_normal(out[name].shape)
        drawn = base * np.exp(spread * noise) if base else spread * noise
        out[name] = jnp.asarray(drawn.astype(out[name].dtype))
    for name, factor in factors.items():
        out[name] = (out[name] * factor).astype(out[name].dtype)
    return out
```

```python
from contextlib import ExitStack

import numpy as np

import concourse.bass as bass
from concourse import mybir

F32 = mybir.dt.float32
I32 = mybir.dt.int32
ALU = mybir.AluOpType
ACT = mybir.ActivationFunctionType
AX = mybir.AxisListType

P = 128
B, T, D = 4, 512, 512
NT = T // P
KD = D // P
HEADS, HD = 16, 32
GROUPS = D // P
HPG = HEADS // GROUPS
ROT = HD // 4
CTX = 256
KC = CTX // P
INNER, STATE, RANK, TAPS = 512, 16, 16, 4
MI = INNER // P
NG = 4
EXPERTS, TOPK, CAP, HID = 64, 8, 256, 192
CJ = CAP // P
SLOTS = EXPERTS * CAP
NTOK = B * T
TILES = NTOK // P
EPS = 1e-5

C_ID = 0
C_TRI = C_ID + P
C_BD = C_TRI + P
C_ROTA = C_BD + P
C_ROTB = C_ROTA + NT * 2 * ROT
C_QD = C_ROTB + NT * 2 * ROT
C_KD = C_QD + HEADS
C_RC = C_KD + HEADS
C_SLOT = C_RC + GROUPS
C_TRASH = C_SLOT + EXPERTS
C_TOK = C_TRASH + NT * TOPK
C_END = C_TOK + NT

USES = {
    "A0": ["ctx0", "xdbl"] + [f"{n}{c}" for c in range(NT) for n in ("xT", "k", "qT", "O")] + ["yT0", "yT2", "x2T0", "x2T2"],
    "A1": ["ctx1"] + [f"{n}{c}" for c in range(NT) for n in ("q", "v", "kT") + (("I",) if c else ())]
          + ["yT1", "yT3", "x2T1", "x2T3"],
    "S0": [n for c in range(NT) for n in ([f"aT{c - 1}"] if c else []) + [f"r0_{c}", f"r2_{c}"]
           + ([f"U{c}"] if c < NT - 1 else [])] + [f"aT{NT - 1}", "logits"],
    "S1": [n for c in range(NT) for n in [f"r1_{c}"] + ([f"wo{c - 1}"] if c else []) + [f"r3_{c}"]] + [f"wo{NT - 1}", "pos"],
}
for _m in range(MI):
    USES[f"Y{_m}"] = [f"in{_m}", f"dt{_m}", f"y{_m}"]
BANK_OF = {use: (bank, n) for bank, uses in USES.items() for n, use in enumerate(uses)}

HEAD = 1

VECTOR_STEPS, SCALAR_STEPS, POOL_STEPS = 68, 5, 9


def wait(eng, sem, value):
    if isinstance(value, int) and value <= 0:
        return
    eng.wait_ge(sem, value)


def pause(eng, spare):
    eng.tensor_tensor(spare[:, 0:1], spare[:, 1:2], spare[:, 1:2], ALU.mult)


class Chain:

    def __init__(self, eng, sem, base=0):
        self.eng, self.sem, self.base, self.n = eng, sem, base, 0

    def step(self, instruction):
        instruction.then_inc(self.sem, 1)
        self.n += 1

    def settle(self):
        self.eng.wait_ge(self.sem, self.base + self.n)


def build(nc, x, ctx, wq, wk, wv, wo, rms_w, in_w, conv_w, conv_b, xp_w, dt_w, dt_b, a_log, d_skip,
          router, gate_up, down, consts, dmask, out, scratch="Internal"):
    bc_dram = nc.dram_tensor("bc_rows", [B, 2 * STATE, T], F32, kind=scratch).ap()
    x2_dram = nc.dram_tensor("x2_rows", [NTOK, D], F32, kind=scratch).ap()
    table_dram = nc.dram_tensor("slot_table", [2 * SLOTS, 1], I32, kind=scratch).ap()
    ye_dram = nc.dram_tensor("expert_rows", [SLOTS, D], F32, kind=scratch).ap()

    with ExitStack() as whole:
        def keep(name, shape, dt=F32):
            return whole.enter_context(nc.sbuf_tensor(name, shape, dt))

        cs = keep("cs", [P, C_END])
        slot_idx = keep("slot_idx", [P, TILES, TOPK], I32)
        slot_w = keep("slot_w", [P, TILES, TOPK])
        half = keep("half", [P, NT])
        spare = [keep(f"spare{i}", [P, 3]) for i in range(2)]
        ident = cs[:, C_ID:C_ID + P]

        mixers(nc, x, ctx, wq, wk, wv, wo, rms_w, in_w, conv_w, conv_b, xp_w, dt_w, dt_b, a_log, d_skip,
               router, consts, dmask, bc_dram, x2_dram, table_dram, cs, ident, slot_idx, slot_w, half, spare)
        experts(nc, gate_up, down, x2_dram, table_dram, ye_dram, ident, spare)
        combine(nc, x2_dram, ye_dram, out, slot_idx, slot_w, half, spare)


def mixers(nc, x, ctx, wq, wk, wv, wo, rms_w, in_w, conv_w, conv_b, xp_w, dt_w, dt_b, a_log, d_skip,
           router, consts, dmask_in, bc_dram, x2_dram, table_dram, cs, ident, slot_idx, slot_w, half, spare):
    with ExitStack() as mem:
        def sb(name, shape, dt=F32):
            return mem.enter_context(nc.sbuf_tensor(name, shape, dt))

        def sem(name):
            return mem.enter_context(nc.semaphore(name))

        bank = {n: mem.enter_context(nc.psum_tensor(f"bank_{n}", [P, 512], F32)) for n in USES}

        wqkv = sb("wqkv", [P, 3, KD, D])
        wo_sb = sb("wo_sb", [P, KD, D])
        in_wT = sb("in_wT", [P, KC, INNER])
        xp_wT = sb("xp_wT", [P, MI, RANK + 2 * STATE])
        dt_wT = sb("dt_wT", [RANK, INNER])
        rT = sb("rT", [P, KD, EXPERTS])
        dmask = sb("dmask", [P, HPG, GROUPS * P])
        conv_c = sb("conv_c", [P, MI, TAPS])
        vecs = sb("vecs", [P, 4 * MI])
        cb, dtb, dsk, rms_c = (vecs[:, n * MI:(n + 1) * MI] for n in range(4))
        a_sc = sb("a_sc", [P, MI, STATE])
        ones = sb("ones", [P, P])

        u = sb("u", [P, MI, T])
        dt = sb("dt", [P, MI, T])
        dtu = sb("dtu", [P, MI, T])
        xin = sb("xin", [P, MI, T + TAPS - 1])
        bmat = sb("bmat", [P, 2, NG, T])
        cmat = sb("cmat", [P, 2, NG, T])
        da = sb("da", [P, 2, NG, T])
        dbu = sb("dbu", [P, 2, NG, T])
        h = sb("h", [P, NG, T])
        x_in = sb("x_in", [P, 2, D])
        xT = sb("xT", [P, KD, P])
        qk = sb("qk", [P, 2 * HEADS, HD])
        v = sb("v", [P, D])
        kdec = sb("kdec", [P, HEADS, HD])
        rot = sb("rot", [P, 2, 2 * HEADS, 2, ROT])
        qT = sb("qT", [P, GROUPS, P])
        kT = sb("kT", [P, GROUPS, P])
        pr = sb("pr", [P, HPG, GROUPS, P])
        attn = sb("attn", [P, HEADS, HD])
        aT = sb("aT", [P, KD, P])
        kv = sb("kv", [P, GROUPS, P])
        kvs = sb("kvs", [P, GROUPS, P])
        x1 = sb("x1", [P, NT, D])
        junk = sb("junk", [P, D])
        ssq = sb("ssq", [P, NT])
        rms = sb("rms", [P, NT])
        st = sb("st", [P, NT, 6])
        mv = sb("mv", [P, NT, 2])
        rstd = sb("rstd", [P, NT])
        xdbl = sb("xdbl", [RANK + 2 * STATE, T])
        prev = sb("prev", [P, EXPERTS])
        top = sb("top", [P, NT, TOPK])
        small = sb("small", [P, 4, NT])
        idxf = sb("idxf", [P, 2, NT, TOPK])
        idx_s = sb("idx_s", [P, NT * TOPK], I32)
        tok_i = sb("tok_i", [P, NT], I32)
        spill_f = sb("spill_f", [P, NT * TOPK])

        tok_f = sb("tokf", [P, NT])
        ctx_sb = pr[:, :, :, :].rearrange("p a b c -> p (a b c)")[:, 0:NT * CTX].rearrange("p (t d) -> p t d", t=NT)
        ctxT = h
        zero_i = kv[:, :, :].rearrange("p a b -> p (a b)")[:, 0:SLOTS // P].bitcast(I32)
        flat_pr = pr[:, :, :, :].rearrange("p a b c -> p (a b c)")
        lsm, prob, mask = (flat_pr[:, n * NT * EXPERTS:(n + 1) * NT * EXPERTS].rearrange("p (j e) -> p j e", j=NT)
                           for n in range(3))
        acc = dbu[:, 0, :, :]
        ex = dbu[:, 0, :, :]
        ln = dbu[:, 1, :, :]
        lin = h
        y3 = xin[:, :, TAPS - 1:]
        sz = dtu
        x2 = u
        x2T = dbu[:, 0, :, :]
        tmp = rot[:, :, :, :, :].rearrange("p a h b c -> p (a h b c)")[:, 0:D]
        tmp2 = rot[:, :, :, :, :].rearrange("p a h b c -> p (a h b c)")[:, D:2 * D]
        hot = h[:, :, :].rearrange("p a b -> p (a b)").rearrange("p (j k e) -> p (j k) e", j=NT, k=TOPK)

        setup(nc, wq, wk, wv, wo, rms_w, in_w, conv_w, conv_b, xp_w, dt_w, dt_b, a_log, d_skip, router,
              consts, dmask_in, table_dram, cs, ident, half, spare, wqkv, wo_sb, in_wT, xp_wT, dt_wT, rT, dmask,
              conv_c, vecs, rms_c, a_sc, ones, xin, da, bmat, cmat, x1, prev, tok_f, spill_f, zero_i, bank)

        filled = {n: sem(f"filled_{n}") for n in USES}
        drained = {n: sem(f"drained_{n}") for n in USES}
        ctx_loaded = sem("ctx_loaded")
        x_loaded = [sem(f"x_loaded{i}") for i in range(2)]
        bc_stored = sem("bc_stored")
        bc_loaded = [sem(f"bc_loaded{i}") for i in range(2)]
        x2_stored = sem("x2_stored")
        scattered = sem("scattered")
        spread = sem("spread")
        convolved = sem("convolved")
        u_ready = sem("u_ready")
        soft_ready = sem("soft_ready")
        dt_ready = sem("dt_ready")
        dtu_ready = sem("dtu_ready")
        da_ready = sem("da_ready")
        dbu_ready = sem("dbu_ready")
        scanned = sem("scanned")
        yc_ready = sem("yc_ready")
        y_summed = sem("y_summed")
        rotated = sem("rotated")
        kdec_ready = sem("kdec_ready")
        kv_scaled = sem("kv_scaled")
        kv_ready = sem("kv_ready")
        squared = sem("squared")
        rms_ready = sem("rms_ready")
        stats_ready = sem("stats_ready")
        rstd_ready = sem("rstd_ready")
        x1_ready = sem("x1_ready")
        sz_ready = sem("sz_ready")
        y3_ready = sem("y3_ready")
        stats2_ready = sem("stats2_ready")
        rstd2_ready = sem("rstd2_ready")
        x2_ready = sem("x2_ready")
        exped = sem("exped")
        masked = sem("masked")
        routed = sem("routed")
        vector_steps = sem("vector_steps")
        scalar_steps = sem("scalar_steps")
        pool_steps = sem("pool_steps")

        def count(use, b):
            name, n = BANK_OF[use]
            return name, len(USES[name]) * b + n + 1

        def to_fill(eng, use, b):
            name, value = count(use, b)
            wait(eng, drained[name], HEAD + value - 1)
            return bank[name]

        def full(eng, use, b):
            name, value = count(use, b)
            wait(eng, filled[name], value)
            return bank[name]

        def taken(eng, use, b):
            name, value = count(use, b)
            wait(eng, drained[name], HEAD + value)

        def fill_sem(use):
            return filled[BANK_OF[use][0]]

        def drain_sem(use):
            return drained[BANK_OF[use][0]]

        def last_sequence_over(eng, b):
            wait(eng, routed, HEAD + b)

        SCANS = MI * (STATE // NG)

        def state_ready(eng, c, b):
            if c == 0:
                taken(eng, "U0", b)
            else:
                wait(eng, kv_ready, (NT - 2) * b + c)

        def states_summed(eng, n, b):
            g, m = divmod(n, MI)
            if g < STATE // NG - 1:
                wait(eng, y_summed, (SCANS - MI) * b + n + 1)
            else:
                full(eng, f"y{m}", b)

        block = mem.enter_context(nc.Block())

        @block.sync
        def _(sp):
            with sp.Fori(0, B) as b:
                last_sequence_over(sp, b)
                sp.dma_start(ctx_sb, ctx[b].rearrange("(t p) d -> p t d", p=P)).then_inc(ctx_loaded, 16)

                def load_x(c):
                    if c >= 2:
                        wait(sp, stats_ready, NT * b + c - 1)
                    sp.dma_start(x_in[:, c % 2, :], x[b, c * P:(c + 1) * P, :]).then_inc(x_loaded[c % 2], 16)

                load_x(0)
                load_x(1)
                taken(sp, "xdbl", b)
                sp.dma_start(bc_dram[b], xdbl[RANK:, :]).then_inc(bc_stored, 16)
                wait(sp, bc_stored, 16 * (b + 1))
                for g in range(STATE // NG):
                    if g >= 2:
                        wait(sp, yc_ready, SCANS * b + MI * (g - 1))
                    for dst, row in ((bmat, NG * g), (cmat, STATE + NG * g)):
                        sp.dma_start(dst[:, g % 2, :, :], bc_dram[b, row:row + NG, :].partition_broadcast(P))\
                            .then_inc(bc_loaded[g % 2], 16)
                    if 1 <= g < 3:
                        load_x(g + 1)
                for j in range(NT):
                    wait(sp, x2_ready, NT * b + j + 1)
                    sp.dma_start(x2_dram.rearrange("(b t p) d -> b t p d", b=B, p=P)[b, j], x2[:, j, :])\
                        .then_inc(x2_stored, 16)
            sp.wait_ge(x2_stored, 16 * NT * B)
            sp.wait_ge(bc_stored, 16 * B)

        @block.tensor
        def _(pe):
            with pe.Fori(0, B) as b:
                last_sequence_over(pe, b)
                wait(pe, ctx_loaded, 16 * (b + 1))
                for k in range(KC):
                    ps = to_fill(pe, f"ctx{k}", b)
                    for t in range(NT):
                        ins = pe.transpose(ps[:, t * P:(t + 1) * P], ctx_sb[:, t, k * P:(k + 1) * P], ident)
                    ins.then_inc(fill_sem(f"ctx{k}"), 1)
                for k in range(KC):
                    taken(pe, f"ctx{k}", b)
                for m in range(MI):
                    ps = to_fill(pe, f"in{m}", b)
                    for k in range(KC):
                        ins = pe.matmul(ps[:, :], in_wT[:, k, m * P:(m + 1) * P], ctxT[:, k, :],
                                        start=(k == 0), stop=(k == KC - 1))
                    ins.then_inc(fill_sem(f"in{m}"), 1)
                ps = to_fill(pe, "xdbl", b)
                for m in range(MI):
                    wait(pe, u_ready, MI * b + m + 1)
                    ins = pe.matmul(ps[0:RANK + 2 * STATE, :], xp_wT[:, m, :], u[:, m, :],
                                    start=(m == 0), stop=(m == MI - 1))
                ins.then_inc(fill_sem("xdbl"), 1)
                taken(pe, "xdbl", b)
                for m in range(MI):
                    ps = to_fill(pe, f"dt{m}", b)
                    pe.matmul(ps[:, :], dt_wT[:, m * P:(m + 1) * P], xdbl[0:RANK, :], start=True, stop=True)\
                        .then_inc(fill_sem(f"dt{m}"), 1)

                def sum_states(g, m):
                    n = MI * g + m
                    if g == 0:
                        to_fill(pe, f"y{m}", b)
                    wait(pe, yc_ready, SCANS * b + n + 1)
                    for i in range(NG):
                        ins = pe.matmul(bank[f"Y{m}"][:, :], ident, dbu[:, n % 2, i, :],
                                        start=(g == 0 and i == 0), stop=(g == STATE // NG - 1 and i == NG - 1))
                    ins.then_inc(fill_sem(f"y{m}") if g == STATE // NG - 1 else y_summed, 1)

                def turn(c):
                    wait(pe, x_loaded[c % 2], 16 * (2 * b + c // 2 + 1))
                    ps = to_fill(pe, f"xT{c}", b)
                    for k in range(KD):
                        ins = pe.transpose(ps[:, k * P:(k + 1) * P], x_in[:, c % 2, k * P:(k + 1) * P], ident)
                    ins.then_inc(fill_sem(f"xT{c}"), 1)

                def project(c, name):
                    taken(pe, f"xT{c}", b)
                    ps = to_fill(pe, f"{name}{c}", b)
                    for k in range(KD):
                        ins = pe.matmul(ps[:, :], xT[:, k, :], wqkv[:, "qkv".index(name), k, :],
                                        start=(k == 0), stop=(k == KD - 1))
                    ins.then_inc(fill_sem(f"{name}{c}"), 1)

                def turn_qk(c):
                    wait(pe, rotated, NT * b + c + 1)
                    for n, name in enumerate(("qT", "kT")):
                        ps = to_fill(pe, f"{name}{c}", b)
                        for g in range(GROUPS):
                            src = qk[:, n * HEADS + g * HPG:n * HEADS + (g + 1) * HPG, :].rearrange("p h d -> p (h d)")
                            ins = pe.transpose(ps[:, g * P:(g + 1) * P], src, ident)
                        ins.then_inc(fill_sem(f"{name}{c}"), 1)

                def scores(c, r):
                    taken(pe, f"qT{c}", b)
                    taken(pe, f"kT{c}", b)
                    ps = to_fill(pe, f"r{r}_{c}", b)
                    for g in range(GROUPS):
                        ins = pe.matmul(ps[:, g * P:(g + 1) * P], kT[r * HD:(r + 1) * HD, g, :],
                                        qT[r * HD:(r + 1) * HD, g, :], start=True, stop=True)
                    ins.then_inc(fill_sem(f"r{r}_{c}"), 1)

                def mix_values(c):
                    taken(pe, f"v{c}", b)
                    for r in range(2, HPG):
                        taken(pe, f"r{r}_{c}", b)
                    ps = to_fill(pe, f"O{c}", b)
                    for hd in range(HEADS):
                        ins = pe.matmul(ps[:, hd * HD:(hd + 1) * HD], pr[:, hd % HPG, hd // HPG, :],
                                        v[:, hd * HD:(hd + 1) * HD], start=True, stop=True)
                    ins.then_inc(fill_sem(f"O{c}"), 1)
                    if c:
                        state_ready(pe, c - 1, b)
                        ps = to_fill(pe, f"I{c}", b)
                        for g in range(GROUPS):
                            ins = pe.matmul(ps[:, g * P:(g + 1) * P], qT[:, g, :], kv[:, g, :], start=True, stop=True)
                        ins.then_inc(fill_sem(f"I{c}"), 1)
                    if c < NT - 1:
                        wait(pe, kdec_ready, (NT - 1) * b + c + 1)
                        ps = to_fill(pe, f"U{c}", b)
                        for g in range(GROUPS):
                            ins = pe.matmul(ps[:, g * P:(g + 1) * P],
                                            kdec[:, g * HPG:(g + 1) * HPG, :].rearrange("p h d -> p (h d)"),
                                            v[:, g * P:(g + 1) * P], start=True, stop=True)
                        ins.then_inc(fill_sem(f"U{c}"), 1)

                def turn_mixed(c):
                    taken(pe, f"O{c}", b)
                    ps = to_fill(pe, f"aT{c}", b)
                    for k in range(KD):
                        src = attn[:, k * HPG:(k + 1) * HPG, :].rearrange("p h d -> p (h d)")
                        ins = pe.transpose(ps[:, k * P:(k + 1) * P], src, ident)
                    ins.then_inc(fill_sem(f"aT{c}"), 1)

                def project_out(c):
                    taken(pe, f"aT{c}", b)
                    ps = to_fill(pe, f"wo{c}", b)
                    for k in range(KD):
                        ins = pe.matmul(ps[:, :], aT[:, k, :], wo_sb[:, k, :], start=(k == 0), stop=(k == KD - 1))
                    ins.then_inc(fill_sem(f"wo{c}"), 1)

                for c in range(NT):
                    turn(c)
                    project(c, "q")
                    sum_states(c, 0)
                    project(c, "k")
                    project(c, "v")
                    sum_states(c, 1)
                    if c:
                        turn_mixed(c - 1)
                    turn_qk(c)
                    scores(c, 0)
                    scores(c, 1)
                    if c:
                        project_out(c - 1)
                    sum_states(c, 2)
                    scores(c, 2)
                    scores(c, 3)
                    sum_states(c, 3)
                    mix_values(c)
                turn_mixed(NT - 1)
                project_out(NT - 1)
                wait(pe, y3_ready, MI * (b + 1))
                for j in range(NT):
                    ps = to_fill(pe, f"yT{j}", b)
                    for m in range(MI):
                        ins = pe.transpose(ps[:, m * P:(m + 1) * P], y3[:, m, j * P:(j + 1) * P], ident)
                    ins.then_inc(fill_sem(f"yT{j}"), 1)
                for j in range(NT):
                    wait(pe, x2_ready, NT * b + j + 1)
                    ps = to_fill(pe, f"x2T{j}", b)
                    for k in range(KD):
                        ins = pe.transpose(ps[:, k * P:(k + 1) * P], x2[:, j, k * P:(k + 1) * P], ident)
                    ins.then_inc(fill_sem(f"x2T{j}"), 1)
                ps = to_fill(pe, "logits", b)
                for j in range(NT):
                    taken(pe, f"x2T{j}", b)
                    for k in range(KD):
                        ins = pe.matmul(ps[:, j * EXPERTS:(j + 1) * EXPERTS], x2T[:, j, k * P:(k + 1) * P],
                                        rT[:, k, :], start=(k == 0), stop=(k == KD - 1))
                ins.then_inc(fill_sem("logits"), 1)
                wait(pe, masked, b + 1)
                ps = to_fill(pe, "pos", b)
                for j in range(NT):
                    dst = ps[:, j * EXPERTS:(j + 1) * EXPERTS]
                    pe.matmul(dst, cs[:, C_TRI:C_TRI + P], mask[:, j, :], start=True, stop=False)
                    for i in range(j):
                        pe.matmul(dst, ones[:, :], mask[:, i, :], start=False, stop=False)
                    ins = pe.matmul(dst, ones[:, :], prev[:, :], start=False, stop=True)
                ins.then_inc(fill_sem("pos"), 1)

        @block.scalar
        def _(act):
            with act.Fori(0, B) as b:
                last_sequence_over(act, b)
                own = Chain(act, scalar_steps, SCALAR_STEPS * b)

                def take(use, dst):
                    act.activation(dst, full(act, use, b)[0:dst.shape[0], :], ACT.Copy).then_inc(drain_sem(use), 1)

                for k in range(KC):
                    take(f"ctx{k}", ctxT[:, k, :])
                for m in range(MI):
                    take(f"in{m}", xin[:, m, TAPS - 1:])
                for m in range(MI):
                    wait(act, convolved, MI * b + m + 1)
                    act.activation(u[:, m, :], acc[:, m, :], ACT.Silu, bias=cb[:, m:m + 1]).then_inc(u_ready, 1)
                take("xdbl", xdbl[:, :])
                wait(act, u_ready, MI * (b + 1))
                for m in range(MI):
                    ps = full(act, f"dt{m}", b)
                    own.step(act.activation(ex[:, m, :], ps[:, :], ACT.Abs, bias=dtb[:, m:m + 1]))
                    act.activation(lin[:, m, :], ps[:, :], ACT.Relu, bias=dtb[:, m:m + 1]).then_inc(drain_sem(f"dt{m}"), 1)
                own.settle()
                own.step(act.activation(ex, ex, ACT.Exp, scale=-1.0))
                own.settle()
                act.activation(ln, ex, ACT.Ln, bias=1.0).then_inc(soft_ready, 1)

                def decays(n):
                    g, m = divmod(n, MI)
                    if n == 0:
                        wait(act, dt_ready, b + 1)
                    if n >= 2:
                        wait(act, scanned, SCANS * b + n - 1)
                    for i in range(NG):
                        s = NG * g + i
                        ins = act.activation(da[:, n % 2, i, 1:], dt[:, m, 1:], ACT.Exp, scale=a_sc[:, m, s:s + 1])
                    ins.then_inc(da_ready, 1)

                def square(c):
                    taken(act, f"O{c}", b)
                    act.activation(junk[:, :], flat(attn[:, :, :]), ACT.Square, accum_out=ssq[:, c:c + 1]).then_inc(squared, 1)

                decays(0)
                for c in range(NT):
                    decays(MI * c + 1)
                    take(f"xT{c}", flat(xT[:, :, :]))
                    take(f"q{c}", flat(qk[:, 0:HEADS, :]))
                    if c:
                        square(c - 1)
                    decays(MI * c + 2)
                    take(f"k{c}", flat(qk[:, HEADS:, :]))
                    take(f"v{c}", v[:, :])
                    decays(MI * c + 3)
                    if c:
                        take(f"aT{c - 1}", flat(aT[:, :, :]))
                    take(f"qT{c}", flat(qT[:, :, :]))
                    take(f"kT{c}", flat(kT[:, :, :]))
                    if c < NT - 1:
                        decays(MI * c + 4)
                square(NT - 1)
                take(f"aT{NT - 1}", flat(aT[:, :, :]))
                for m in range(MI):
                    wait(act, x1_ready, NT * b + m + 1)
                    if m == 0:
                        wait(act, dbu_ready, SCANS * (b + 1))
                    act.activation(sz[:, m, :], x1[:, m, :], ACT.Silu).then_inc(sz_ready, 1)
                for j in range(NT):
                    take(f"x2T{j}", x2T[:, j, :])
                taken(act, "logits", b)
                act.activation(lsm[:, :, :], lsm[:, :, :], ACT.Exp).then_inc(exped, 1)
                wait(act, x2_stored, 16 * NT * (b + 1))
            assert own.n == SCALAR_STEPS, own.n

        @block.gpsimd
        def _(pool):
            with pool.Fori(0, B) as b:
                last_sequence_over(pool, b)
                own = Chain(pool, pool_steps, POOL_STEPS * b)

                def root(dst, src, scale, done):
                    pause(pool, spare[1])
                    own.step(pool.tensor_scalar(dst, src, scale, EPS, ALU.mult, ALU.add))
                    own.settle()
                    pool.tensor_tensor(dst, dst, half[:, 0:dst.shape[1]], ALU.pow).then_inc(done, 1)

                def inputs(n):
                    g, m = divmod(n, MI)
                    wait(pool, bc_loaded[g % 2], 64 * b + 32 * (g // 2 + 1))
                    if n >= 2:
                        states_summed(pool, n - 2, b)
                    pool.tensor_tensor(dbu[:, n % 2, :, :], bmat[:, g % 2, :, :],
                                       dtu[:, m, :].unsqueeze(1).broadcast_to([P, NG, T]), ALU.mult).then_inc(dbu_ready, 1)

                wait(pool, dt_ready, b + 1)
                for m in range(MI):
                    pool.tensor_tensor(dtu[:, m, :], dt[:, m, :], u[:, m, :], ALU.mult).then_inc(dtu_ready, 1)
                wait(pool, dtu_ready, MI * (b + 1))
                for c in range(NT):
                    inputs(MI * c)
                    if c >= 2:
                        wait(pool, stats_ready, NT * b + c - 1)
                        root(rstd[:, c - 2:c - 1], mv[:, c - 2, 1:2], 1.0, rstd_ready)
                    inputs(MI * c + 1)
                    inputs(MI * c + 2)
                    if c:
                        wait(pool, squared, NT * b + c)
                        root(rms[:, c - 1:c], ssq[:, c - 1:c], 1.0 / D, rms_ready)
                    inputs(MI * c + 3)
                    if c < NT - 1:
                        wait(pool, rotated, NT * b + c + 1)
                        if c:
                            full(pool, f"U{c - 1}", b)
                        pool.tensor_tensor(kdec[:, :, :], qk[:, HEADS:, :],
                                           cs[:, C_KD:C_KD + HEADS].unsqueeze(2).broadcast_to([P, HEADS, HD]),
                                           ALU.mult).then_inc(kdec_ready, 1)
                    if 1 <= c < NT - 1:
                        state_ready(pool, c - 1, b)
                        pool.tensor_tensor(kvs[:, :, :], kv[:, :, :],
                                           cs[:, C_RC:C_RC + GROUPS].unsqueeze(2).broadcast_to([P, GROUPS, P]),
                                           ALU.mult).then_inc(kv_scaled, 1)
                wait(pool, stats_ready, NT * b + NT - 1)
                root(rstd[:, NT - 2:NT - 1], mv[:, NT - 2, 1:2], 1.0, rstd_ready)
                wait(pool, squared, NT * (b + 1))
                root(rms[:, NT - 1:NT], ssq[:, NT - 1:NT], 1.0 / D, rms_ready)
                wait(pool, stats_ready, NT * (b + 1))
                root(rstd[:, NT - 1:NT], mv[:, NT - 1, 1:2], 1.0, rstd_ready)
                wait(pool, stats2_ready, NT * (b + 1))
                wait(pool, x1_ready, NT * (b + 1))
                root(rstd[:, :], mv[:, :, 1], 1.0, rstd2_ready)
                wait(pool, routed, HEAD + b + 1)
                pause(pool, spare[1])
                for j in range(NT):
                    for k in range(TOPK):
                        n = j * TOPK + k
                        pool.indirect_dma_start(table_dram, bass.IndirectOffsetOnAxis(ap=idx_s[:, n:n + 1], axis=0),
                                                tok_i[:, j:j + 1], None).then_inc(scattered, 16)
                wait(pool, scattered, 16 * NT * TOPK * (b + 1))
                wait(pool, spread, HEAD + b)
                pool.tensor_tensor(spare[1][:, 2:3], spare[1][:, 1:2], spare[1][:, 1:2], ALU.mult).then_inc(spread, 1)
            pool.wait_ge(scattered, 16 * TILES * TOPK)
            assert own.n == POOL_STEPS, own.n

        @block.vector
        def _(dve):
            for s in (*drained.values(), routed, spread):
                dve.sem_inc(s, HEAD)
            with dve.Fori(0, B) as b:
                last_sequence_over(dve, b)
                wait(dve, spread, HEAD + b)
                own = Chain(dve, vector_steps, VECTOR_STEPS * b)

                for t in range(TAPS):
                    for m in range(MI):
                        src = xin[:, m, t:t + T]
                        if t == 0:
                            taken(dve, f"in{m}", b)
                            own.step(dve.tensor_scalar(acc[:, m, :], src, conv_c[:, m, 0:1], None, ALU.mult))
                            continue
                        ins = dve.scalar_tensor_tensor(out=acc[:, m, :], in0=src, scalar=conv_c[:, m, t:t + 1],
                                                       in1=acc[:, m, :], op0=ALU.mult, op1=ALU.add)
                        if t < TAPS - 1:
                            own.step(ins)
                        else:
                            ins.then_inc(convolved, 1)
                    if t < TAPS - 1:
                        own.settle()
                wait(dve, soft_ready, b + 1)
                own.step(dve.tensor_scalar(dt[:, :, :], ex, 1.0, None, ALU.add))
                own.settle()
                own.step(dve.scalar_tensor_tensor(out=dt[:, :, :], in0=dt[:, :, :], scalar=1.0, in1=ex,
                                                  op0=ALU.subtract, op1=ALU.subtract))
                own.settle()
                own.step(dve.tensor_tensor(dt[:, :, :], ln, dt[:, :, :], ALU.subtract))
                own.settle()
                own.step(dve.scalar_tensor_tensor(out=dt[:, :, :], in0=dt[:, :, :], scalar=0.0, in1=ex,
                                                  op0=ALU.max, op1=ALU.min))
                own.settle()
                dve.tensor_tensor(dt[:, :, :], lin[:, :, :], dt[:, :, :], ALU.add).then_inc(dt_ready, 1)
                wait(dve, dt_ready, b + 1)

                def scan(n):
                    g, m = divmod(n, MI)
                    if n:
                        wait(dve, yc_ready, SCANS * b + n)
                    wait(dve, da_ready, SCANS * b + n + 1)
                    wait(dve, dbu_ready, SCANS * b + n + 1)
                    dve.tensor_tensor_scan(h[:, :, :].rearrange("p s t -> p (s t)"),
                                           da[:, n % 2, :, :].rearrange("p s t -> p (s t)"),
                                           dbu[:, n % 2, :, :].rearrange("p s t -> p (s t)"),
                                           0.0, ALU.mult, ALU.add).then_inc(scanned, 1)
                    wait(dve, scanned, SCANS * b + n + 1)
                    if m == 0:
                        wait(dve, bc_loaded[g % 2], 64 * b + 32 * (g // 2 + 1))
                    dve.tensor_tensor(dbu[:, n % 2, :, :], h[:, :, :], cmat[:, g % 2, :, :], ALU.mult).then_inc(yc_ready, 1)

                def rotate(c):
                    taken(dve, f"q{c}", b)
                    taken(dve, f"k{c}", b)
                    if c >= 2:
                        taken(dve, f"O{c - 1}", b)
                        state_ready(dve, c - 1, b)
                    pair = [P, 2 * HEADS, 2, ROT]
                    for n, (part, col) in enumerate(((0, C_ROTA), (HD // 2, C_ROTB))):
                        table = cs[:, col + c * 2 * ROT:col + (c + 1) * 2 * ROT].rearrange("p (a r) -> p a r", a=2)
                        own.step(dve.tensor_tensor(rot[:, n, :, :, :], qk[:, :, part:part + ROT].unsqueeze(2).broadcast_to(pair),
                                                   table.unsqueeze(1).broadcast_to(pair), ALU.mult))
                    own.settle()
                    own.step(dve.tensor_tensor(qk[:, :, 0:ROT], rot[:, 0, :, 0, :], rot[:, 1, :, 0, :], ALU.add))
                    dve.tensor_tensor(qk[:, :, HD // 2:HD // 2 + ROT], rot[:, 1, :, 1, :], rot[:, 0, :, 1, :], ALU.subtract)\
                        .then_inc(rotated, 1)

                def mask_scores(c, r):
                    use = f"r{r}_{c}"
                    dve.tensor_tensor(pr[:, r, :, :].rearrange("p g c -> p (g c)"), full(dve, use, b)[:, :], dmask[:, r, :],
                                      ALU.mult).then_inc(drain_sem(use), 1)

                def mixed_heads(c):
                    if c == 0:
                        dve.tensor_copy(flat(attn[:, :, :]), full(dve, "O0", b)[:, :]).then_inc(drain_sem("O0"), 1)
                    else:
                        inter = full(dve, f"I{c}", b)
                        full(dve, f"aT{c - 1}", b)
                        wait(dve, squared, NT * b + c)
                        wait(dve, rotated, NT * b + c + 1)
                        dve.tensor_tensor(tmp.rearrange("p (h d) -> p h d", h=HEADS),
                                          inter[:, :].rearrange("p (h d) -> p h d", h=HEADS),
                                          cs[:, C_QD:C_QD + HEADS].unsqueeze(2).broadcast_to([P, HEADS, HD]), ALU.mult)\
                            .then_inc(drain_sem(f"I{c}"), 1)
                        taken(dve, f"I{c}", b)
                        dve.tensor_tensor(flat(attn[:, :, :]), full(dve, f"O{c}", b)[:, :], tmp, ALU.add)\
                            .then_inc(drain_sem(f"O{c}"), 1)
                    if c < NT - 1:
                        update = full(dve, f"U{c}", b)[:, :].rearrange("p (g e) -> p g e", g=GROUPS)
                        blocks = cs[:, C_BD:C_BD + P].unsqueeze(1).broadcast_to([P, GROUPS, P])
                        dst = kv[:, :, :] if c == 0 else tmp2.rearrange("p (g e) -> p g e", g=GROUPS)
                        dve.tensor_tensor(dst, update, blocks, ALU.mult).then_inc(drain_sem(f"U{c}"), 1)
                        if c:
                            wait(dve, kv_scaled, (NT - 2) * b + c)
                            taken(dve, f"U{c}", b)
                            dve.tensor_tensor(kv[:, :, :], kvs[:, :, :], dst, ALU.add).then_inc(kv_ready, 1)

                def add_attention(c):
                    wait(dve, rms_ready, NT * b + c + 1)
                    wait(dve, x_loaded[c % 2], 16 * (2 * b + c // 2 + 1))
                    dve.scalar_tensor_tensor(out=x1[:, c, :], in0=full(dve, f"wo{c}", b)[:, :], scalar=rms[:, c:c + 1],
                                             in1=x_in[:, c % 2, :], op0=ALU.mult, op1=ALU.add).then_inc(drain_sem(f"wo{c}"), 1)
                    taken(dve, f"wo{c}", b)
                    own.step(dve.bn_stats(st[:, c, :], x1[:, c, :]))
                    own.settle()
                    pause(dve, spare[0])
                    dve.bn_aggr(mv[:, c, :], st[:, c, :]).then_inc(stats_ready, 1)

                def normalise(dst, c, done):
                    dve.tensor_scalar(dst[:, c, :], dst[:, c, :], mv[:, c, 0:1], rstd[:, c:c + 1], ALU.subtract, ALU.mult)\
                        .then_inc(done, 1)

                def first_norm(c):
                    wait(dve, stats_ready, NT * b + c + 1)
                    wait(dve, rstd_ready, NT * b + c + 1)
                    normalise(x1, c, x1_ready)

                for c in range(NT):
                    scan(MI * c)
                    if c:
                        mixed_heads(c - 1)
                    scan(MI * c + 1)
                    rotate(c)
                    scan(MI * c + 2)
                    mask_scores(c, 0)
                    mask_scores(c, 1)
                    if c:
                        add_attention(c - 1)
                    scan(MI * c + 3)
                    mask_scores(c, 2)
                    mask_scores(c, 3)
                    if c:
                        first_norm(c - 1)
                mixed_heads(NT - 1)
                for m in range(MI):
                    dve.scalar_tensor_tensor(out=y3[:, m, :], in0=u[:, m, :], scalar=dsk[:, m:m + 1],
                                             in1=full(dve, f"y{m}", b)[:, :], op0=ALU.mult, op1=ALU.add)\
                        .then_inc(drain_sem(f"y{m}"), 1)
                add_attention(NT - 1)
                first_norm(NT - 1)
                for m in range(MI):
                    taken(dve, f"y{m}", b)
                    wait(dve, sz_ready, MI * b + m + 1)
                    dve.tensor_tensor(y3[:, m, :], y3[:, m, :], sz[:, m, :], ALU.mult).then_inc(y3_ready, 1)
                wait(dve, x1_ready, NT * (b + 1))
                for j in range(NT):
                    dve.tensor_tensor(x2[:, j, :], full(dve, f"yT{j}", b)[:, :], x1[:, j, :], ALU.add)\
                        .then_inc(drain_sem(f"yT{j}"), 1)
                    taken(dve, f"yT{j}", b)
                    own.step(dve.bn_stats(st[:, j, :], x2[:, j, :]))
                own.settle()
                pause(dve, spare[0])
                for j in range(NT):
                    dve.bn_aggr(mv[:, j, :], st[:, j, :]).then_inc(stats2_ready, 1)
                wait(dve, stats2_ready, NT * (b + 1))
                wait(dve, rstd2_ready, b + 1)
                for j in range(NT):
                    normalise(x2, j, x2_ready)

                def each(t):
                    return t.unsqueeze(2).broadcast_to([P, NT, EXPERTS])

                logits = full(dve, "logits", b)[:, 0:NT * EXPERTS].rearrange("p (j e) -> p j e", j=NT)
                own.step(dve.tensor_reduce(small[:, 0, :], logits, AX.X, ALU.max))
                own.settle()
                dve.tensor_tensor(lsm[:, :, :], logits, each(small[:, 0, :]), ALU.subtract).then_inc(drain_sem("logits"), 1)
                wait(dve, exped, b + 1)
                own.step(dve.tensor_reduce(small[:, 1, :], lsm[:, :, :], AX.X, ALU.add))
                own.settle()
                own.step(dve.reciprocal(small[:, 2, :], small[:, 1, :]))
                own.settle()
                own.step(dve.tensor_tensor(prob[:, :, :], lsm[:, :, :], each(small[:, 2, :]), ALU.mult))
                own.settle()
                pause(dve, spare[0])
                for j in range(NT):
                    own.step(dve.max(top[:, j, :], prob[:, j, :]))
                own.settle()
                pause(dve, spare[0])
                for j in range(NT):
                    own.step(dve.match_replace(out=mask[:, j, :], in_to_replace=top[:, j, :], in_values=prob[:, j, :],
                                               imm_value=-1.0))
                own.step(dve.tensor_reduce(small[:, 3, :], top[:, :, :], AX.X, ALU.add))
                own.settle()
                dve.tensor_scalar(mask[:, :, :], mask[:, :, :], 0.0, None, ALU.is_lt).then_inc(masked, 1)
                own.step(dve.reciprocal(small[:, 0, :], small[:, 3, :]))
                own.settle()
                own.step(dve.tensor_tensor(lsm[:, :, :], prob[:, :, :], each(small[:, 0, :]), ALU.mult))
                own.settle()
                wait(dve, masked, b + 1)
                place = full(dve, "pos", b)[:, 0:NT * EXPERTS].rearrange("p (j e) -> p j e", j=NT)
                own.step(dve.scalar_tensor_tensor(out=prob[:, :, :], in0=place, scalar=float(CAP), in1=mask[:, :, :],
                                                  op0=ALU.is_lt, op1=ALU.mult))
                taken(dve, f"O{NT - 1}", b)
                key = tmp[:, 0:NT * EXPERTS].rearrange("p (j e) -> p j e", j=NT)
                dve.tensor_tensor(key, place, cs[:, C_SLOT:C_SLOT + EXPERTS].unsqueeze(1).broadcast_to([P, NT, EXPERTS]),
                                  ALU.add).then_inc(drain_sem("pos"), 1)
                chosen = tmp[:, NT * EXPERTS:NT * EXPERTS + EXPERTS]
                own.step(dve.tensor_reduce(chosen, mask[:, :, :].rearrange("p j e -> p e j"), AX.X, ALU.add))
                taken(dve, "pos", b)
                own.settle()
                own.step(dve.tensor_tensor(prev[:, :], prev[:, :], chosen, ALU.add))
                own.step(dve.tensor_tensor(key, key, prob[:, :, :], ALU.mult))
                own.step(dve.tensor_tensor(lsm[:, :, :], lsm[:, :, :], prob[:, :, :], ALU.mult))
                own.settle()
                pause(dve, spare[0])
                for j in range(NT):
                    own.step(dve.max(idxf[:, 0, j, :], key[:, j, :]))
                own.settle()
                cube = [P, NT, TOPK, EXPERTS]
                own.step(dve.tensor_tensor(hot, key.unsqueeze(2).broadcast_to(cube),
                                           idxf[:, 0, :, :].unsqueeze(3).broadcast_to(cube), ALU.is_equal))
                own.settle()
                own.step(dve.tensor_tensor(hot, hot, lsm[:, :, :].unsqueeze(2).broadcast_to(cube), ALU.mult))
                own.step(dve.scalar_tensor_tensor(out=idxf[:, 1, :, :], in0=idxf[:, 0, :, :], scalar=0.0,
                                                  in1=spill_f[:, :].rearrange("p (j k) -> p j k", j=NT),
                                                  op0=ALU.is_equal, op1=ALU.mult))
                own.settle()
                own.step(dve.tensor_reduce(slot_w[:, bass.ds(NT * b, NT), :], hot, AX.X, ALU.add))
                own.step(dve.tensor_scalar(slot_idx[:, bass.ds(NT * b, NT), :], idxf[:, 0, :, :], -1.0, 0.0, ALU.add, ALU.max))
                own.step(dve.tensor_copy(tok_i[:, :], tok_f[:, :]))
                own.settle()
                own.step(dve.tensor_scalar(tok_f[:, :], tok_f[:, :], float(T), None, ALU.add))
                own.step(dve.tensor_scalar(spill_f[:, :], spill_f[:, :], float(T * TOPK), None, ALU.add))
                own.settle()
                dve.scalar_tensor_tensor(out=idx_s[:, :].rearrange("p (j k) -> p j k", j=NT), in0=idxf[:, 0, :, :],
                                         scalar=-1.0, in1=idxf[:, 1, :, :], op0=ALU.add, op1=ALU.add).then_inc(routed, 1)
            assert own.n == VECTOR_STEPS, own.n


def flat(t):
    return t.rearrange("p a b -> p (a b)")


def setup(nc, wq, wk, wv, wo, rms_w, in_w, conv_w, conv_b, xp_w, dt_w, dt_b, a_log, d_skip, router,
          consts, dmask_in, table_dram, cs, ident, half, spare, wqkv, wo_sb, in_wT, xp_wT, dt_wT, rT, dmask,
          conv_c, vecs, rms_c, a_sc, ones, xin, da, stage1, stage2, x1, prev, tok_f, spill_f, zero_i, bank):
    with ExitStack() as mem:
        def sem(name):
            return mem.enter_context(nc.semaphore(name))

        const_loaded = sem("const_loaded")
        raw_loaded = sem("raw_loaded")
        wo_loaded = sem("wo_loaded")
        weights_loaded = sem("weights_loaded")
        zeroed = sem("zeroed")
        table_cleared = sem("table_cleared")
        turned = sem("turned")
        copied = sem("copied")
        a_exp = sem("a_exp")
        a_ready = sem("a_ready")
        pads = sem("pads")

        raw = stage1[:, 0, :, :].rearrange("p s t -> p (s t)")
        raw_in = raw[:, 0:MI * CTX].rearrange("p (t d) -> p t d", t=MI)
        raw_dt = raw[:, MI * CTX:MI * CTX + MI * RANK].rearrange("p (t r) -> p t r", t=MI)
        raw2 = stage2[:, 0, :, :].rearrange("p s t -> p (s t)")
        raw_xp = raw2[0:RANK + 2 * STATE, 0:INNER]
        raw_r = raw2[0:EXPERTS, INNER:INNER + D]
        raw_vec = raw2[0:4 * MI, INNER + D:INNER + D + P]
        block = mem.enter_context(nc.Block())

        @block.sync
        def _(sp):
            sp.dma_start(cs[:, :], consts).then_inc(const_loaded, 16)
            sp.dma_start(raw_in, in_w.rearrange("(t p) d -> p t d", p=P)).then_inc(raw_loaded, 16)
            sp.dma_start(raw_dt, dt_w.rearrange("(t p) r -> p t r", p=P)).then_inc(raw_loaded, 16)
            sp.dma_start(raw_xp, xp_w).then_inc(raw_loaded, 16)
            sp.dma_start(raw_r, router).then_inc(raw_loaded, 16)
            sp.dma_start(a_sc[:, :, :], a_log.rearrange("(m p) s -> p m s", p=P)).then_inc(raw_loaded, 16)
            sp.dma_start(wo_sb[:, :, :], wo.rearrange("(k p) n -> p k n", p=P)).then_inc(wo_loaded, 16)
            for n, w in enumerate((wq, wk, wv)):
                sp.dma_start(wqkv[:, n, :, :], w.rearrange("(k p) n -> p k n", p=P)).then_inc(weights_loaded, 16)
            sp.dma_start(dmask[:, :, :], dmask_in).then_inc(weights_loaded, 16)
            wait(sp, zeroed, 1)
            sp.dma_start(table_dram[0:SLOTS, :].rearrange("(p n) a -> p (n a)", p=P), zero_i).then_inc(table_cleared, 16)
            sp.wait_ge(weights_loaded, 80)
            sp.wait_ge(table_cleared, 16)

        @block.scalar
        def _(act):
            for n, vec in enumerate((conv_b, dt_b, d_skip, rms_w)):
                act.dma_start(raw_vec[n * MI:(n + 1) * MI, :], vec.rearrange("(k p) -> k p", p=P)).then_inc(raw_loaded, 16)
            act.dma_start(conv_c[:, :, :], conv_w.rearrange("(m p) a t -> p m (a t)", p=P)).then_inc(weights_loaded, 16)
            act.wait_ge(raw_loaded, 16 * 9)
            act.activation(a_sc[:, :, :], a_sc[:, :, :], ACT.Exp).then_inc(a_exp, 1)
            for k, name in enumerate(("A0", "A1")):
                act.wait_ge(turned, k + 1)
                act.activation(in_wT[:, k, :], bank[name][:, :], ACT.Copy).then_inc(copied, 1)
            act.wait_ge(turned, 3)
            act.activation(xp_wT[:, :, :], bank["S0"][:, 0:MI * (RANK + 2 * STATE)].rearrange("p (m r) -> p m r", m=MI),
                           ACT.Copy).then_inc(copied, 1)
            act.wait_ge(turned, 4)
            act.activation(dt_wT[:, :], bank["S1"][0:RANK, :], ACT.Copy).then_inc(copied, 1)
            act.wait_ge(turned, 5)
            act.activation(rT[:, :, :], bank["Y0"][:, 0:KD * EXPERTS].rearrange("p (k e) -> p k e", k=KD), ACT.Copy)\
                .then_inc(copied, 1)
            act.wait_ge(turned, 6)
            act.activation(vecs[:, :], bank["Y1"][:, 0:4 * MI], ACT.Copy).then_inc(copied, 1)
            act.wait_ge(weights_loaded, 80)

        @block.tensor
        def _(pe):
            pe.wait_ge(const_loaded, 16)
            pe.wait_ge(raw_loaded, 16 * 9)
            for k, name in enumerate(("A0", "A1")):
                for t in range(MI):
                    ins = pe.transpose(bank[name][:, t * P:(t + 1) * P], raw_in[:, t, k * P:(k + 1) * P], ident)
                ins.then_inc(turned, 1)
            rows = RANK + 2 * STATE
            for m in range(MI):
                ins = pe.transpose(bank["S0"][:, m * rows:(m + 1) * rows], raw_xp[:, m * P:(m + 1) * P],
                                   ident[0:rows, 0:rows])
            ins.then_inc(turned, 1)
            for m in range(MI):
                ins = pe.transpose(bank["S1"][0:RANK, m * P:(m + 1) * P], raw_dt[:, m, :], ident)
            ins.then_inc(turned, 1)
            for k in range(KD):
                ins = pe.transpose(bank["Y0"][:, k * EXPERTS:(k + 1) * EXPERTS], raw_r[:, k * P:(k + 1) * P],
                                   ident[0:EXPERTS, 0:EXPERTS])
            ins.then_inc(turned, 1)
            pe.transpose(bank["Y1"][:, 0:4 * MI], raw_vec, ident[0:4 * MI, 0:4 * MI]).then_inc(turned, 1)

        @block.vector
        def _(dve):
            dve.memset(zero_i, 0).then_inc(zeroed, 1)
            dve.memset(half[:, :], -0.5)
            for s in spare:
                dve.memset(s[:, :], 1.0)
            dve.memset(ones[:, :], 1.0)
            dve.memset(prev[:, :], 0.0)
            dve.memset(da[:, :, :, 0:1], 0.0)
            dve.memset(xin[:, :, 0:TAPS - 1], 0.0).then_inc(pads, 1)
            dve.wait_ge(const_loaded, 16)
            dve.tensor_copy(tok_f[:, :], cs[:, C_TOK:C_TOK + NT])
            dve.tensor_copy(spill_f[:, :], cs[:, C_TRASH:C_TRASH + NT * TOPK])
            dve.wait_ge(a_exp, 1)
            dve.tensor_scalar(a_sc[:, :, :], a_sc[:, :, :], -1.0, None, ALU.mult).then_inc(a_ready, 1)
            dve.wait_ge(wo_loaded, 16)
            dve.wait_ge(copied, 6)
            for k in range(KD):
                ins = dve.tensor_scalar(wo_sb[:, k, :], wo_sb[:, k, :], rms_c[:, k:k + 1], None, ALU.mult)
            ins.then_inc(a_ready, 1)
            dve.wait_ge(a_ready, 2)


def experts(nc, gate_up, down, x2_dram, table_dram, ye_dram, ident, spare):
    with ExitStack() as mem:
        def sb(name, shape, dt=F32):
            return mem.enter_context(nc.sbuf_tensor(name, shape, dt))

        def ps(name):
            return mem.enter_context(nc.psum_tensor(name, [P, 512], F32))

        def sem(name):
            return mem.enter_context(nc.semaphore(name))

        H2 = HID - P
        tab_i = sb("tab_i", [P, P], I32)
        tab_f = sb("tab_f", [P, P])
        tokens = sb("tokens", [P, EXPERTS, CJ], I32)
        idx = sb("idx", [P, 2, CJ], I32)
        xe = sb("xe", [P, 2, CJ, D])
        xeT = sb("xeT", [P, 2, KD, CAP])
        w1 = sb("w1", [P, 2, KD, 2 * HID])
        w2 = sb("w2", [P, 2, 2, D])
        sg = sb("sg", [P, 2, 2 * CAP])
        hid = sb("hid", [P, 2, 2 * CAP])
        ye = sb("ye", [P, 2, CJ, D])
        turn_ps = [ps(f"turn{j}") for j in range(CJ)]
        low_ps = [ps(f"low{s}") for s in range(2)]
        high_ps = [ps(f"high{s}") for s in range(2)]
        out_ps = [ps(f"out{j}") for j in range(CJ)]

        table_loaded = sem("table_loaded")
        table_float = sem("table_float")
        table_turned = sem("table_turned")
        tokens_ready = sem("tokens_ready")
        idx_ready = sem("idx_ready")
        gathered = [sem(f"gathered{s}") for s in range(2)]
        w1_loaded = [sem(f"w1_loaded{s}") for s in range(2)]
        w2_loaded = [sem(f"w2_loaded{s}") for s in range(2)]
        xe_turned = sem("xe_turned")
        xeT_ready = sem("xeT_ready")
        low_done = sem("low_done")
        high_done = sem("high_done")
        silu_low = sem("silu_low")
        silu_high = sem("silu_high")
        hid_ready = sem("hid_ready")
        out_done = sem("out_done")
        ye_ready = sem("ye_ready")
        ye_stored = [sem(f"ye_stored{s}") for s in range(2)]
        block = mem.enter_context(nc.Block())

        @block.sync
        def _(sp):
            sp.dma_start(tab_i[:, :], table_dram[0:SLOTS, :].rearrange("(n p) a -> n (p a)", p=P)).then_inc(table_loaded, 16)

            def load(e, slot):
                if not (isinstance(e, int) and e < 2):
                    wait(sp, high_done, e - 1)
                sp.dma_start(w1[:, slot, :, :], gate_up[e].rearrange("(k p) f -> p k f", p=P)).then_inc(w1_loaded[slot], 16)
                if not (isinstance(e, int) and e < 2):
                    wait(sp, out_done, CJ * (e - 1))
                sp.dma_start(w2[:, slot, 0, :], down[e, 0:P, :]).then_inc(w2_loaded[slot], 16)
                sp.dma_start(w2[P - H2:, slot, 1, :], down[e, P:, :]).then_inc(w2_loaded[slot], 16)

            load(0, 0)
            load(1, 1)

            def store(e, slot):
                for j in range(CJ):
                    wait(sp, ye_ready, CJ * e + j + 1)
                    sp.dma_start(ye_dram.rearrange("(e j p) d -> e j p d", e=EXPERTS, p=P)[e, j], ye[:, slot, j, :])\
                        .then_inc(ye_stored[slot], 16)

            with sp.Fori(0, (EXPERTS - 2) // 2) as i:
                for s in range(2):
                    load(2 * i + 2 + s, s)
                    store(2 * i + s, s)
            store(EXPERTS - 2, 0)
            store(EXPERTS - 1, 1)
            for s in range(2):
                sp.wait_ge(ye_stored[s], 16 * CJ * (EXPERTS // 2))

        @block.gpsimd
        def _(pool):
            def gather(e, slot, pair):
                if not (isinstance(e, int) and e < 2):
                    wait(pool, xe_turned, CJ * (e - 1))
                    wait(pool, gathered[slot], 16 * CJ * pair)
                pool.tensor_copy(idx[:, slot, :], tokens[:, e, :] if isinstance(e, int)
                                 else flat(tokens[:, bass.ds(e, 1), :])).then_inc(idx_ready, 1)
                wait(pool, idx_ready, e + 1)
                pause(pool, spare[1])
                for j in range(CJ):
                    pool.indirect_dma_start(xe[:, slot, j, :], None, x2_dram,
                                            bass.IndirectOffsetOnAxis(ap=idx[:, slot, j:j + 1], axis=0))\
                        .then_inc(gathered[slot], 16)

            wait(pool, tokens_ready, 1)
            gather(0, 0, 0)
            gather(1, 1, 0)
            with pool.Fori(0, (EXPERTS - 2) // 2) as i:
                for s in range(2):
                    gather(2 * i + 2 + s, s, i + 1)

        def turn(pe, e, slot, pair):
            wait(pe, gathered[slot], 16 * CJ * (pair + 1))
            for j in range(CJ):
                if not (isinstance(e, int) and e < 1):
                    wait(pe, xeT_ready, CJ * (e - 1) + j + 1)
                for k in range(KD):
                    ins = pe.transpose(turn_ps[j][:, k * P:(k + 1) * P], xe[:, slot, j, k * P:(k + 1) * P], ident)
                ins.then_inc(xe_turned, 1)

        def first_product(pe, e, slot, pair):
            wait(pe, xeT_ready, CJ * (e + 1))
            wait(pe, w1_loaded[slot], 16 * (pair + 1))
            if not (isinstance(e, int) and e < 2):
                wait(pe, hid_ready, 2 * (e - 1))
            for n in range(2):
                for k in range(KD):
                    ins = pe.matmul(low_ps[slot][:, n * CAP:(n + 1) * CAP], w1[:, slot, k, n * HID:n * HID + P],
                                    xeT[:, slot, k, :], start=(k == 0), stop=(k == KD - 1))
            ins.then_inc(low_done, 1)
            for n in range(2):
                for k in range(KD):
                    ins = pe.matmul(high_ps[slot][n * H2:(n + 1) * H2, 0:CAP], w1[:, slot, k, n * HID + P:(n + 1) * HID],
                                    xeT[:, slot, k, :], start=(k == 0), stop=(k == KD - 1))
            ins.then_inc(high_done, 1)

        def second_product(pe, e, slot, pair):
            wait(pe, hid_ready, 2 * (e + 1))
            wait(pe, w2_loaded[slot], 32 * (pair + 1))
            for j in range(CJ):
                if not (isinstance(e, int) and e < 1):
                    wait(pe, ye_ready, CJ * (e - 1) + j + 1)
                pe.matmul(out_ps[j][:, :], hid[:, slot, j * P:(j + 1) * P], w2[:, slot, 0, :], start=True, stop=False)
                pe.matmul(out_ps[j][:, :], hid[P - H2:, slot, CAP + j * P:CAP + (j + 1) * P], w2[P - H2:, slot, 1, :],
                          start=False, stop=True).then_inc(out_done, 1)

        @block.tensor
        def _(pe):
            pe.wait_ge(table_float, 1)
            pe.transpose(turn_ps[0][:, 0:P], tab_f[:, :], ident).then_inc(table_turned, 1)
            pe.wait_ge(tokens_ready, 1)
            turn(pe, 0, 0, 0)
            turn(pe, 1, 1, 0)
            first_product(pe, 0, 0, 0)
            turn(pe, 2, 0, 1)
            first_product(pe, 1, 1, 0)
            second_product(pe, 0, 0, 0)
            with pe.Fori(0, (EXPERTS - 4) // 2) as i:
                turn(pe, 2 * i + 3, 1, i + 1)
                first_product(pe, 2 * i + 2, 0, i + 1)
                second_product(pe, 2 * i + 1, 1, i)
                turn(pe, 2 * i + 4, 0, i + 2)
                first_product(pe, 2 * i + 3, 1, i + 1)
                second_product(pe, 2 * i + 2, 0, i + 1)
            last = EXPERTS // 2 - 1
            turn(pe, EXPERTS - 1, 1, last)
            first_product(pe, EXPERTS - 2, 0, last)
            second_product(pe, EXPERTS - 3, 1, last - 1)
            first_product(pe, EXPERTS - 1, 1, last)
            second_product(pe, EXPERTS - 2, 0, last)
            second_product(pe, EXPERTS - 1, 1, last)

        def take_turned(act, e, slot):
            for j in range(CJ):
                wait(act, xe_turned, CJ * e + j + 1)
                if not (isinstance(e, int) and e < 2):
                    wait(act, high_done, e - 1)
                act.activation(xeT[:, slot, :, j * P:(j + 1) * P], turn_ps[j][:, :].rearrange("p (k t) -> p k t", k=KD),
                               ACT.Copy).then_inc(xeT_ready, 1)

        def gates(act, e, slot):
            wait(act, low_done, e + 1)
            if not (isinstance(e, int) and e < 2):
                wait(act, hid_ready, 2 * (e - 1))
            act.activation(sg[:, slot, 0:CAP], low_ps[slot][:, 0:CAP], ACT.Silu).then_inc(silu_low, 1)
            wait(act, high_done, e + 1)
            act.activation(sg[P - H2:, slot, CAP:], high_ps[slot][0:H2, 0:CAP], ACT.Silu).then_inc(silu_high, 1)

        @block.scalar
        def _(act):
            take_turned(act, 0, 0)
            take_turned(act, 1, 1)
            gates(act, 0, 0)
            take_turned(act, 2, 0)
            gates(act, 1, 1)
            take_turned(act, 3, 1)
            gates(act, 2, 0)
            with act.Fori(1, (EXPERTS - 2) // 2) as i:
                take_turned(act, 2 * i + 2, 0)
                gates(act, 2 * i + 1, 1)
                take_turned(act, 2 * i + 3, 1)
                gates(act, 2 * i + 2, 0)
            gates(act, EXPERTS - 1, 1)

        def gated(dve, e, slot):
            if not (isinstance(e, int) and e < 2):
                wait(dve, out_done, CJ * (e - 1))
            wait(dve, silu_low, e + 1)
            dve.tensor_tensor(hid[:, slot, 0:CAP], low_ps[slot][:, CAP:], sg[:, slot, 0:CAP], ALU.mult).then_inc(hid_ready, 1)
            wait(dve, silu_high, e + 1)
            dve.tensor_tensor(hid[P - H2:, slot, CAP:], high_ps[slot][H2:, 0:CAP], sg[P - H2:, slot, CAP:], ALU.mult)\
                .then_inc(hid_ready, 1)

        def take_out(dve, e, slot, pair):
            if not (isinstance(e, int) and e < 2):
                wait(dve, ye_stored[slot], 16 * CJ * pair)
            for j in range(CJ):
                wait(dve, out_done, CJ * e + j + 1)
                dve.tensor_copy(ye[:, slot, j, :], out_ps[j][:, :]).then_inc(ye_ready, 1)

        @block.vector
        def _(dve):
            dve.wait_ge(table_loaded, 16)
            dve.tensor_copy(tab_f[:, :], tab_i[:, :]).then_inc(table_float, 1)
            dve.wait_ge(table_turned, 1)
            dve.tensor_copy(tokens[:, :, :].rearrange("p e j -> p (e j)"), turn_ps[0][:, 0:P]).then_inc(tokens_ready, 1)
            gated(dve, 0, 0)
            gated(dve, 1, 1)
            take_out(dve, 0, 0, 0)
            gated(dve, 2, 0)
            take_out(dve, 1, 1, 0)
            with dve.Fori(1, (EXPERTS - 2) // 2) as i:
                gated(dve, 2 * i + 1, 1)
                take_out(dve, 2 * i, 0, i)
                gated(dve, 2 * i + 2, 0)
                take_out(dve, 2 * i + 1, 1, i)
            gated(dve, EXPERTS - 1, 1)
            take_out(dve, EXPERTS - 2, 0, EXPERTS // 2 - 1)
            take_out(dve, EXPERTS - 1, 1, EXPERTS // 2 - 1)


def combine(nc, x2_dram, ye_dram, out, slot_idx, slot_w, half, spare):
    with ExitStack() as mem:
        def sb(name, shape, dt=F32):
            return mem.enter_context(nc.sbuf_tensor(name, shape, dt))

        def sem(name):
            return mem.enter_context(nc.semaphore(name))

        rows = sb("rows", [P, 2, TOPK, D])
        xr = sb("xr", [P, 2, D])
        even = sb("even", [P, 2, D])
        odd = sb("odd", [P, 2, D])
        stt = sb("stt", [P, 2, 6])
        mvc = sb("mvc", [P, 2, 2])
        root = sb("root", [P, 2])

        rows_gathered = [sem(f"rows_gathered{s}") for s in range(2)]
        xr_loaded = [sem(f"xr_loaded{s}") for s in range(2)]
        summed = sem("summed")
        var_ready = sem("var_ready")
        shifted = sem("var_shifted")
        root_ready = sem("root_ready")
        final = sem("final")
        out_stored = [sem(f"out_stored{s}") for s in range(2)]
        sum_steps = sem("sum_steps")
        PER = TOPK + 1
        block = mem.enter_context(nc.Block())

        @block.sync
        def _(sp):
            for t in range(TILES):
                s = t % 2
                if t >= 2:
                    sp.wait_ge(summed, t - 1)
                sp.dma_start(xr[:, s, :], x2_dram[t * P:(t + 1) * P, :]).then_inc(xr_loaded[s], 16)
                if t:
                    sp.wait_ge(final, t)
                    sp.dma_start(out.rearrange("b (t p) d -> (b t) p d", p=P)[t - 1], even[:, 1 - s, :])\
                        .then_inc(out_stored[1 - s], 16)
            sp.wait_ge(final, TILES)
            sp.dma_start(out.rearrange("b (t p) d -> (b t) p d", p=P)[TILES - 1], even[:, 1, :]).then_inc(out_stored[1], 16)
            for s in range(2):
                sp.wait_ge(out_stored[s], 16 * (TILES // 2))

        @block.gpsimd
        def _(pool):
            def root_of(t):
                s = t % 2
                pool.wait_ge(var_ready, t + 1)
                pool.tensor_scalar(root[:, s:s + 1], mvc[:, s, 1:2], 1.0, EPS, ALU.mult, ALU.add).then_inc(shifted, 1)
                pool.wait_ge(shifted, t + 1)
                pool.tensor_tensor(root[:, s:s + 1], root[:, s:s + 1], half[:, 0:1], ALU.pow).then_inc(root_ready, 1)

            for t in range(TILES):
                if t >= 2:
                    pool.wait_ge(summed, t - 1)
                for k in range(TOPK):
                    pool.indirect_dma_start(rows[:, t % 2, k, :], None, ye_dram,
                                            bass.IndirectOffsetOnAxis(ap=slot_idx[:, t, k:k + 1], axis=0))\
                        .then_inc(rows_gathered[t % 2], 16)
                if t >= 2:
                    root_of(t - 2)
            root_of(TILES - 2)
            root_of(TILES - 1)

        @block.vector
        def _(dve):
            def last_norm(t):
                s = t % 2
                dve.wait_ge(root_ready, t + 1)
                dve.tensor_scalar(even[:, s, :], even[:, s, :], mvc[:, s, 0:1], root[:, s:s + 1], ALU.subtract, ALU.mult)\
                    .then_inc(final, 1)

            for t in range(TILES):
                s = t % 2
                own = Chain(dve, sum_steps, PER * t)
                dve.wait_ge(xr_loaded[s], 16 * (t // 2 + 1))
                dve.wait_ge(rows_gathered[s], 16 * TOPK * (t // 2 + 1))
                if t >= 2:
                    dve.wait_ge(out_stored[s], 16 * (t // 2))
                for k in range(TOPK):
                    w = slot_w[:, t, k:k + 1]
                    if k == 1:
                        own.step(dve.tensor_scalar(odd[:, s, :], rows[:, s, 1, :], w, None, ALU.mult))
                        continue
                    part = odd if k % 2 else even
                    if k >= 2:
                        dve.wait_ge(sum_steps, PER * t + k - 1)
                    own.step(dve.scalar_tensor_tensor(out=part[:, s, :], in0=rows[:, s, k, :], scalar=w,
                                                      in1=xr[:, s, :] if k == 0 else part[:, s, :],
                                                      op0=ALU.mult, op1=ALU.add))
                own.settle()
                dve.tensor_tensor(even[:, s, :], even[:, s, :], odd[:, s, :], ALU.add).then_inc(summed, 1)
                dve.wait_ge(summed, t + 1)
                own.step(dve.bn_stats(stt[:, s, :], even[:, s, :]))
                own.settle()
                dve.bn_aggr(mvc[:, s, :], stt[:, s, :]).then_inc(var_ready, 1)
                if t:
                    last_norm(t - 1)
            last_norm(TILES - 1)


def constants():
    c = np.zeros((P, C_END), np.float32)
    p = np.arange(P)
    c[:, C_ID:C_ID + P] = np.eye(P)
    c[:, C_TRI:C_TRI + P] = p[:, None] < p[None, :]
    c[:, C_BD:C_BD + P] = p[:, None] // HD == p[None, :] // HD
    freq = np.float32(1 / 1024) ** np.linspace(0, 1, ROT, dtype=np.float32)
    t = np.arange(T, dtype=np.float32)
    theta = (t[:, None] * freq[None, :]).astype(np.float64).reshape(NT, P, ROT)
    cos, sin = np.cos(theta), np.sin(theta)
    for col, pair in ((C_ROTA, (cos, sin)), (C_ROTB, (sin, cos))):
        c[:, col:col + NT * 2 * ROT] = np.stack(pair, 2).transpose(1, 0, 2, 3).reshape(P, -1)
    start = 2.0 ** (-2.0 ** (-(np.log2(HEADS) - 3)))
    slopes = np.array([start * start ** i for i in range(HEADS)], np.float32)
    r = np.exp(-slopes).astype(np.float32).astype(np.float64)
    c[:, C_QD:C_QD + HEADS] = r[None, :] ** (p[:, None] + 1.0)
    c[:, C_KD:C_KD + HEADS] = r[None, :] ** (P - 1.0 - p[:, None])
    for g in range(GROUPS):
        c[:, C_RC + g] = r[g * HPG + p // HD] ** float(P)
    c[:, C_SLOT:C_SLOT + EXPERTS] = np.arange(EXPERTS) * CAP + 1
    c[:, C_TRASH:C_TRASH + NT * TOPK] = SLOTS + 1 + p[:, None] + P * np.arange(NT * TOPK)[None, :]
    c[:, C_TOK:C_TOK + NT] = p[:, None] + P * np.arange(NT)[None, :]
    diff = p[None, :] - p[:, None]
    dm = np.where(diff >= 0, r[:, None, None] ** np.maximum(diff, 0)[None], 0.0)
    dm = dm.reshape(GROUPS, HPG, P, P).transpose(2, 1, 0, 3).reshape(P, HPG, GROUPS * P)
    return c, dm.astype(np.float32)


_INS = ["x", "ctx_1024", "L0_attn_Wq", "L0_attn_Wk", "L0_attn_Wv", "L0_attn_Wo", "L0_attn_rms_w", "L0_xattn_in_proj_w",
        "L0_xattn_conv_w", "L0_xattn_conv_b", "L0_xattn_x_proj_w", "L0_xattn_dt_proj_w", "L0_xattn_dt_proj_b",
        "L0_xattn_A_log", "L0_xattn_D", "L0_ffn_router_weight", "L0_ffn_gate_up_proj", "L0_ffn_down_proj"]


def kernel(**inputs):
    import concourse.bacc as bacc
    from concourse.bass_utils import run_bass_kernel_spmd

    nc = bacc.Bacc("TRN2", target_bir_lowering=False, num_devices=1)
    arrays, args = {}, []
    table, decay = constants()
    for name, a in [(n, inputs[n]) for n in _INS] + [("table", table), ("decay", decay)]:
        a = np.ascontiguousarray(a)
        arrays[f"in_{name}"] = a
        args.append(nc.dram_tensor(f"in_{name}", a.shape, F32, kind="ExternalInput").ap())
    args.append(nc.dram_tensor("out", (B, T, D), F32, kind="ExternalOutput").ap())
    build(nc, *args)
    return run_bass_kernel_spmd(nc, [arrays], core_ids=[0]).results[0]["out"]
```

```python
from contextlib import ExitStack

import numpy as np

import concourse.bass as bass
from concourse import mybir

F32 = mybir.dt.float32
F32R = mybir.dt.float32r
I32 = mybir.dt.int32
ALU = mybir.AluOpType
ACT = mybir.ActivationFunctionType
AX = mybir.AxisListType

P = 128
B, T, D = 4, 512, 512
NT = T // P
KD = D // P
HEADS, HD = 16, 32
GROUPS = D // P
HPG = HEADS // GROUPS
ROT = HD // 4
CTX = 256
KC = CTX // P
INNER, STATE, RANK, TAPS = 512, 16, 16, 4
MI = INNER // P
NG = 4
EXPERTS, TOPK, CAP, HID = 64, 8, 256, 192
CJ = CAP // P
SLOTS = EXPERTS * CAP
NTOK = B * T
TILES = NTOK // P
EPS = 1e-5

C_ID = 0
C_TRI = C_ID + P
C_BD = C_TRI + P
C_ROTA = C_BD + P
C_ROTB = C_ROTA + NT * 2 * ROT
C_QD = C_ROTB + NT * 2 * ROT
C_KD = C_QD + HEADS
C_RC = C_KD + HEADS
C_SLOT = C_RC + GROUPS
C_TRASH = C_SLOT + EXPERTS
C_TOK = C_TRASH + NT * TOPK
C_END = C_TOK + NT

USES = {
    "A0": ["ctx0", "xdbl"] + [f"{n}{c}" for c in range(NT) for n in ("xT", "k", "qT", "O")] + ["yT0", "yT2", "x2T0", "x2T2"],
    "A1": ["ctx1"] + [f"{n}{c}" for c in range(NT) for n in ("q", "v", "kT") + (("I",) if c else ())]
          + ["yT1", "yT3", "x2T1", "x2T3"],
    "S0": [n for c in range(NT) for n in ([f"aT{c - 1}"] if c else []) + [f"r0_{c}", f"r2_{c}"]
           + ([f"U{c}"] if c < NT - 1 else [])] + [f"aT{NT - 1}", "logits"],
    "S1": [n for c in range(NT) for n in [f"r1_{c}"] + ([f"wo{c - 1}"] if c else []) + [f"r3_{c}"]] + [f"wo{NT - 1}", "pos"],
}
for _m in range(MI):
    USES[f"Y{_m}"] = [f"in{_m}", f"dt{_m}", f"y{_m}"]
BANK_OF = {use: (bank, n) for bank, uses in USES.items() for n, use in enumerate(uses)}

HEAD = 1

VECTOR_STEPS, SCALAR_STEPS, POOL_STEPS = 68, 5, 9


def wait(eng, sem, value):
    if isinstance(value, int) and value <= 0:
        return
    eng.wait_ge(sem, value)


def pause(eng, spare):
    eng.tensor_tensor(spare[:, 0:1], spare[:, 1:2], spare[:, 1:2], ALU.mult)


class Chain:

    def __init__(self, eng, sem, base=0):
        self.eng, self.sem, self.base, self.n = eng, sem, base, 0

    def step(self, instruction):
        instruction.then_inc(self.sem, 1)
        self.n += 1

    def settle(self):
        self.eng.wait_ge(self.sem, self.base + self.n)


def build(nc, x, ctx, wq, wk, wv, wo, rms_w, in_w, conv_w, conv_b, xp_w, dt_w, dt_b, a_log, d_skip,
          router, gate_up, down, consts, dmask, out, scratch="Internal"):
    bc_dram = nc.dram_tensor("bc_rows", [B, 2 * STATE, T], F32, kind=scratch).ap()
    x2_dram = nc.dram_tensor("x2_rows", [NTOK, D], F32, kind=scratch).ap()
    table_dram = nc.dram_tensor("slot_table", [2 * SLOTS, 1], I32, kind=scratch).ap()
    ye_dram = nc.dram_tensor("expert_rows", [SLOTS, D], F32, kind=scratch).ap()

    with ExitStack() as whole:
        def keep(name, shape, dt=F32):
            return whole.enter_context(nc.sbuf_tensor(name, shape, dt))

        cs = keep("cs", [P, C_END])
        slot_idx = keep("slot_idx", [P, TILES, TOPK], I32)
        slot_w = keep("slot_w", [P, TILES, TOPK])
        half = keep("half", [P, NT])
        spare = [keep(f"spare{i}", [P, 3]) for i in range(2)]
        ident = cs[:, C_ID:C_ID + P]

        mixers(nc, x, ctx, wq, wk, wv, wo, rms_w, in_w, conv_w, conv_b, xp_w, dt_w, dt_b, a_log, d_skip,
               router, consts, dmask, bc_dram, x2_dram, table_dram, cs, ident, slot_idx, slot_w, half, spare)
        experts(nc, gate_up, down, x2_dram, table_dram, ye_dram, ident, spare)
        combine(nc, x2_dram, ye_dram, out, slot_idx, slot_w, half, spare)


def mixers(nc, x, ctx, wq, wk, wv, wo, rms_w, in_w, conv_w, conv_b, xp_w, dt_w, dt_b, a_log, d_skip,
           router, consts, dmask_in, bc_dram, x2_dram, table_dram, cs, ident, slot_idx, slot_w, half, spare):
    with ExitStack() as mem:
        def sb(name, shape, dt=F32):
            return mem.enter_context(nc.sbuf_tensor(name, shape, dt))

        def sem(name):
            return mem.enter_context(nc.semaphore(name))

        bank = {n: mem.enter_context(nc.psum_tensor(f"bank_{n}", [P, 512], F32)) for n in USES}

        wqkv = sb("wqkv", [P, 3, KD, D])
        wo_sb = sb("wo_sb", [P, KD, D])
        in_wT = sb("in_wT", [P, KC, INNER])
        xp_wT = sb("xp_wT", [P, MI, RANK + 2 * STATE])
        dt_wT = sb("dt_wT", [RANK, INNER])
        rT = sb("rT", [P, KD, EXPERTS])
        dmask = sb("dmask", [P, HPG, GROUPS * P])
        conv_c = sb("conv_c", [P, MI, TAPS])
        vecs = sb("vecs", [P, 4 * MI])
        cb, dtb, dsk, rms_c = (vecs[:, n * MI:(n + 1) * MI] for n in range(4))
        a_sc = sb("a_sc", [P, MI, STATE])
        ones = sb("ones", [P, P])

        u = sb("u", [P, MI, T])
        dt = sb("dt", [P, MI, T])
        dtu = sb("dtu", [P, MI, T])
        xin = sb("xin", [P, MI, T + TAPS - 1])
        bmat = sb("bmat", [P, 2, NG, T])
        cmat = sb("cmat", [P, 2, NG, T])
        da = sb("da", [P, 2, NG, T])
        dbu = sb("dbu", [P, 2, NG, T])
        h = sb("h", [P, NG, T])
        x_in = sb("x_in", [P, 2, D])
        xT = sb("xT", [P, KD, P])
        qk = sb("qk", [P, 2 * HEADS, HD])
        v = sb("v", [P, D])
        kdec = sb("kdec", [P, HEADS, HD])
        rot = sb("rot", [P, 2, 2 * HEADS, 2, ROT])
        qT = sb("qT", [P, GROUPS, P])
        kT = sb("kT", [P, GROUPS, P])
        pr = sb("pr", [P, HPG, GROUPS, P])
        attn = sb("attn", [P, HEADS, HD])
        aT = sb("aT", [P, KD, P])
        kv = sb("kv", [P, GROUPS, P])
        kvs = sb("kvs", [P, GROUPS, P])
        x1 = sb("x1", [P, NT, D])
        junk = sb("junk", [P, D])
        ssq = sb("ssq", [P, NT])
        rms = sb("rms", [P, NT])
        st = sb("st", [P, NT, 6])
        mv = sb("mv", [P, NT, 2])
        rstd = sb("rstd", [P, NT])
        xdbl = sb("xdbl", [RANK + 2 * STATE, T])
        prev = sb("prev", [P, EXPERTS])
        top = sb("top", [P, NT, TOPK])
        small = sb("small", [P, 4, NT])
        idxf = sb("idxf", [P, 2, NT, TOPK])
        idx_s = sb("idx_s", [P, NT * TOPK], I32)
        tok_i = sb("tok_i", [P, NT], I32)
        spill_f = sb("spill_f", [P, NT * TOPK])

        tok_f = sb("tokf", [P, NT])
        ctx_sb = pr[:, :, :, :].rearrange("p a b c -> p (a b c)")[:, 0:NT * CTX].rearrange("p (t d) -> p t d", t=NT)
        ctxT = h
        zero_i = kv[:, :, :].rearrange("p a b -> p (a b)")[:, 0:SLOTS // P].bitcast(I32)
        flat_pr = pr[:, :, :, :].rearrange("p a b c -> p (a b c)")
        lsm, prob, mask = (flat_pr[:, n * NT * EXPERTS:(n + 1) * NT * EXPERTS].rearrange("p (j e) -> p j e", j=NT)
                           for n in range(3))
        acc = dbu[:, 0, :, :]
        ex = dbu[:, 0, :, :]
        ln = dbu[:, 1, :, :]
        lin = h
        y3 = xin[:, :, TAPS - 1:]
        sz = dtu
        x2 = u
        x2T = dbu[:, 0, :, :]
        tmp = rot[:, :, :, :, :].rearrange("p a h b c -> p (a h b c)")[:, 0:D]
        tmp2 = rot[:, :, :, :, :].rearrange("p a h b c -> p (a h b c)")[:, D:2 * D]
        hot = h[:, :, :].rearrange("p a b -> p (a b)").rearrange("p (j k e) -> p (j k) e", j=NT, k=TOPK)

        setup(nc, wq, wk, wv, wo, rms_w, in_w, conv_w, conv_b, xp_w, dt_w, dt_b, a_log, d_skip, router,
              consts, dmask_in, table_dram, cs, ident, half, spare, wqkv, wo_sb, in_wT, xp_wT, dt_wT, rT, dmask,
              conv_c, vecs, rms_c, a_sc, ones, xin, da, bmat, cmat, x1, prev, tok_f, spill_f, zero_i, bank)

        filled = {n: sem(f"filled_{n}") for n in USES}
        drained = {n: sem(f"drained_{n}") for n in USES}
        ctx_loaded = sem("ctx_loaded")
        x_loaded = [sem(f"x_loaded{i}") for i in range(2)]
        bc_stored = sem("bc_stored")
        bc_loaded = [sem(f"bc_loaded{i}") for i in range(2)]
        x2_stored = sem("x2_stored")
        scattered = sem("scattered")
        spread = sem("spread")
        convolved = sem("convolved")
        u_ready = sem("u_ready")
        soft_ready = sem("soft_ready")
        dt_ready = sem("dt_ready")
        dtu_ready = sem("dtu_ready")
        da_ready = sem("da_ready")
        dbu_ready = sem("dbu_ready")
        scanned = sem("scanned")
        yc_ready = sem("yc_ready")
        y_summed = sem("y_summed")
        rotated = sem("rotated")
        kdec_ready = sem("kdec_ready")
        kv_scaled = sem("kv_scaled")
        kv_ready = sem("kv_ready")
        squared = sem("squared")
        rms_ready = sem("rms_ready")
        stats_ready = sem("stats_ready")
        rstd_ready = sem("rstd_ready")
        x1_ready = sem("x1_ready")
        sz_ready = sem("sz_ready")
        y3_ready = sem("y3_ready")
        stats2_ready = sem("stats2_ready")
        rstd2_ready = sem("rstd2_ready")
        x2_ready = sem("x2_ready")
        exped = sem("exped")
        masked = sem("masked")
        routed = sem("routed")
        vector_steps = sem("vector_steps")
        scalar_steps = sem("scalar_steps")
        pool_steps = sem("pool_steps")

        def count(use, b):
            name, n = BANK_OF[use]
            return name, len(USES[name]) * b + n + 1

        def to_fill(eng, use, b):
            name, value = count(use, b)
            wait(eng, drained[name], HEAD + value - 1)
            return bank[name]

        def full(eng, use, b):
            name, value = count(use, b)
            wait(eng, filled[name], value)
            return bank[name]

        def taken(eng, use, b):
            name, value = count(use, b)
            wait(eng, drained[name], HEAD + value)

        def fill_sem(use):
            return filled[BANK_OF[use][0]]

        def drain_sem(use):
            return drained[BANK_OF[use][0]]

        def last_sequence_over(eng, b):
            wait(eng, routed, HEAD + b)

        SCANS = MI * (STATE // NG)

        def state_ready(eng, c, b):
            if c == 0:
                taken(eng, "U0", b)
            else:
                wait(eng, kv_ready, (NT - 2) * b + c)

        def states_summed(eng, n, b):
            g, m = divmod(n, MI)
            if g < STATE // NG - 1:
                wait(eng, y_summed, (SCANS - MI) * b + n + 1)
            else:
                full(eng, f"y{m}", b)

        block = mem.enter_context(nc.Block())

        @block.sync
        def _(sp):
            with sp.Fori(0, B) as b:
                last_sequence_over(sp, b)
                sp.dma_start(ctx_sb, ctx[b].rearrange("(t p) d -> p t d", p=P)).then_inc(ctx_loaded, 16)

                def load_x(c):
                    if c >= 2:
                        wait(sp, stats_ready, NT * b + c - 1)
                    sp.dma_start(x_in[:, c % 2, :], x[b, c * P:(c + 1) * P, :]).then_inc(x_loaded[c % 2], 16)

                load_x(0)
                load_x(1)
                taken(sp, "xdbl", b)
                sp.dma_start(bc_dram[b], xdbl[RANK:, :]).then_inc(bc_stored, 16)
                wait(sp, bc_stored, 16 * (b + 1))
                for g in range(STATE // NG):
                    if g >= 2:
                        wait(sp, yc_ready, SCANS * b + MI * (g - 1))
                    for dst, row in ((bmat, NG * g), (cmat, STATE + NG * g)):
                        sp.dma_start(dst[:, g % 2, :, :], bc_dram[b, row:row + NG, :].partition_broadcast(P))\
                            .then_inc(bc_loaded[g % 2], 16)
                    if 1 <= g < 3:
                        load_x(g + 1)
                for j in range(NT):
                    wait(sp, x2_ready, NT * b + j + 1)
                    sp.dma_start(x2_dram.rearrange("(b t p) d -> b t p d", b=B, p=P)[b, j], x2[:, j, :])\
                        .then_inc(x2_stored, 16)
            sp.wait_ge(x2_stored, 16 * NT * B)
            sp.wait_ge(bc_stored, 16 * B)

        @block.tensor
        def _(pe):
            with pe.Fori(0, B) as b:
                last_sequence_over(pe, b)
                wait(pe, ctx_loaded, 16 * (b + 1))
                for k in range(KC):
                    ps = to_fill(pe, f"ctx{k}", b)
                    for t in range(NT):
                        ins = pe.transpose(ps[:, t * P:(t + 1) * P], ctx_sb[:, t, k * P:(k + 1) * P], ident)
                    ins.then_inc(fill_sem(f"ctx{k}"), 1)
                for k in range(KC):
                    taken(pe, f"ctx{k}", b)
                for m in range(MI):
                    ps = to_fill(pe, f"in{m}", b)
                    for k in range(KC):
                        ins = pe.matmul(ps[:, :], in_wT[:, k, m * P:(m + 1) * P], ctxT[:, k, :],
                                        start=(k == 0), stop=(k == KC - 1))
                    ins.then_inc(fill_sem(f"in{m}"), 1)
                ps = to_fill(pe, "xdbl", b)
                for m in range(MI):
                    wait(pe, u_ready, MI * b + m + 1)
                    ins = pe.matmul(ps[0:RANK + 2 * STATE, :], xp_wT[:, m, :], u[:, m, :],
                                    start=(m == 0), stop=(m == MI - 1))
                ins.then_inc(fill_sem("xdbl"), 1)
                taken(pe, "xdbl", b)
                for m in range(MI):
                    ps = to_fill(pe, f"dt{m}", b)
                    pe.matmul(ps[:, :], dt_wT[:, m * P:(m + 1) * P], xdbl[0:RANK, :], start=True, stop=True)\
                        .then_inc(fill_sem(f"dt{m}"), 1)

                def sum_states(g, m):
                    n = MI * g + m
                    if g == 0:
                        to_fill(pe, f"y{m}", b)
                    wait(pe, yc_ready, SCANS * b + n + 1)
                    for i in range(NG):
                        ins = pe.matmul(bank[f"Y{m}"][:, :], ident, dbu[:, n % 2, i, :],
                                        start=(g == 0 and i == 0), stop=(g == STATE // NG - 1 and i == NG - 1))
                    ins.then_inc(fill_sem(f"y{m}") if g == STATE // NG - 1 else y_summed, 1)

                def turn(c):
                    wait(pe, x_loaded[c % 2], 16 * (2 * b + c // 2 + 1))
                    ps = to_fill(pe, f"xT{c}", b)
                    for k in range(KD):
                        ins = pe.transpose(ps[:, k * P:(k + 1) * P], x_in[:, c % 2, k * P:(k + 1) * P], ident)
                    ins.then_inc(fill_sem(f"xT{c}"), 1)

                def project(c, name):
                    taken(pe, f"xT{c}", b)
                    ps = to_fill(pe, f"{name}{c}", b)
                    for k in range(KD):
                        ins = pe.matmul(ps[:, :], xT[:, k, :], wqkv[:, "qkv".index(name), k, :],
                                        start=(k == 0), stop=(k == KD - 1))
                    ins.then_inc(fill_sem(f"{name}{c}"), 1)

                def turn_qk(c):
                    wait(pe, rotated, NT * b + c + 1)
                    for n, name in enumerate(("qT", "kT")):
                        ps = to_fill(pe, f"{name}{c}", b)
                        for g in range(GROUPS):
                            src = qk[:, n * HEADS + g * HPG:n * HEADS + (g + 1) * HPG, :].rearrange("p h d -> p (h d)")
                            ins = pe.transpose(ps[:, g * P:(g + 1) * P], src, ident)
                        ins.then_inc(fill_sem(f"{name}{c}"), 1)

                def scores(c, r):
                    taken(pe, f"qT{c}", b)
                    taken(pe, f"kT{c}", b)
                    ps = to_fill(pe, f"r{r}_{c}", b)
                    for g in range(GROUPS):
                        ins = pe.matmul(ps[:, g * P:(g + 1) * P], kT[r * HD:(r + 1) * HD, g, :],
                                        qT[r * HD:(r + 1) * HD, g, :], start=True, stop=True)
                    ins.then_inc(fill_sem(f"r{r}_{c}"), 1)

                def mix_values(c):
                    taken(pe, f"v{c}", b)
                    for r in range(2, HPG):
                        taken(pe, f"r{r}_{c}", b)
                    ps = to_fill(pe, f"O{c}", b)
                    for hd in range(HEADS):
                        ins = pe.matmul(ps[:, hd * HD:(hd + 1) * HD], pr[:, hd % HPG, hd // HPG, :],
                                        v[:, hd * HD:(hd + 1) * HD], start=True, stop=True)
                    ins.then_inc(fill_sem(f"O{c}"), 1)
                    if c:
                        state_ready(pe, c - 1, b)
                        ps = to_fill(pe, f"I{c}", b)
                        for g in range(GROUPS):
                            ins = pe.matmul(ps[:, g * P:(g + 1) * P], qT[:, g, :], kv[:, g, :], start=True, stop=True)
                        ins.then_inc(fill_sem(f"I{c}"), 1)
                    if c < NT - 1:
                        wait(pe, kdec_ready, (NT - 1) * b + c + 1)
                        ps = to_fill(pe, f"U{c}", b)
                        for g in range(GROUPS):
                            ins = pe.matmul(ps[:, g * P:(g + 1) * P],
                                            kdec[:, g * HPG:(g + 1) * HPG, :].rearrange("p h d -> p (h d)"),
                                            v[:, g * P:(g + 1) * P], start=True, stop=True)
                        ins.then_inc(fill_sem(f"U{c}"), 1)

                def turn_mixed(c):
                    taken(pe, f"O{c}", b)
                    ps = to_fill(pe, f"aT{c}", b)
                    for k in range(KD):
                        src = attn[:, k * HPG:(k + 1) * HPG, :].rearrange("p h d -> p (h d)")
                        ins = pe.transpose(ps[:, k * P:(k + 1) * P], src, ident)
                    ins.then_inc(fill_sem(f"aT{c}"), 1)

                def project_out(c):
                    taken(pe, f"aT{c}", b)
                    ps = to_fill(pe, f"wo{c}", b)
                    for k in range(KD):
                        ins = pe.matmul(ps[:, :], aT[:, k, :], wo_sb[:, k, :], start=(k == 0), stop=(k == KD - 1))
                    ins.then_inc(fill_sem(f"wo{c}"), 1)

                for c in range(NT):
                    turn(c)
                    project(c, "q")
                    sum_states(c, 0)
                    project(c, "k")
                    project(c, "v")
                    sum_states(c, 1)
                    if c:
                        turn_mixed(c - 1)
                    turn_qk(c)
                    scores(c, 0)
                    scores(c, 1)
                    if c:
                        project_out(c - 1)
                    sum_states(c, 2)
                    scores(c, 2)
                    scores(c, 3)
                    sum_states(c, 3)
                    mix_values(c)
                turn_mixed(NT - 1)
                project_out(NT - 1)
                wait(pe, y3_ready, MI * (b + 1))
                for j in range(NT):
                    ps = to_fill(pe, f"yT{j}", b)
                    for m in range(MI):
                        ins = pe.transpose(ps[:, m * P:(m + 1) * P], y3[:, m, j * P:(j + 1) * P], ident)
                    ins.then_inc(fill_sem(f"yT{j}"), 1)
                for j in range(NT):
                    wait(pe, x2_ready, NT * b + j + 1)
                    ps = to_fill(pe, f"x2T{j}", b)
                    for k in range(KD):
                        ins = pe.transpose(ps[:, k * P:(k + 1) * P], x2[:, j, k * P:(k + 1) * P], ident)
                    ins.then_inc(fill_sem(f"x2T{j}"), 1)
                ps = to_fill(pe, "logits", b)
                for j in range(NT):
                    taken(pe, f"x2T{j}", b)
                    for k in range(KD):
                        ins = pe.matmul(ps[:, j * EXPERTS:(j + 1) * EXPERTS], x2T[:, j, k * P:(k + 1) * P],
                                        rT[:, k, :], start=(k == 0), stop=(k == KD - 1))
                ins.then_inc(fill_sem("logits"), 1)
                wait(pe, masked, b + 1)
                ps = to_fill(pe, "pos", b)
                for j in range(NT):
                    dst = ps[:, j * EXPERTS:(j + 1) * EXPERTS]
                    pe.matmul(dst, cs[:, C_TRI:C_TRI + P], mask[:, j, :], start=True, stop=False)
                    for i in range(j):
                        pe.matmul(dst, ones[:, :], mask[:, i, :], start=False, stop=False)
                    ins = pe.matmul(dst, ones[:, :], prev[:, :], start=False, stop=True)
                ins.then_inc(fill_sem("pos"), 1)

        @block.scalar
        def _(act):
            with act.Fori(0, B) as b:
                last_sequence_over(act, b)
                own = Chain(act, scalar_steps, SCALAR_STEPS * b)

                def take(use, dst):
                    act.activation(dst, full(act, use, b)[0:dst.shape[0], :], ACT.Copy).then_inc(drain_sem(use), 1)

                for k in range(KC):
                    take(f"ctx{k}", ctxT[:, k, :])
                for m in range(MI):
                    take(f"in{m}", xin[:, m, TAPS - 1:])
                for m in range(MI):
                    wait(act, convolved, MI * b + m + 1)
                    act.activation(u[:, m, :], acc[:, m, :], ACT.Silu, bias=cb[:, m:m + 1]).then_inc(u_ready, 1)
                take("xdbl", xdbl[:, :])
                wait(act, u_ready, MI * (b + 1))
                for m in range(MI):
                    ps = full(act, f"dt{m}", b)
                    own.step(act.activation(ex[:, m, :], ps[:, :], ACT.Abs, bias=dtb[:, m:m + 1]))
                    act.activation(lin[:, m, :], ps[:, :], ACT.Relu, bias=dtb[:, m:m + 1]).then_inc(drain_sem(f"dt{m}"), 1)
                own.settle()
                own.step(act.activation(ex, ex, ACT.Exp, scale=-1.0))
                own.settle()
                act.activation(ln, ex, ACT.Ln, bias=1.0).then_inc(soft_ready, 1)

                def decays(n):
                    g, m = divmod(n, MI)
                    if n == 0:
                        wait(act, dt_ready, b + 1)
                    if n >= 2:
                        wait(act, scanned, SCANS * b + n - 1)
                    for i in range(NG):
                        s = NG * g + i
                        ins = act.activation(da[:, n % 2, i, 1:], dt[:, m, 1:], ACT.Exp, scale=a_sc[:, m, s:s + 1])
                    ins.then_inc(da_ready, 1)

                def square(c):
                    taken(act, f"O{c}", b)
                    act.activation(junk[:, :], flat(attn[:, :, :]), ACT.Square, accum_out=ssq[:, c:c + 1]).then_inc(squared, 1)

                decays(0)
                for c in range(NT):
                    decays(MI * c + 1)
                    take(f"xT{c}", flat(xT[:, :, :]))
                    take(f"q{c}", flat(qk[:, 0:HEADS, :]))
                    if c:
                        square(c - 1)
                    decays(MI * c + 2)
                    take(f"k{c}", flat(qk[:, HEADS:, :]))
                    take(f"v{c}", v[:, :])
                    decays(MI * c + 3)
                    if c:
                        take(f"aT{c - 1}", flat(aT[:, :, :]))
                    take(f"qT{c}", flat(qT[:, :, :]))
                    take(f"kT{c}", flat(kT[:, :, :]))
                    if c < NT - 1:
                        decays(MI * c + 4)
                square(NT - 1)
                take(f"aT{NT - 1}", flat(aT[:, :, :]))
                for m in range(MI):
                    wait(act, x1_ready, NT * b + m + 1)
                    if m == 0:
                        wait(act, dbu_ready, SCANS * (b + 1))
                    act.activation(sz[:, m, :], x1[:, m, :], ACT.Silu).then_inc(sz_ready, 1)
                for j in range(NT):
                    take(f"x2T{j}", x2T[:, j, :])
                taken(act, "logits", b)
                act.activation(lsm[:, :, :], lsm[:, :, :], ACT.Exp).then_inc(exped, 1)
                wait(act, x2_stored, 16 * NT * (b + 1))
            assert own.n == SCALAR_STEPS, own.n

        @block.gpsimd
        def _(pool):
            with pool.Fori(0, B) as b:
                last_sequence_over(pool, b)
                own = Chain(pool, pool_steps, POOL_STEPS * b)

                def root(dst, src, scale, done):
                    pause(pool, spare[1])
                    own.step(pool.tensor_scalar(dst, src, scale, EPS, ALU.mult, ALU.add))
                    own.settle()
                    pool.tensor_tensor(dst, dst, half[:, 0:dst.shape[1]], ALU.pow).then_inc(done, 1)

                def inputs(n):
                    g, m = divmod(n, MI)
                    wait(pool, bc_loaded[g % 2], 64 * b + 32 * (g // 2 + 1))
                    if n >= 2:
                        states_summed(pool, n - 2, b)
                    pool.tensor_tensor(dbu[:, n % 2, :, :], bmat[:, g % 2, :, :],
                                       dtu[:, m, :].unsqueeze(1).broadcast_to([P, NG, T]), ALU.mult).then_inc(dbu_ready, 1)

                wait(pool, dt_ready, b + 1)
                for m in range(MI):
                    pool.tensor_tensor(dtu[:, m, :], dt[:, m, :], u[:, m, :], ALU.mult).then_inc(dtu_ready, 1)
                wait(pool, dtu_ready, MI * (b + 1))
                for c in range(NT):
                    inputs(MI * c)
                    if c >= 2:
                        wait(pool, stats_ready, NT * b + c - 1)
                        root(rstd[:, c - 2:c - 1], mv[:, c - 2, 1:2], 1.0, rstd_ready)
                    inputs(MI * c + 1)
                    inputs(MI * c + 2)
                    if c:
                        wait(pool, squared, NT * b + c)
                        root(rms[:, c - 1:c], ssq[:, c - 1:c], 1.0 / D, rms_ready)
                    inputs(MI * c + 3)
                    if c < NT - 1:
                        wait(pool, rotated, NT * b + c + 1)
                        if c:
                            full(pool, f"U{c - 1}", b)
                        pool.tensor_tensor(kdec[:, :, :], qk[:, HEADS:, :],
                                           cs[:, C_KD:C_KD + HEADS].unsqueeze(2).broadcast_to([P, HEADS, HD]),
                                           ALU.mult).then_inc(kdec_ready, 1)
                    if 1 <= c < NT - 1:
                        state_ready(pool, c - 1, b)
                        pool.tensor_tensor(kvs[:, :, :], kv[:, :, :],
                                           cs[:, C_RC:C_RC + GROUPS].unsqueeze(2).broadcast_to([P, GROUPS, P]),
                                           ALU.mult).then_inc(kv_scaled, 1)
                wait(pool, stats_ready, NT * b + NT - 1)
                root(rstd[:, NT - 2:NT - 1], mv[:, NT - 2, 1:2], 1.0, rstd_ready)
                wait(pool, squared, NT * (b + 1))
                root(rms[:, NT - 1:NT], ssq[:, NT - 1:NT], 1.0 / D, rms_ready)
                wait(pool, stats_ready, NT * (b + 1))
                root(rstd[:, NT - 1:NT], mv[:, NT - 1, 1:2], 1.0, rstd_ready)
                wait(pool, stats2_ready, NT * (b + 1))
                wait(pool, x1_ready, NT * (b + 1))
                root(rstd[:, :], mv[:, :, 1], 1.0, rstd2_ready)
                wait(pool, routed, HEAD + b + 1)
                pause(pool, spare[1])
                for j in range(NT):
                    for k in range(TOPK):
                        n = j * TOPK + k
                        pool.indirect_dma_start(table_dram, bass.IndirectOffsetOnAxis(ap=idx_s[:, n:n + 1], axis=0),
                                                tok_i[:, j:j + 1], None).then_inc(scattered, 16)
                wait(pool, scattered, 16 * NT * TOPK * (b + 1))
                wait(pool, spread, HEAD + b)
                pool.tensor_tensor(spare[1][:, 2:3], spare[1][:, 1:2], spare[1][:, 1:2], ALU.mult).then_inc(spread, 1)
            pool.wait_ge(scattered, 16 * TILES * TOPK)
            assert own.n == POOL_STEPS, own.n

        @block.vector
        def _(dve):
            for s in (*drained.values(), routed, spread):
                dve.sem_inc(s, HEAD)
            with dve.Fori(0, B) as b:
                last_sequence_over(dve, b)
                wait(dve, spread, HEAD + b)
                own = Chain(dve, vector_steps, VECTOR_STEPS * b)

                for t in range(TAPS):
                    for m in range(MI):
                        src = xin[:, m, t:t + T]
                        if t == 0:
                            taken(dve, f"in{m}", b)
                            own.step(dve.tensor_scalar(acc[:, m, :], src, conv_c[:, m, 0:1], None, ALU.mult))
                            continue
                        ins = dve.scalar_tensor_tensor(out=acc[:, m, :], in0=src, scalar=conv_c[:, m, t:t + 1],
                                                       in1=acc[:, m, :], op0=ALU.mult, op1=ALU.add)
                        if t < TAPS - 1:
                            own.step(ins)
                        else:
                            ins.then_inc(convolved, 1)
                    if t < TAPS - 1:
                        own.settle()
                wait(dve, soft_ready, b + 1)
                own.step(dve.tensor_scalar(dt[:, :, :], ex, 1.0, None, ALU.add))
                own.settle()
                own.step(dve.scalar_tensor_tensor(out=dt[:, :, :], in0=dt[:, :, :], scalar=1.0, in1=ex,
                                                  op0=ALU.subtract, op1=ALU.subtract))
                own.settle()
                own.step(dve.tensor_tensor(dt[:, :, :], ln, dt[:, :, :], ALU.subtract))
                own.settle()
                own.step(dve.scalar_tensor_tensor(out=dt[:, :, :], in0=dt[:, :, :], scalar=0.0, in1=ex,
                                                  op0=ALU.max, op1=ALU.min))
                own.settle()
                dve.tensor_tensor(dt[:, :, :], lin[:, :, :], dt[:, :, :], ALU.add).then_inc(dt_ready, 1)
                wait(dve, dt_ready, b + 1)

                def scan(n):
                    g, m = divmod(n, MI)
                    if n:
                        wait(dve, yc_ready, SCANS * b + n)
                    wait(dve, da_ready, SCANS * b + n + 1)
                    wait(dve, dbu_ready, SCANS * b + n + 1)
                    dve.tensor_tensor_scan(h[:, :, :].rearrange("p s t -> p (s t)"),
                                           da[:, n % 2, :, :].rearrange("p s t -> p (s t)"),
                                           dbu[:, n % 2, :, :].rearrange("p s t -> p (s t)"),
                                           0.0, ALU.mult, ALU.add).then_inc(scanned, 1)
                    wait(dve, scanned, SCANS * b + n + 1)
                    if m == 0:
                        wait(dve, bc_loaded[g % 2], 64 * b + 32 * (g // 2 + 1))
                    dve.tensor_tensor(dbu[:, n % 2, :, :], h[:, :, :], cmat[:, g % 2, :, :], ALU.mult).then_inc(yc_ready, 1)

                def rotate(c):
                    taken(dve, f"q{c}", b)
                    taken(dve, f"k{c}", b)
                    if c >= 2:
                        taken(dve, f"O{c - 1}", b)
                        state_ready(dve, c - 1, b)
                    pair = [P, 2 * HEADS, 2, ROT]
                    for n, (part, col) in enumerate(((0, C_ROTA), (HD // 2, C_ROTB))):
                        table = cs[:, col + c * 2 * ROT:col + (c + 1) * 2 * ROT].rearrange("p (a r) -> p a r", a=2)
                        own.step(dve.tensor_tensor(rot[:, n, :, :, :], qk[:, :, part:part + ROT].unsqueeze(2).broadcast_to(pair),
                                                   table.unsqueeze(1).broadcast_to(pair), ALU.mult))
                    own.settle()
                    own.step(dve.tensor_tensor(qk[:, :, 0:ROT], rot[:, 0, :, 0, :], rot[:, 1, :, 0, :], ALU.add))
                    dve.tensor_tensor(qk[:, :, HD // 2:HD // 2 + ROT], rot[:, 1, :, 1, :], rot[:, 0, :, 1, :], ALU.subtract)\
                        .then_inc(rotated, 1)

                def mask_scores(c, r):
                    use = f"r{r}_{c}"
                    dve.tensor_tensor(pr[:, r, :, :].rearrange("p g c -> p (g c)"), full(dve, use, b)[:, :], dmask[:, r, :],
                                      ALU.mult).then_inc(drain_sem(use), 1)

                def mixed_heads(c):
                    if c == 0:
                        dve.tensor_copy(flat(attn[:, :, :]), full(dve, "O0", b)[:, :]).then_inc(drain_sem("O0"), 1)
                    else:
                        inter = full(dve, f"I{c}", b)
                        full(dve, f"aT{c - 1}", b)
                        wait(dve, squared, NT * b + c)
                        wait(dve, rotated, NT * b + c + 1)
                        dve.tensor_tensor(tmp.rearrange("p (h d) -> p h d", h=HEADS),
                                          inter[:, :].rearrange("p (h d) -> p h d", h=HEADS),
                                          cs[:, C_QD:C_QD + HEADS].unsqueeze(2).broadcast_to([P, HEADS, HD]), ALU.mult)\
                            .then_inc(drain_sem(f"I{c}"), 1)
                        taken(dve, f"I{c}", b)
                        dve.tensor_tensor(flat(attn[:, :, :]), full(dve, f"O{c}", b)[:, :], tmp, ALU.add)\
                            .then_inc(drain_sem(f"O{c}"), 1)
                    if c < NT - 1:
                        update = full(dve, f"U{c}", b)[:, :].rearrange("p (g e) -> p g e", g=GROUPS)
                        blocks = cs[:, C_BD:C_BD + P].unsqueeze(1).broadcast_to([P, GROUPS, P])
                        dst = kv[:, :, :] if c == 0 else tmp2.rearrange("p (g e) -> p g e", g=GROUPS)
                        dve.tensor_tensor(dst, update, blocks, ALU.mult).then_inc(drain_sem(f"U{c}"), 1)
                        if c:
                            wait(dve, kv_scaled, (NT - 2) * b + c)
                            taken(dve, f"U{c}", b)
                            dve.tensor_tensor(kv[:, :, :], kvs[:, :, :], dst, ALU.add).then_inc(kv_ready, 1)

                def add_attention(c):
                    wait(dve, rms_ready, NT * b + c + 1)
                    wait(dve, x_loaded[c % 2], 16 * (2 * b + c // 2 + 1))
                    dve.scalar_tensor_tensor(out=x1[:, c, :], in0=full(dve, f"wo{c}", b)[:, :], scalar=rms[:, c:c + 1],
                                             in1=x_in[:, c % 2, :], op0=ALU.mult, op1=ALU.add).then_inc(drain_sem(f"wo{c}"), 1)
                    taken(dve, f"wo{c}", b)
                    own.step(dve.bn_stats(st[:, c, :], x1[:, c, :]))
                    own.settle()
                    pause(dve, spare[0])
                    dve.bn_aggr(mv[:, c, :], st[:, c, :]).then_inc(stats_ready, 1)

                def normalise(dst, c, done):
                    dve.tensor_scalar(dst[:, c, :], dst[:, c, :], mv[:, c, 0:1], rstd[:, c:c + 1], ALU.subtract, ALU.mult)\
                        .then_inc(done, 1)

                def first_norm(c):
                    wait(dve, stats_ready, NT * b + c + 1)
                    wait(dve, rstd_ready, NT * b + c + 1)
                    normalise(x1, c, x1_ready)

                for c in range(NT):
                    scan(MI * c)
                    if c:
                        mixed_heads(c - 1)
                    scan(MI * c + 1)
                    rotate(c)
                    scan(MI * c + 2)
                    mask_scores(c, 0)
                    mask_scores(c, 1)
                    if c:
                        add_attention(c - 1)
                    scan(MI * c + 3)
                    mask_scores(c, 2)
                    mask_scores(c, 3)
                    if c:
                        first_norm(c - 1)
                mixed_heads(NT - 1)
                for m in range(MI):
                    dve.scalar_tensor_tensor(out=y3[:, m, :], in0=u[:, m, :], scalar=dsk[:, m:m + 1],
                                             in1=full(dve, f"y{m}", b)[:, :], op0=ALU.mult, op1=ALU.add)\
                        .then_inc(drain_sem(f"y{m}"), 1)
                add_attention(NT - 1)
                first_norm(NT - 1)
                for m in range(MI):
                    taken(dve, f"y{m}", b)
                    wait(dve, sz_ready, MI * b + m + 1)
                    dve.tensor_tensor(y3[:, m, :], y3[:, m, :], sz[:, m, :], ALU.mult).then_inc(y3_ready, 1)
                wait(dve, x1_ready, NT * (b + 1))
                for j in range(NT):
                    dve.tensor_tensor(x2[:, j, :], full(dve, f"yT{j}", b)[:, :], x1[:, j, :], ALU.add)\
                        .then_inc(drain_sem(f"yT{j}"), 1)
                    taken(dve, f"yT{j}", b)
                    own.step(dve.bn_stats(st[:, j, :], x2[:, j, :]))
                own.settle()
                pause(dve, spare[0])
                for j in range(NT):
                    dve.bn_aggr(mv[:, j, :], st[:, j, :]).then_inc(stats2_ready, 1)
                wait(dve, stats2_ready, NT * (b + 1))
                wait(dve, rstd2_ready, b + 1)
                for j in range(NT):
                    normalise(x2, j, x2_ready)

                def each(t):
                    return t.unsqueeze(2).broadcast_to([P, NT, EXPERTS])

                logits = full(dve, "logits", b)[:, 0:NT * EXPERTS].rearrange("p (j e) -> p j e", j=NT)
                own.step(dve.tensor_reduce(small[:, 0, :], logits, AX.X, ALU.max))
                own.settle()
                dve.tensor_tensor(lsm[:, :, :], logits, each(small[:, 0, :]), ALU.subtract).then_inc(drain_sem("logits"), 1)
                wait(dve, exped, b + 1)
                own.step(dve.tensor_reduce(small[:, 1, :], lsm[:, :, :], AX.X, ALU.add))
                own.settle()
                own.step(dve.reciprocal(small[:, 2, :], small[:, 1, :]))
                own.settle()
                own.step(dve.tensor_tensor(prob[:, :, :], lsm[:, :, :], each(small[:, 2, :]), ALU.mult))
                own.settle()
                pause(dve, spare[0])
                for j in range(NT):
                    own.step(dve.max(top[:, j, :], prob[:, j, :]))
                own.settle()
                pause(dve, spare[0])
                for j in range(NT):
                    own.step(dve.match_replace(out=mask[:, j, :], in_to_replace=top[:, j, :], in_values=prob[:, j, :],
                                               imm_value=-1.0))
                own.step(dve.tensor_reduce(small[:, 3, :], top[:, :, :], AX.X, ALU.add))
                own.settle()
                dve.tensor_scalar(mask[:, :, :], mask[:, :, :], 0.0, None, ALU.is_lt).then_inc(masked, 1)
                own.step(dve.reciprocal(small[:, 0, :], small[:, 3, :]))
                own.settle()
                own.step(dve.tensor_tensor(lsm[:, :, :], prob[:, :, :], each(small[:, 0, :]), ALU.mult))
                own.settle()
                wait(dve, masked, b + 1)
                place = full(dve, "pos", b)[:, 0:NT * EXPERTS].rearrange("p (j e) -> p j e", j=NT)
                own.step(dve.scalar_tensor_tensor(out=prob[:, :, :], in0=place, scalar=float(CAP), in1=mask[:, :, :],
                                                  op0=ALU.is_lt, op1=ALU.mult))
                taken(dve, f"O{NT - 1}", b)
                key = tmp[:, 0:NT * EXPERTS].rearrange("p (j e) -> p j e", j=NT)
                dve.tensor_tensor(key, place, cs[:, C_SLOT:C_SLOT + EXPERTS].unsqueeze(1).broadcast_to([P, NT, EXPERTS]),
                                  ALU.add).then_inc(drain_sem("pos"), 1)
                chosen = tmp[:, NT * EXPERTS:NT * EXPERTS + EXPERTS]
                own.step(dve.tensor_reduce(chosen, mask[:, :, :].rearrange("p j e -> p e j"), AX.X, ALU.add))
                taken(dve, "pos", b)
                own.settle()
                own.step(dve.tensor_tensor(prev[:, :], prev[:, :], chosen, ALU.add))
                own.step(dve.tensor_tensor(key, key, prob[:, :, :], ALU.mult))
                own.step(dve.tensor_tensor(lsm[:, :, :], lsm[:, :, :], prob[:, :, :], ALU.mult))
                own.settle()
                pause(dve, spare[0])
                for j in range(NT):
                    own.step(dve.max(idxf[:, 0, j, :], key[:, j, :]))
                own.settle()
                cube = [P, NT, TOPK, EXPERTS]
                own.step(dve.tensor_tensor(hot, key.unsqueeze(2).broadcast_to(cube),
                                           idxf[:, 0, :, :].unsqueeze(3).broadcast_to(cube), ALU.is_equal))
                own.settle()
                own.step(dve.tensor_tensor(hot, hot, lsm[:, :, :].unsqueeze(2).broadcast_to(cube), ALU.mult))
                own.step(dve.scalar_tensor_tensor(out=idxf[:, 1, :, :], in0=idxf[:, 0, :, :], scalar=0.0,
                                                  in1=spill_f[:, :].rearrange("p (j k) -> p j k", j=NT),
                                                  op0=ALU.is_equal, op1=ALU.mult))
                own.settle()
                own.step(dve.tensor_reduce(slot_w[:, bass.ds(NT * b, NT), :], hot, AX.X, ALU.add))
                own.step(dve.tensor_scalar(slot_idx[:, bass.ds(NT * b, NT), :], idxf[:, 0, :, :], -1.0, 0.0, ALU.add, ALU.max))
                own.step(dve.tensor_copy(tok_i[:, :], tok_f[:, :]))
                own.settle()
                own.step(dve.tensor_scalar(tok_f[:, :], tok_f[:, :], float(T), None, ALU.add))
                own.step(dve.tensor_scalar(spill_f[:, :], spill_f[:, :], float(T * TOPK), None, ALU.add))
                own.settle()
                dve.scalar_tensor_tensor(out=idx_s[:, :].rearrange("p (j k) -> p j k", j=NT), in0=idxf[:, 0, :, :],
                                         scalar=-1.0, in1=idxf[:, 1, :, :], op0=ALU.add, op1=ALU.add).then_inc(routed, 1)
            assert own.n == VECTOR_STEPS, own.n


def flat(t):
    return t.rearrange("p a b -> p (a b)")


def setup(nc, wq, wk, wv, wo, rms_w, in_w, conv_w, conv_b, xp_w, dt_w, dt_b, a_log, d_skip, router,
          consts, dmask_in, table_dram, cs, ident, half, spare, wqkv, wo_sb, in_wT, xp_wT, dt_wT, rT, dmask,
          conv_c, vecs, rms_c, a_sc, ones, xin, da, stage1, stage2, x1, prev, tok_f, spill_f, zero_i, bank):
    with ExitStack() as mem:
        def sem(name):
            return mem.enter_context(nc.semaphore(name))

        const_loaded = sem("const_loaded")
        raw_loaded = sem("raw_loaded")
        wo_loaded = sem("wo_loaded")
        weights_loaded = sem("weights_loaded")
        zeroed = sem("zeroed")
        table_cleared = sem("table_cleared")
        turned = sem("turned")
        copied = sem("copied")
        a_exp = sem("a_exp")
        a_ready = sem("a_ready")
        pads = sem("pads")

        raw = stage1[:, 0, :, :].rearrange("p s t -> p (s t)")
        raw_in = raw[:, 0:MI * CTX].rearrange("p (t d) -> p t d", t=MI)
        raw_dt = raw[:, MI * CTX:MI * CTX + MI * RANK].rearrange("p (t r) -> p t r", t=MI)
        raw2 = stage2[:, 0, :, :].rearrange("p s t -> p (s t)")
        raw_xp = raw2[0:RANK + 2 * STATE, 0:INNER]
        raw_r = raw2[0:EXPERTS, INNER:INNER + D]
        raw_vec = raw2[0:4 * MI, INNER + D:INNER + D + P]
        block = mem.enter_context(nc.Block())

        @block.sync
        def _(sp):
            sp.dma_start(cs[:, :], consts).then_inc(const_loaded, 16)
            sp.dma_start(raw_in, in_w.rearrange("(t p) d -> p t d", p=P)).then_inc(raw_loaded, 16)
            sp.dma_start(raw_dt, dt_w.rearrange("(t p) r -> p t r", p=P)).then_inc(raw_loaded, 16)
            sp.dma_start(raw_xp, xp_w).then_inc(raw_loaded, 16)
            sp.dma_start(raw_r, router).then_inc(raw_loaded, 16)
            sp.dma_start(a_sc[:, :, :], a_log.rearrange("(m p) s -> p m s", p=P)).then_inc(raw_loaded, 16)
            sp.dma_start(wo_sb[:, :, :], wo.rearrange("(k p) n -> p k n", p=P)).then_inc(wo_loaded, 16)
            for n, w in enumerate((wq, wk, wv)):
                sp.dma_start(wqkv[:, n, :, :], w.rearrange("(k p) n -> p k n", p=P)).then_inc(weights_loaded, 16)
            sp.dma_start(dmask[:, :, :], dmask_in).then_inc(weights_loaded, 16)
            wait(sp, zeroed, 1)
            sp.dma_start(table_dram[0:SLOTS, :].rearrange("(p n) a -> p (n a)", p=P), zero_i).then_inc(table_cleared, 16)
            sp.wait_ge(weights_loaded, 80)
            sp.wait_ge(table_cleared, 16)

        @block.scalar
        def _(act):
            for n, vec in enumerate((conv_b, dt_b, d_skip, rms_w)):
                act.dma_start(raw_vec[n * MI:(n + 1) * MI, :], vec.rearrange("(k p) -> k p", p=P)).then_inc(raw_loaded, 16)
            act.dma_start(conv_c[:, :, :], conv_w.rearrange("(m p) a t -> p m (a t)", p=P)).then_inc(weights_loaded, 16)
            act.wait_ge(raw_loaded, 16 * 9)
            act.activation(a_sc[:, :, :], a_sc[:, :, :], ACT.Exp).then_inc(a_exp, 1)
            for k, name in enumerate(("A0", "A1")):
                act.wait_ge(turned, k + 1)
                act.activation(in_wT[:, k, :], bank[name][:, :], ACT.Copy).then_inc(copied, 1)
            act.wait_ge(turned, 3)
            act.activation(xp_wT[:, :, :], bank["S0"][:, 0:MI * (RANK + 2 * STATE)].rearrange("p (m r) -> p m r", m=MI),
                           ACT.Copy).then_inc(copied, 1)
            act.wait_ge(turned, 4)
            act.activation(dt_wT[:, :], bank["S1"][0:RANK, :], ACT.Copy).then_inc(copied, 1)
            act.wait_ge(turned, 5)
            act.activation(rT[:, :, :], bank["Y0"][:, 0:KD * EXPERTS].rearrange("p (k e) -> p k e", k=KD), ACT.Copy)\
                .then_inc(copied, 1)
            act.wait_ge(turned, 6)
            act.activation(vecs[:, :], bank["Y1"][:, 0:4 * MI], ACT.Copy).then_inc(copied, 1)
            act.wait_ge(weights_loaded, 80)

        @block.tensor
        def _(pe):
            pe.wait_ge(const_loaded, 16)
            pe.wait_ge(raw_loaded, 16 * 9)
            for k, name in enumerate(("A0", "A1")):
                for t in range(MI):
                    ins = pe.transpose(bank[name][:, t * P:(t + 1) * P], raw_in[:, t, k * P:(k + 1) * P], ident)
                ins.then_inc(turned, 1)
            rows = RANK + 2 * STATE
            for m in range(MI):
                ins = pe.transpose(bank["S0"][:, m * rows:(m + 1) * rows], raw_xp[:, m * P:(m + 1) * P],
                                   ident[0:rows, 0:rows])
            ins.then_inc(turned, 1)
            for m in range(MI):
                ins = pe.transpose(bank["S1"][0:RANK, m * P:(m + 1) * P], raw_dt[:, m, :], ident)
            ins.then_inc(turned, 1)
            for k in range(KD):
                ins = pe.transpose(bank["Y0"][:, k * EXPERTS:(k + 1) * EXPERTS], raw_r[:, k * P:(k + 1) * P],
                                   ident[0:EXPERTS, 0:EXPERTS])
            ins.then_inc(turned, 1)
            pe.transpose(bank["Y1"][:, 0:4 * MI], raw_vec, ident[0:4 * MI, 0:4 * MI]).then_inc(turned, 1)

        @block.vector
        def _(dve):
            dve.memset(zero_i, 0).then_inc(zeroed, 1)
            dve.memset(half[:, :], -0.5)
            for s in spare:
                dve.memset(s[:, :], 1.0)
            dve.memset(ones[:, :], 1.0)
            dve.memset(prev[:, :], 0.0)
            dve.memset(da[:, :, :, 0:1], 0.0)
            dve.memset(xin[:, :, 0:TAPS - 1], 0.0).then_inc(pads, 1)
            dve.wait_ge(const_loaded, 16)
            dve.tensor_copy(tok_f[:, :], cs[:, C_TOK:C_TOK + NT])
            dve.tensor_copy(spill_f[:, :], cs[:, C_TRASH:C_TRASH + NT * TOPK])
            dve.wait_ge(a_exp, 1)
            dve.tensor_scalar(a_sc[:, :, :], a_sc[:, :, :], -1.0, None, ALU.mult).then_inc(a_ready, 1)
            dve.wait_ge(wo_loaded, 16)
            dve.wait_ge(copied, 6)
            for k in range(KD):
                ins = dve.tensor_scalar(wo_sb[:, k, :], wo_sb[:, k, :], rms_c[:, k:k + 1], None, ALU.mult)
            ins.then_inc(a_ready, 1)
            dve.wait_ge(a_ready, 2)


def experts(nc, gate_up, down, x2_dram, table_dram, ye_dram, ident, spare):
    with ExitStack() as mem:
        def sb(name, shape, dt=F32):
            return mem.enter_context(nc.sbuf_tensor(name, shape, dt))

        def ps(name):
            return mem.enter_context(nc.psum_tensor(name, [P, 512], F32))

        def sem(name):
            return mem.enter_context(nc.semaphore(name))

        H2 = HID - P
        W1 = 2 * HID
        OWN = 2 * P
        tab_i = sb("tab_i", [P, P], I32)
        tab_f = sb("tab_f", [P, P])
        tokens = sb("tokens", [P, EXPERTS, CJ], I32)
        idx = sb("idx", [P, 2, CJ], I32)
        xe = sb("xe", [P, 2, CJ, D])
        xh = sb("xh", [P, 2, KD, CAP], F32R)
        xl = sb("xl", [P, 2, KD, CAP], F32R)
        w1 = sb("w1", [P, 2, KD, W1])
        w1h = sb("w1h", [P, 2, KD, W1], F32R)
        w1l = sb("w1l", [P, 2, KD, W1], F32R)
        w2 = sb("w2", [P, 2, 2, D])
        w2h = sb("w2h", [P, 2, 2, D], F32R)
        w2l = sb("w2l", [P, 2, 2, D], F32R)
        sg = sb("sg", [P, 2, 2 * CAP])
        hid = sb("hid", [P, 2, 2 * CAP])
        hh = sb("hh", [P, 2, 2 * CAP], F32R)
        hl = sb("hl", [P, 2, CAP], F32R)
        rest = sb("rest", [P, 2, CAP], F32R)
        ye = sb("ye", [P, 2, CJ, D])
        turn_ps = [ps(f"turn{j}") for j in range(CJ)]
        low_ps = [ps(f"low{s}") for s in range(2)]
        high_ps = [ps(f"high{s}") for s in range(2)]
        out_ps = [ps(f"out{j}") for j in range(CJ)]

        table_loaded = sem("table_loaded")
        table_float = sem("table_float")
        table_turned = sem("table_turned")
        tokens_ready = sem("tokens_ready")
        idx_ready = sem("idx_ready")
        gathered = [sem(f"gathered{s}") for s in range(2)]
        w1_loaded = [sem(f"w1_loaded{s}") for s in range(2)]
        w2_loaded = [sem(f"w2_loaded{s}") for s in range(2)]
        w1h_ready = sem("w1h_ready")
        w1l_own = sem("w1l_own")
        w1l_other = sem("w1l_other")
        w2h_ready = sem("w2h_ready")
        w2l_ready = sem("w2l_ready")
        xe_turned = sem("xe_turned")
        xh_ready = sem("xh_ready")
        xl_ready = sem("xl_ready")
        low_done = sem("low_done")
        high_done = sem("high_done")
        silu_low = sem("silu_low")
        silu_high = sem("silu_high")
        hid_ready = sem("hid_ready")
        hh_ready = sem("hh_ready")
        hl_ready = sem("hl_ready")
        out_done = sem("out_done")
        ye_ready = sem("ye_ready")
        ye_stored = [sem(f"ye_stored{s}") for s in range(2)]
        block = mem.enter_context(nc.Block())

        FIRST, LOOP, END = -2, 6, EXPERTS + 3
        PAIRS = (EXPERTS - 2 - LOOP) // 2

        def pipeline(eng, step):
            for c in range(FIRST, LOOP):
                step(0, c)
            with eng.Fori(0, PAIRS) as i:
                step(i, LOOP)
                step(i, LOOP + 1)
            for c in range(LOOP + 2 * PAIRS, END):
                step(0, c)

        def expert(i, c):
            if isinstance(i, int) and not 0 <= 2 * i + c < EXPERTS:
                return None
            return 2 * i + c, c % 2, i + c // 2

        @block.sync
        def _(sp):
            sp.dma_start(tab_i[:, :], table_dram[0:SLOTS, :].rearrange("(n p) a -> n (p a)", p=P)).then_inc(table_loaded, 16)

            def load_first(e, slot, pair):
                rows = gate_up[e].rearrange("(k p) f -> p k f", p=P)
                wait(sp, w1l_own, e - 1)
                sp.dma_start(w1[:, slot, :, 0:HID], rows[:, :, 0:HID]).then_inc(w1_loaded[slot], 16)
                sp.dma_start(w1[:, slot, :, HID:OWN], rows[:, :, HID + P:]).then_inc(w1_loaded[slot], 16)
                wait(sp, w1l_other, e - 1)
                sp.dma_start(w1[:, slot, :, OWN:], rows[:, :, HID:HID + P]).then_inc(w1_loaded[slot], 16)

            def load_second(e, slot, pair):
                wait(sp, w2l_ready, e - 1)
                sp.dma_start(w2[:, slot, 0, :], down[e, 0:P, :]).then_inc(w2_loaded[slot], 16)
                for half_of in range(2):
                    sp.dma_start(w2[half_of * H2:(half_of + 1) * H2, slot, 1, :], down[e, P:, :])\
                        .then_inc(w2_loaded[slot], 16)

            def store(e, slot, pair):
                for j in range(CJ):
                    wait(sp, ye_ready, CJ * e + j + 1)
                    sp.dma_start(ye_dram.rearrange("(e j p) d -> e j p d", e=EXPERTS, p=P)[e, j], ye[:, slot, j, :])\
                        .then_inc(ye_stored[slot], 16)

            def step(i, c):
                if e := expert(i, c + 2):
                    load_first(*e)
                if e := expert(i, c + 1):
                    load_second(*e)
                if e := expert(i, c - 3):
                    store(*e)

            pipeline(sp, step)
            for s in range(2):
                sp.wait_ge(ye_stored[s], 16 * CJ * (EXPERTS // 2))

        @block.gpsimd
        def _(pool):
            def gather(e, slot, pair):
                wait(pool, xe_turned, CJ * (e - 1))
                wait(pool, gathered[slot], 16 * CJ * pair)
                pool.tensor_copy(idx[:, slot, :], tokens[:, e, :] if isinstance(e, int)
                                 else flat(tokens[:, bass.ds(e, 1), :])).then_inc(idx_ready, 1)
                wait(pool, idx_ready, e + 1)
                pause(pool, spare[1])
                for j in range(CJ):
                    pool.indirect_dma_start(xe[:, slot, j, :], None, x2_dram,
                                            bass.IndirectOffsetOnAxis(ap=idx[:, slot, j:j + 1], axis=0))\
                        .then_inc(gathered[slot], 16)

            def first_rests(e, slot, pair):
                wait(pool, w1h_ready, e + 1)
                pool.tensor_tensor(w1l[:, slot, :, 0:OWN], w1[:, slot, :, 0:OWN], w1h[:, slot, :, 0:OWN].bitcast(F32),
                                   ALU.subtract).then_inc(w1l_own, 1)

            def step(i, c):
                if e := expert(i, c + 2):
                    gather(*e)
                if e := expert(i, c + 1):
                    first_rests(*e)

            wait(pool, tokens_ready, 1)
            pipeline(pool, step)

        @block.tensor
        def _(pe):
            def turn(e, slot, pair):
                wait(pe, gathered[slot], 16 * CJ * (pair + 1))
                for j in range(CJ):
                    wait(pe, xl_ready, CJ * (e - 1) + j + 1)
                    for k in range(KD):
                        ins = pe.transpose(turn_ps[j][:, k * P:(k + 1) * P], xe[:, slot, j, k * P:(k + 1) * P], ident)
                    ins.then_inc(xe_turned, 1)

            def first_product(e, slot, pair):
                wait(pe, xl_ready, CJ * (e + 1))
                wait(pe, w1l_own, e + 1)
                wait(pe, w1l_other, e + 1)
                wait(pe, hid_ready, 2 * (e - 1))
                for dst, at, done in ((low_ps[slot][:, 0:CAP], 0, None), (low_ps[slot][:, CAP:], OWN, low_done),
                                      (high_ps[slot][:, 0:CAP], P, high_done)):
                    for k in range(KD):
                        for n, (w, x) in enumerate(((w1h, xh), (w1h, xl), (w1l, xh))):
                            ins = pe.matmul(dst, w[:, slot, k, at:at + P], x[:, slot, k, :],
                                            start=(k == 0 and n == 0), stop=(k == KD - 1 and n == 2))
                    if done:
                        ins.then_inc(done, 1)

            def second_product(e, slot, pair):
                wait(pe, hl_ready, 2 * (e + 1))
                wait(pe, hh_ready, 3 * (e + 1))
                wait(pe, w2l_ready, e + 1)
                for j in range(CJ):
                    wait(pe, ye_ready, CJ * (e - 1) + j + 1)
                    cols = slice(j * P, (j + 1) * P)
                    terms = ((hh, w2h, 0), (hh, w2l, 0), (hl, w2h, 0), (rest, w2h, 1), (rest, w2l, 1))
                    for n, (h, w, part) in enumerate(terms):
                        ins = pe.matmul(out_ps[j][:, :], h[:, slot, cols], w[:, slot, part, :],
                                        start=(n == 0), stop=(n == len(terms) - 1))
                    ins.then_inc(out_done, 1)

            def step(i, c):
                if e := expert(i, c + 1):
                    turn(*e)
                if e := expert(i, c):
                    first_product(*e)
                if e := expert(i, c - 2):
                    second_product(*e)

            pe.wait_ge(table_float, 1)
            pe.transpose(turn_ps[0][:, 0:P], tab_f[:, :], ident).then_inc(table_turned, 1)
            pe.wait_ge(tokens_ready, 1)
            pipeline(pe, step)

        @block.scalar
        def _(act):
            def round_rows(e, slot, pair):
                for j in range(CJ):
                    wait(act, xe_turned, CJ * e + j + 1)
                    wait(act, high_done, e - 1)
                    act.activation(xh[:, slot, :, j * P:(j + 1) * P], turn_ps[j][:, :].rearrange("p (k t) -> p k t", k=KD),
                                   ACT.Copy).then_inc(xh_ready, 1)

            def round_first(e, slot, pair):
                wait(act, w1_loaded[slot], 48 * (pair + 1))
                wait(act, high_done, e - 1)
                act.activation(w1h[:, slot, :, :], w1[:, slot, :, :], ACT.Copy).then_inc(w1h_ready, 1)

            def round_second(e, slot, pair):
                wait(act, w2_loaded[slot], 48 * (pair + 1))
                wait(act, out_done, CJ * (e - 1))
                act.activation(w2h[:, slot, :, :], w2[:, slot, :, :], ACT.Copy).then_inc(w2h_ready, 1)

            def gates(e, slot, pair):
                wait(act, low_done, e + 1)
                wait(act, hid_ready, 2 * (e - 1))
                act.activation(sg[:, slot, 0:CAP], low_ps[slot][:, 0:CAP], ACT.Silu).then_inc(silu_low, 1)
                wait(act, high_done, e + 1)
                act.activation(sg[P - H2:, slot, CAP:], high_ps[slot][0:H2, 0:CAP], ACT.Silu).then_inc(silu_high, 1)

            def round_hidden(e, slot, pair):
                wait(act, out_done, CJ * (e - 1))
                wait(act, hid_ready, 2 * e + 1)
                act.activation(hh[:, slot, 0:CAP], hid[:, slot, 0:CAP], ACT.Copy).then_inc(hh_ready, 1)
                wait(act, hid_ready, 2 * e + 2)
                act.activation(hh[P - H2:, slot, CAP:], hid[P - H2:, slot, CAP:], ACT.Copy).then_inc(hh_ready, 1)
                act.activation(rest[0:H2, slot, :], hid[P - H2:, slot, CAP:], ACT.Copy).then_inc(hh_ready, 1)

            def step(i, c):
                if e := expert(i, c - 1):
                    round_hidden(*e)
                if e := expert(i, c + 1):
                    round_rows(*e)
                    round_first(*e)
                if e := expert(i, c - 1):
                    round_second(*e)
                if e := expert(i, c):
                    gates(*e)

            pipeline(act, step)

        @block.vector
        def _(dve):
            def row_rests(e, slot, pair):
                for j in range(CJ):
                    cols = slice(j * P, (j + 1) * P)
                    wait(dve, xh_ready, CJ * e + j + 1)
                    dve.tensor_tensor(xl[:, slot, :, cols], turn_ps[j][:, :].rearrange("p (k t) -> p k t", k=KD),
                                      xh[:, slot, :, cols].bitcast(F32), ALU.subtract).then_inc(xl_ready, 1)

            def first_rests(e, slot, pair):
                wait(dve, w1h_ready, e + 1)
                dve.tensor_tensor(w1l[:, slot, :, OWN:], w1[:, slot, :, OWN:], w1h[:, slot, :, OWN:].bitcast(F32),
                                  ALU.subtract).then_inc(w1l_other, 1)

            def second_rests(e, slot, pair):
                wait(dve, w2h_ready, e + 1)
                dve.tensor_tensor(w2l[:, slot, :, :], w2[:, slot, :, :], w2h[:, slot, :, :].bitcast(F32), ALU.subtract)\
                    .then_inc(w2l_ready, 1)

            def gated(e, slot, pair):
                wait(dve, hl_ready, 2 * (e - 1))
                wait(dve, hh_ready, 3 * (e - 1))
                wait(dve, silu_low, e + 1)
                dve.tensor_tensor(hid[:, slot, 0:CAP], low_ps[slot][:, CAP:], sg[:, slot, 0:CAP], ALU.mult)\
                    .then_inc(hid_ready, 1)
                wait(dve, silu_high, e + 1)
                dve.tensor_tensor(hid[P - H2:, slot, CAP:], high_ps[slot][P - H2:, 0:CAP], sg[P - H2:, slot, CAP:], ALU.mult)\
                    .then_inc(hid_ready, 1)

            def hidden_rests(e, slot, pair):
                wait(dve, hh_ready, 3 * e + 1)
                dve.tensor_tensor(hl[:, slot, :], hid[:, slot, 0:CAP], hh[:, slot, 0:CAP].bitcast(F32), ALU.subtract)\
                    .then_inc(hl_ready, 1)
                wait(dve, hh_ready, 3 * e + 2)
                dve.tensor_tensor(rest[P - H2:, slot, :], hid[P - H2:, slot, CAP:], hh[P - H2:, slot, CAP:].bitcast(F32),
                                  ALU.subtract).then_inc(hl_ready, 1)

            def take_out(e, slot, pair):
                wait(dve, ye_stored[slot], 16 * CJ * pair)
                for j in range(CJ):
                    wait(dve, out_done, CJ * e + j + 1)
                    dve.tensor_copy(ye[:, slot, j, :], out_ps[j][:, :]).then_inc(ye_ready, 1)

            def step(i, c):
                if e := expert(i, c - 3):
                    take_out(*e)
                if e := expert(i, c - 1):
                    hidden_rests(*e)
                if e := expert(i, c + 1):
                    row_rests(*e)
                    first_rests(*e)
                if e := expert(i, c - 1):
                    second_rests(*e)
                if e := expert(i, c):
                    gated(*e)

            dve.wait_ge(table_loaded, 16)
            dve.tensor_copy(tab_f[:, :], tab_i[:, :]).then_inc(table_float, 1)
            dve.wait_ge(table_turned, 1)
            dve.tensor_copy(tokens[:, :, :].rearrange("p e j -> p (e j)"), turn_ps[0][:, 0:P]).then_inc(tokens_ready, 1)
            pipeline(dve, step)


def combine(nc, x2_dram, ye_dram, out, slot_idx, slot_w, half, spare):
    with ExitStack() as mem:
        def sb(name, shape, dt=F32):
            return mem.enter_context(nc.sbuf_tensor(name, shape, dt))

        def sem(name):
            return mem.enter_context(nc.semaphore(name))

        rows = sb("rows", [P, 2, TOPK, D])
        xr = sb("xr", [P, 2, D])
        even = sb("even", [P, 2, D])
        odd = sb("odd", [P, 2, D])
        stt = sb("stt", [P, 2, 6])
        mvc = sb("mvc", [P, 2, 2])
        root = sb("root", [P, 2])

        rows_gathered = [sem(f"rows_gathered{s}") for s in range(2)]
        xr_loaded = [sem(f"xr_loaded{s}") for s in range(2)]
        summed = sem("summed")
        var_ready = sem("var_ready")
        shifted = sem("var_shifted")
        root_ready = sem("root_ready")
        final = sem("final")
        out_stored = [sem(f"out_stored{s}") for s in range(2)]
        sum_steps = sem("sum_steps")
        PER = TOPK + 1
        block = mem.enter_context(nc.Block())

        @block.sync
        def _(sp):
            for t in range(TILES):
                s = t % 2
                if t >= 2:
                    sp.wait_ge(summed, t - 1)
                sp.dma_start(xr[:, s, :], x2_dram[t * P:(t + 1) * P, :]).then_inc(xr_loaded[s], 16)
                if t:
                    sp.wait_ge(final, t)
                    sp.dma_start(out.rearrange("b (t p) d -> (b t) p d", p=P)[t - 1], even[:, 1 - s, :])\
                        .then_inc(out_stored[1 - s], 16)
            sp.wait_ge(final, TILES)
            sp.dma_start(out.rearrange("b (t p) d -> (b t) p d", p=P)[TILES - 1], even[:, 1, :]).then_inc(out_stored[1], 16)
            for s in range(2):
                sp.wait_ge(out_stored[s], 16 * (TILES // 2))

        @block.gpsimd
        def _(pool):
            def root_of(t):
                s = t % 2
                pool.wait_ge(var_ready, t + 1)
                pool.tensor_scalar(root[:, s:s + 1], mvc[:, s, 1:2], 1.0, EPS, ALU.mult, ALU.add).then_inc(shifted, 1)
                pool.wait_ge(shifted, t + 1)
                pool.tensor_tensor(root[:, s:s + 1], root[:, s:s + 1], half[:, 0:1], ALU.pow).then_inc(root_ready, 1)

            for t in range(TILES):
                if t >= 2:
                    pool.wait_ge(summed, t - 1)
                for k in range(TOPK):
                    pool.indirect_dma_start(rows[:, t % 2, k, :], None, ye_dram,
                                            bass.IndirectOffsetOnAxis(ap=slot_idx[:, t, k:k + 1], axis=0))\
                        .then_inc(rows_gathered[t % 2], 16)
                if t >= 2:
                    root_of(t - 2)
            root_of(TILES - 2)
            root_of(TILES - 1)

        @block.vector
        def _(dve):
            def last_norm(t):
                s = t % 2
                dve.wait_ge(root_ready, t + 1)
                dve.tensor_scalar(even[:, s, :], even[:, s, :], mvc[:, s, 0:1], root[:, s:s + 1], ALU.subtract, ALU.mult)\
                    .then_inc(final, 1)

            for t in range(TILES):
                s = t % 2
                own = Chain(dve, sum_steps, PER * t)
                dve.wait_ge(xr_loaded[s], 16 * (t // 2 + 1))
                dve.wait_ge(rows_gathered[s], 16 * TOPK * (t // 2 + 1))
                if t >= 2:
                    dve.wait_ge(out_stored[s], 16 * (t // 2))
                for k in range(TOPK):
                    w = slot_w[:, t, k:k + 1]
                    if k == 1:
                        own.step(dve.tensor_scalar(odd[:, s, :], rows[:, s, 1, :], w, None, ALU.mult))
                        continue
                    part = odd if k % 2 else even
                    if k >= 2:
                        dve.wait_ge(sum_steps, PER * t + k - 1)
                    own.step(dve.scalar_tensor_tensor(out=part[:, s, :], in0=rows[:, s, k, :], scalar=w,
                                                      in1=xr[:, s, :] if k == 0 else part[:, s, :],
                                                      op0=ALU.mult, op1=ALU.add))
                own.settle()
                dve.tensor_tensor(even[:, s, :], even[:, s, :], odd[:, s, :], ALU.add).then_inc(summed, 1)
                dve.wait_ge(summed, t + 1)
                own.step(dve.bn_stats(stt[:, s, :], even[:, s, :]))
                own.settle()
                dve.bn_aggr(mvc[:, s, :], stt[:, s, :]).then_inc(var_ready, 1)
                if t:
                    last_norm(t - 1)
            last_norm(TILES - 1)


def constants():
    c = np.zeros((P, C_END), np.float32)
    p = np.arange(P)
    c[:, C_ID:C_ID + P] = np.eye(P)
    c[:, C_TRI:C_TRI + P] = p[:, None] < p[None, :]
    c[:, C_BD:C_BD + P] = p[:, None] // HD == p[None, :] // HD
    freq = np.float32(1 / 1024) ** np.linspace(0, 1, ROT, dtype=np.float32)
    t = np.arange(T, dtype=np.float32)
    theta = (t[:, None] * freq[None, :]).astype(np.float64).reshape(NT, P, ROT)
    cos, sin = np.cos(theta), np.sin(theta)
    for col, pair in ((C_ROTA, (cos, sin)), (C_ROTB, (sin, cos))):
        c[:, col:col + NT * 2 * ROT] = np.stack(pair, 2).transpose(1, 0, 2, 3).reshape(P, -1)
    start = 2.0 ** (-2.0 ** (-(np.log2(HEADS) - 3)))
    slopes = np.array([start * start ** i for i in range(HEADS)], np.float32)
    r = np.exp(-slopes).astype(np.float32).astype(np.float64)
    c[:, C_QD:C_QD + HEADS] = r[None, :] ** (p[:, None] + 1.0)
    c[:, C_KD:C_KD + HEADS] = r[None, :] ** (P - 1.0 - p[:, None])
    for g in range(GROUPS):
        c[:, C_RC + g] = r[g * HPG + p // HD] ** float(P)
    c[:, C_SLOT:C_SLOT + EXPERTS] = np.arange(EXPERTS) * CAP + 1
    c[:, C_TRASH:C_TRASH + NT * TOPK] = SLOTS + 1 + p[:, None] + P * np.arange(NT * TOPK)[None, :]
    c[:, C_TOK:C_TOK + NT] = p[:, None] + P * np.arange(NT)[None, :]
    diff = p[None, :] - p[:, None]
    dm = np.where(diff >= 0, r[:, None, None] ** np.maximum(diff, 0)[None], 0.0)
    dm = dm.reshape(GROUPS, HPG, P, P).transpose(2, 1, 0, 3).reshape(P, HPG, GROUPS * P)
    return c, dm.astype(np.float32)


_INS = ["x", "ctx_1024", "L0_attn_Wq", "L0_attn_Wk", "L0_attn_Wv", "L0_attn_Wo", "L0_attn_rms_w", "L0_xattn_in_proj_w",
        "L0_xattn_conv_w", "L0_xattn_conv_b", "L0_xattn_x_proj_w", "L0_xattn_dt_proj_w", "L0_xattn_dt_proj_b",
        "L0_xattn_A_log", "L0_xattn_D", "L0_ffn_router_weight", "L0_ffn_gate_up_proj", "L0_ffn_down_proj"]


def kernel(**inputs):
    import concourse.bacc as bacc
    from concourse.bass_utils import run_bass_kernel_spmd

    nc = bacc.Bacc("TRN2", target_bir_lowering=False, num_devices=1)
    arrays, args = {}, []
    table, decay = constants()
    for name, a in [(n, inputs[n]) for n in _INS] + [("table", table), ("decay", decay)]:
        a = np.ascontiguousarray(a)
        arrays[f"in_{name}"] = a
        args.append(nc.dram_tensor(f"in_{name}", a.shape, F32, kind="ExternalInput").ap())
    args.append(nc.dram_tensor("out", (B, T, D), F32, kind="ExternalOutput").ap())
    build(nc, *args)
    return run_bass_kernel_spmd(nc, [arrays], core_ids=[0]).results[0]["out"]
```

```python
from contextlib import ExitStack

import numpy as np

import concourse.bass as bass
from concourse import mybir

F32 = mybir.dt.float32
F32R = mybir.dt.float32r
I32 = mybir.dt.int32
ALU = mybir.AluOpType
ACT = mybir.ActivationFunctionType
AX = mybir.AxisListType

P = 128
B, T, D = 4, 512, 512
NT = T // P
KD = D // P
HEADS, HD = 16, 32
GROUPS = D // P
HPG = HEADS // GROUPS
ROT = HD // 4
CTX = 256
KC = CTX // P
INNER, STATE, RANK, TAPS = 512, 16, 16, 4
MI = INNER // P
NG = 4
EXPERTS, TOPK, CAP, HID = 64, 8, 256, 192
CJ = CAP // P
SLOTS = EXPERTS * CAP
NTOK = B * T
TILES = NTOK // P
EPS = 1e-5

C_ID = 0
C_TRI = C_ID + P
C_BD = C_TRI + P
C_ROTA = C_BD + P
C_ROTB = C_ROTA + NT * 2 * ROT
C_QD = C_ROTB + NT * 2 * ROT
C_KD = C_QD + HEADS
C_RC = C_KD + HEADS
C_SLOT = C_RC + GROUPS
C_TRASH = C_SLOT + EXPERTS
C_TOK = C_TRASH + NT * TOPK
C_END = C_TOK + NT

USES = {
    "A0": ["xT0", "k0", "qT0"] + [n for c in range(NT) for n in ([f"xT{c + 1}", f"k{c + 1}", f"O{c}", f"qT{c + 1}"]
                                                                 if c < NT - 1 else [f"O{c}"])],
    "A1": ["q0", "v0", "kT0"] + [n for c in range(NT) for n in ([f"q{c + 1}"] if c < NT - 1 else [])
                                 + ([f"I{c}"] if c else [])
                                 + ([f"v{c + 1}", f"kT{c + 1}"] if c < NT - 1 else [])],
    "S0": [n for c in range(NT) for n in [f"r0_{c}", f"r2_{c}"] + ([f"U{c}"] if c < NT - 1 else []) + [f"aT{c}"]]
          + ["yT0", "yT2", "x2T0", "x2T2", "logits"],
    "S1": [n for c in range(NT) for n in ([f"wo{c - 1}"] if c else []) + [f"r1_{c}", f"r3_{c}"]]
          + [f"wo{NT - 1}", "yT1", "yT3", "x2T1", "x2T3", "pos"],
    "Y0": ["ctx0", "in0", "xdbl", "dt0", "y0"],
    "Y1": ["ctx1", "in1", "dt1", "y1"],
    "Y2": ["in2", "dt2", "y2"],
    "Y3": ["in3", "dt3", "y3"],
}
BANK_OF = {use: (bank, n) for bank, uses in USES.items() for n, use in enumerate(uses)}

HEAD = 1

FRONT_STEPS = 3 * MI + 4 * MI
TURN_STEPS = 3
NORM_STEPS = 2 * NT
ROUTE_STEPS = 32
SOFT_STEPS = 2 * MI
ROOT_STEPS = 2 * NT + 1


def wait(eng, sem, value):
    if isinstance(value, int) and value <= 0:
        return
    eng.wait_ge(sem, value)


def pause(eng, spare, col=0):
    eng.tensor_tensor(spare[:, col:col + 1], spare[:, 1:2], spare[:, 1:2], ALU.mult)


class Chain:

    def __init__(self, eng, sem, base=0):
        self.eng, self.sem, self.base, self.n = eng, sem, base, 0

    def step(self, instruction):
        instruction.then_inc(self.sem, 1)
        self.n += 1

    def settle(self):
        self.eng.wait_ge(self.sem, self.base + self.n)


def build(nc, x, ctx, wq, wk, wv, wo, rms_w, in_w, conv_w, conv_b, xp_w, dt_w, dt_b, a_log, d_skip,
          router, gate_up, down, consts, dmask, out, scratch="Internal"):
    bc_dram = nc.dram_tensor("bc_rows", [B, 2 * STATE, T], F32, kind=scratch).ap()
    x2_dram = nc.dram_tensor("x2_rows", [NTOK, D], F32, kind=scratch).ap()
    table_dram = nc.dram_tensor("slot_table", [2 * SLOTS, 1], I32, kind=scratch).ap()
    ye_dram = nc.dram_tensor("expert_rows", [SLOTS, D], F32, kind=scratch).ap()

    with ExitStack() as whole:
        def keep(name, shape, dt=F32):
            return whole.enter_context(nc.sbuf_tensor(name, shape, dt))

        cs = keep("cs", [P, C_END])
        slot_idx = keep("slot_idx", [P, TILES, TOPK], I32)
        slot_w = keep("slot_w", [P, TILES, TOPK])
        half = keep("half", [P, NT])
        spare = [keep(f"spare{i}", [P, 4]) for i in range(2)]
        ident = cs[:, C_ID:C_ID + P]

        mixers(nc, x, ctx, wq, wk, wv, wo, rms_w, in_w, conv_w, conv_b, xp_w, dt_w, dt_b, a_log, d_skip,
               router, consts, dmask, bc_dram, x2_dram, table_dram, cs, ident, slot_idx, slot_w, half, spare)
        experts(nc, gate_up, down, x2_dram, table_dram, ye_dram, ident, spare)
        combine(nc, x2_dram, ye_dram, out, slot_idx, slot_w, half, spare)


def mixers(nc, x, ctx, wq, wk, wv, wo, rms_w, in_w, conv_w, conv_b, xp_w, dt_w, dt_b, a_log, d_skip,
           router, consts, dmask_in, bc_dram, x2_dram, table_dram, cs, ident, slot_idx, slot_w, half, spare):
    with ExitStack() as mem:
        def sb(name, shape, dt=F32):
            return mem.enter_context(nc.sbuf_tensor(name, shape, dt))

        def sem(name):
            return mem.enter_context(nc.semaphore(name))

        bank = {n: mem.enter_context(nc.psum_tensor(f"bank_{n}", [P, 512], F32)) for n in USES}

        wqkv = sb("wqkv", [P, 3, KD, D])
        wo_sb = sb("wo_sb", [P, KD, D])
        in_wT = sb("in_wT", [P, KC, INNER])
        xp_wT = sb("xp_wT", [P, MI, RANK + 2 * STATE])
        dt_wT = sb("dt_wT", [RANK, INNER])
        rT = sb("rT", [P, KD, EXPERTS])
        dmask = sb("dmask", [P, HPG, GROUPS * P])
        conv_c = sb("conv_c", [P, MI, TAPS])
        vecs = sb("vecs", [P, 4 * MI])
        cb, dtb, dsk, rms_c = (vecs[:, n * MI:(n + 1) * MI] for n in range(4))
        a_sc = sb("a_sc", [P, MI, STATE])
        ones = sb("ones", [P, P])

        u = sb("u", [P, MI, T])
        dt = sb("dt", [P, MI, T])
        dtu = sb("dtu", [P, MI, T])
        xin = sb("xin", [P, MI, T + TAPS - 1])
        bmat = sb("bmat", [P, 2, NG, T])
        cmat = sb("cmat", [P, 2, NG, T])
        da = sb("da", [P, 2, NG, T])
        dbu = sb("dbu", [P, 2, NG, T])
        h = sb("h", [P, NG, T])
        x_in = sb("x_in", [P, 2, D])
        xT = sb("xT", [P, KD, P])
        qk = sb("qk", [P, 2 * HEADS, HD])
        v = sb("v", [P, D])
        kdec = sb("kdec", [P, HEADS, HD])
        rot = sb("rot", [P, 2, 2 * HEADS, 2, ROT])
        qT = sb("qT", [P, GROUPS, P])
        kT = sb("kT", [P, GROUPS, P])
        pr = sb("pr", [P, HPG, GROUPS, P])
        attn = sb("attn", [P, HEADS, HD])
        aT = sb("aT", [P, KD, P])
        kv = sb("kv", [P, GROUPS, P])
        kvs = sb("kvs", [P, GROUPS, P])
        x1 = sb("x1", [P, NT, D])
        junk = sb("junk", [P, D])
        ssq = sb("ssq", [P, NT])
        rms = sb("rms", [P, NT])
        st = sb("st", [P, NT, 6])
        mv = sb("mv", [P, NT, 2])
        rstd = sb("rstd", [P, NT])
        xdbl = sb("xdbl", [RANK + 2 * STATE, T])
        prev = sb("prev", [P, EXPERTS])
        top = sb("top", [P, NT, TOPK])
        small = sb("small", [P, 4, NT])
        idxf = sb("idxf", [P, 2, NT, TOPK])
        idx_s = sb("idx_s", [P, NT * TOPK], I32)
        tok_i = sb("tok_i", [P, NT], I32)
        spill_f = sb("spill_f", [P, NT * TOPK])

        tok_f = sb("tokf", [P, NT])
        chosen = sb("chosen", [P, EXPERTS])
        ctx_sb = pr[:, :, :, :].rearrange("p a b c -> p (a b c)")[:, 0:NT * CTX].rearrange("p (t d) -> p t d", t=NT)
        ctxT = h
        zero_i = kv[:, :, :].rearrange("p a b -> p (a b)")[:, 0:SLOTS // P].bitcast(I32)
        lsm, prob = (kvs[:, :, :].rearrange("p a b -> p (a b)")[:, n * NT * EXPERTS:(n + 1) * NT * EXPERTS]
                     .rearrange("p (j e) -> p j e", j=NT) for n in range(2))
        mask, key = (aT[:, :, :].rearrange("p a b -> p (a b)")[:, n * NT * EXPERTS:(n + 1) * NT * EXPERTS]
                     .rearrange("p (j e) -> p j e", j=NT) for n in range(2))
        acc = dbu[:, 0, :, :]
        ex = dbu[:, 1, :, :]
        ln = xin[:, :, TAPS - 1:]
        lin = h
        y3 = cmat[:, 0, :, :]
        sz = bmat[:, 0, :, :]
        x2 = bmat[:, 1, :, :]
        x2T = cmat[:, 1, :, :]
        tmp = rot[:, :, :, :, :].rearrange("p a h b c -> p (a h b c)")[:, 0:D]
        tmp2 = rot[:, :, :, :, :].rearrange("p a h b c -> p (a h b c)")[:, D:2 * D]
        hot = xin[:, :, TAPS - 1:].rearrange("p j (k e) -> p j k e", k=TOPK)

        setup(nc, wq, wk, wv, wo, rms_w, in_w, conv_w, conv_b, xp_w, dt_w, dt_b, a_log, d_skip, router,
              consts, dmask_in, table_dram, cs, ident, half, spare, wqkv, wo_sb, in_wT, xp_wT, dt_wT, rT, dmask,
              conv_c, vecs, rms_c, a_sc, ones, xin, da, bmat, cmat, x1, prev, tok_f, spill_f, idx_s, tok_i, zero_i, bank)

        filled = {n: sem(f"filled_{n}") for n in USES}
        drained = {n: sem(f"drained_{n}") for n in USES}
        ctx_loaded = sem("ctx_loaded")
        x_loaded = [sem(f"x_loaded{i}") for i in range(2)]
        bc_stored = sem("bc_stored")
        b_loaded = [sem(f"b_loaded{i}") for i in range(2)]
        c_loaded = [sem(f"c_loaded{i}") for i in range(2)]
        x2_stored = sem("x2_stored")
        scattered = sem("scattered")
        spread = sem("spread")
        convolved = sem("convolved")
        u_ready = sem("u_ready")
        soft_ready = sem("soft_ready")
        dt_ready = sem("dt_ready")
        dtu_ready = sem("dtu_ready")
        da_ready = sem("da_ready")
        dbu_ready = sem("dbu_ready")
        scanned = sem("scanned")
        yc_ready = sem("yc_ready")
        y_summed = sem("y_summed")
        rotated = sem("rotated")
        kdec_ready = sem("kdec_ready")
        kv_scaled = sem("kv_scaled")
        kv_ready = sem("kv_ready")
        squared = sem("squared")
        rms_ready = sem("rms_ready")
        stats_ready = sem("stats_ready")
        rstd_ready = sem("rstd_ready")
        x1_ready = sem("x1_ready")
        sz_ready = sem("sz_ready")
        y3_ready = sem("y3_ready")
        stats2_ready = sem("stats2_ready")
        rstd2_ready = sem("rstd2_ready")
        x2_ready = sem("x2_ready")
        exped = sem("exped")
        masked = sem("masked")
        routed = sem("routed")
        front_steps = sem("front_steps")
        turn_steps = sem("turn_steps")
        norm_steps = sem("norm_steps")
        route_steps = sem("route_steps")
        soft_steps = sem("soft_steps")
        root_steps = sem("root_steps")

        def count(use, b):
            name, n = BANK_OF[use]
            return name, len(USES[name]) * b + n + 1

        def to_fill(eng, use, b):
            name, value = count(use, b)
            wait(eng, drained[name], HEAD + value - 1)
            return bank[name]

        def full(eng, use, b):
            name, value = count(use, b)
            wait(eng, filled[name], value)
            return bank[name]

        def taken(eng, use, b):
            name, value = count(use, b)
            wait(eng, drained[name], HEAD + value)

        def fill_sem(use):
            return filled[BANK_OF[use][0]]

        def drain_sem(use):
            return drained[BANK_OF[use][0]]

        SCANS = MI * (STATE // NG)

        def state_ready(eng, c, b):
            if c == 0:
                taken(eng, "U0", b)
            else:
                wait(eng, kv_ready, (NT - 2) * b + c)

        def states_summed(eng, n, b):
            g, m = divmod(n, MI)
            if g < STATE // NG - 1:
                wait(eng, y_summed, (SCANS - MI) * b + n + 1)
            else:
                full(eng, f"y{m}", b)

        block = mem.enter_context(nc.Block())

        def sequences(eng, change, unit, routing_end):
            change(None, 0)
            unit(0, 0, None)
            with eng.Fori(0, B - 1) as b:
                for c in range(1, NT):
                    unit(b, c, None)
                change(b, b + 1)
                unit(b + 1, 0, b)
            for c in range(1, NT):
                unit(B - 1, c, None)
            change(B - 1, None)
            routing_end(B - 1)

        @block.sync
        def _(sp):
            def load_x(b, c):
                if c >= 2:
                    wait(sp, stats_ready, NT * b + c - 1)
                sp.dma_start(x_in[:, c % 2, :], x[b, c * P:(c + 1) * P, :]).then_inc(x_loaded[c % 2], 16)

            def load_rows(b, g, dst, row, done):
                sp.dma_start(dst[:, g % 2, :, :], bc_dram[b, row + NG * g:row + NG * (g + 1), :].partition_broadcast(P))\
                    .then_inc(done[g % 2], 16)

            def load_b(b, g):
                load_rows(b, g, bmat, 0, b_loaded)

            def load_c(b, g):
                load_rows(b, g, cmat, STATE, c_loaded)

            def change(b, new):
                if new is not None:
                    if b is not None:
                        full(sp, f"O{NT - 1}", b)
                    sp.dma_start(ctx_sb, ctx[new].rearrange("(t p) d -> p t d", p=P)).then_inc(ctx_loaded, 16)
                    if b is not None:
                        wait(sp, stats_ready, NT * b + NT - 1)
                    load_x(new, 0)
                    if b is not None:
                        full(sp, "yT3", b)
                    load_x(new, 1)
                    taken(sp, "xdbl", new)
                    sp.dma_start(bc_dram[new], xdbl[RANK:, :]).then_inc(bc_stored, 16)
                    wait(sp, bc_stored, 16 * (new + 1))
                    load_b(new, 0)
                    load_c(new, 0)
                if b is not None:
                    full(sp, "logits", b)
                    for j in reversed(range(NT)):
                        sp.dma_start(x2_dram.rearrange("(b t p) d -> b t p d", b=B, p=P)[b, j], x2[:, j, :])\
                            .then_inc(x2_stored, 16)

            def unit(b, c, before):
                if c == 0:
                    if before is not None:
                        wait(sp, x2_stored, 16 * NT * (before + 1))
                    load_b(b, 1)
                    load_c(b, 1)
                elif c < NT - 1:
                    wait(sp, yc_ready, SCANS * b + MI * c)
                    load_b(b, c + 1)
                    load_c(b, c + 1)
                    load_x(b, c + 1)

            sequences(sp, change, unit, lambda b: None)
            sp.wait_ge(x2_stored, 16 * NT * B)
            sp.wait_ge(bc_stored, 16 * B)

        @block.tensor
        def _(pe):
            def turn_context(b):
                wait(pe, ctx_loaded, 16 * (b + 1))
                for k in range(KC):
                    ps = to_fill(pe, f"ctx{k}", b)
                    for t in range(NT):
                        ins = pe.transpose(ps[:, t * P:(t + 1) * P], ctx_sb[:, t, k * P:(k + 1) * P], ident)
                    ins.then_inc(fill_sem(f"ctx{k}"), 1)

            def project_context(b):
                for k in range(KC):
                    taken(pe, f"ctx{k}", b)
                for m in range(MI):
                    ps = to_fill(pe, f"in{m}", b)
                    for k in range(KC):
                        ins = pe.matmul(ps[:, :], in_wT[:, k, m * P:(m + 1) * P], ctxT[:, k, :],
                                        start=(k == 0), stop=(k == KC - 1))
                    ins.then_inc(fill_sem(f"in{m}"), 1)

            def project_u(b):
                ps = to_fill(pe, "xdbl", b)
                for m in range(MI):
                    wait(pe, u_ready, MI * b + m + 1)
                    ins = pe.matmul(ps[0:RANK + 2 * STATE, :], xp_wT[:, m, :], u[:, m, :],
                                    start=(m == 0), stop=(m == MI - 1))
                ins.then_inc(fill_sem("xdbl"), 1)

            def project_dt(b):
                taken(pe, "xdbl", b)
                for m in range(MI):
                    ps = to_fill(pe, f"dt{m}", b)
                    pe.matmul(ps[:, :], dt_wT[:, m * P:(m + 1) * P], xdbl[0:RANK, :], start=True, stop=True)\
                        .then_inc(fill_sem(f"dt{m}"), 1)

            def sum_states(b, g, m):
                n = MI * g + m
                if g == 0:
                    to_fill(pe, f"y{m}", b)
                wait(pe, yc_ready, SCANS * b + n + 1)
                for i in range(NG):
                    ins = pe.matmul(bank[f"Y{m}"][:, :], ident, dbu[:, n % 2, i, :],
                                    start=(g == 0 and i == 0), stop=(g == STATE // NG - 1 and i == NG - 1))
                ins.then_inc(fill_sem(f"y{m}") if g == STATE // NG - 1 else y_summed, 1)

            def turn(b, c):
                wait(pe, x_loaded[c % 2], 16 * (2 * b + c // 2 + 1))
                ps = to_fill(pe, f"xT{c}", b)
                for k in range(KD):
                    ins = pe.transpose(ps[:, k * P:(k + 1) * P], x_in[:, c % 2, k * P:(k + 1) * P], ident)
                ins.then_inc(fill_sem(f"xT{c}"), 1)

            def project(b, c, name):
                taken(pe, f"xT{c}", b)
                ps = to_fill(pe, f"{name}{c}", b)
                for k in range(KD):
                    ins = pe.matmul(ps[:, :], xT[:, k, :], wqkv[:, "qkv".index(name), k, :],
                                    start=(k == 0), stop=(k == KD - 1))
                ins.then_inc(fill_sem(f"{name}{c}"), 1)

            def turn_qk(b, c):
                wait(pe, rotated, NT * b + c + 1)
                for n, name in enumerate(("qT", "kT")):
                    ps = to_fill(pe, f"{name}{c}", b)
                    for g in range(GROUPS):
                        src = qk[:, n * HEADS + g * HPG:n * HEADS + (g + 1) * HPG, :].rearrange("p h d -> p (h d)")
                        ins = pe.transpose(ps[:, g * P:(g + 1) * P], src, ident)
                    ins.then_inc(fill_sem(f"{name}{c}"), 1)

            def scores(b, c, r):
                taken(pe, f"qT{c}", b)
                taken(pe, f"kT{c}", b)
                ps = to_fill(pe, f"r{r}_{c}", b)
                for g in range(GROUPS):
                    ins = pe.matmul(ps[:, g * P:(g + 1) * P], kT[r * HD:(r + 1) * HD, g, :],
                                    qT[r * HD:(r + 1) * HD, g, :], start=True, stop=True)
                ins.then_inc(fill_sem(f"r{r}_{c}"), 1)

            def mix_values(b, c):
                taken(pe, f"v{c}", b)
                for r in range(2, HPG):
                    taken(pe, f"r{r}_{c}", b)
                ps = to_fill(pe, f"O{c}", b)
                for hd in range(HEADS):
                    ins = pe.matmul(ps[:, hd * HD:(hd + 1) * HD], pr[:, hd % HPG, hd // HPG, :],
                                    v[:, hd * HD:(hd + 1) * HD], start=True, stop=True)
                ins.then_inc(fill_sem(f"O{c}"), 1)
                if c:
                    state_ready(pe, c - 1, b)
                    ps = to_fill(pe, f"I{c}", b)
                    for g in range(GROUPS):
                        ins = pe.matmul(ps[:, g * P:(g + 1) * P], qT[:, g, :], kv[:, g, :], start=True, stop=True)
                    ins.then_inc(fill_sem(f"I{c}"), 1)
                if c < NT - 1:
                    wait(pe, kdec_ready, (NT - 1) * b + c + 1)
                    ps = to_fill(pe, f"U{c}", b)
                    for g in range(GROUPS):
                        ins = pe.matmul(ps[:, g * P:(g + 1) * P],
                                        kdec[:, g * HPG:(g + 1) * HPG, :].rearrange("p h d -> p (h d)"),
                                        v[:, g * P:(g + 1) * P], start=True, stop=True)
                    ins.then_inc(fill_sem(f"U{c}"), 1)

            def turn_mixed(b, c):
                taken(pe, f"O{c}", b)
                if c:
                    taken(pe, f"I{c}", b)
                ps = to_fill(pe, f"aT{c}", b)
                for k in range(KD):
                    src = attn[:, k * HPG:(k + 1) * HPG, :].rearrange("p h d -> p (h d)")
                    ins = pe.transpose(ps[:, k * P:(k + 1) * P], src, ident)
                ins.then_inc(fill_sem(f"aT{c}"), 1)

            def project_out(b, c):
                taken(pe, f"aT{c}", b)
                ps = to_fill(pe, f"wo{c}", b)
                for k in range(KD):
                    ins = pe.matmul(ps[:, :], aT[:, k, :], wo_sb[:, k, :], start=(k == 0), stop=(k == KD - 1))
                ins.then_inc(fill_sem(f"wo{c}"), 1)

            def turn_back(b):
                wait(pe, y3_ready, MI * (b + 1))
                for j in range(NT):
                    ps = to_fill(pe, f"yT{j}", b)
                    for m in range(MI):
                        ins = pe.transpose(ps[:, m * P:(m + 1) * P], y3[:, m, j * P:(j + 1) * P], ident)
                    ins.then_inc(fill_sem(f"yT{j}"), 1)

            def rate_experts(b):
                for j in range(NT):
                    wait(pe, x2_ready, NT * b + j + 1)
                    ps = to_fill(pe, f"x2T{j}", b)
                    for k in range(KD):
                        ins = pe.transpose(ps[:, k * P:(k + 1) * P], x2[:, j, k * P:(k + 1) * P], ident)
                    ins.then_inc(fill_sem(f"x2T{j}"), 1)
                ps = to_fill(pe, "logits", b)
                for j in range(NT):
                    taken(pe, f"x2T{j}", b)
                    for k in range(KD):
                        ins = pe.matmul(ps[:, j * EXPERTS:(j + 1) * EXPERTS], x2T[:, j, k * P:(k + 1) * P],
                                        rT[:, k, :], start=(k == 0), stop=(k == KD - 1))
                ins.then_inc(fill_sem("logits"), 1)

            def count_places(b):
                wait(pe, masked, b + 1)
                ps = to_fill(pe, "pos", b)
                for j in range(NT):
                    dst = ps[:, j * EXPERTS:(j + 1) * EXPERTS]
                    pe.matmul(dst, cs[:, C_TRI:C_TRI + P], mask[:, j, :], start=True, stop=False)
                    for i in range(j):
                        pe.matmul(dst, ones[:, :], mask[:, i, :], start=False, stop=False)
                    ins = pe.matmul(dst, ones[:, :], prev[:, :], start=False, stop=True)
                ins.then_inc(fill_sem("pos"), 1)

            def change(b, new):
                if new is not None:
                    turn_context(new)
                if b is not None:
                    project_out(b, NT - 1)
                if new is not None:
                    project_context(new)
                    turn(new, 0)
                    project(new, 0, "q")
                    project(new, 0, "k")
                    project_u(new)
                if b is not None:
                    turn_back(b)
                if new is not None:
                    project(new, 0, "v")
                    project_dt(new)
                if b is not None:
                    rate_experts(b)
                if new is not None:
                    turn_qk(new, 0)

            def unit(b, c, before):
                scores(b, c, 0)
                sum_states(b, c, 0)
                if before is not None:
                    count_places(before)
                if c:
                    project_out(b, c - 1)
                sum_states(b, c, 1)
                scores(b, c, 1)
                scores(b, c, 2)
                if c < NT - 1:
                    turn(b, c + 1)
                    project(b, c + 1, "q")
                    sum_states(b, c, 2)
                    scores(b, c, 3)
                    project(b, c + 1, "k")
                    sum_states(b, c, 3)
                    mix_values(b, c)
                else:
                    scores(b, c, 3)
                    sum_states(b, c, 2)
                    mix_values(b, c)
                    sum_states(b, c, 3)
                if c < NT - 1:
                    project(b, c + 1, "v")
                    turn_qk(b, c + 1)
                turn_mixed(b, c)

            sequences(pe, change, unit, count_places)

        @block.scalar
        def _(act):
            def take(b, use, dst):
                act.activation(dst, full(act, use, b)[0:dst.shape[0], :], ACT.Copy).then_inc(drain_sem(use), 1)

            def softplus_parts(b, before):
                own = Chain(act, soft_steps, SOFT_STEPS * b)
                for m in range(MI):
                    own.step(act.activation(ex[:, m, :], full(act, f"dt{m}", b)[:, :], ACT.Abs, bias=dtb[:, m:m + 1]))
                if before is not None:
                    for j in range(NT):
                        take(before, f"x2T{j}", x2T[:, j, :])
                for m in range(MI):
                    wait(act, soft_steps, SOFT_STEPS * b + m + 1)
                    own.step(act.activation(ex[:, m, :], ex[:, m, :], ACT.Exp, scale=-1.0))
                for m in range(MI):
                    wait(act, soft_steps, SOFT_STEPS * b + MI + m + 1)
                    act.activation(ln[:, m, :], ex[:, m, :], ACT.Ln, bias=1.0).then_inc(soft_ready, 1)
                    act.activation(lin[:, m, :], bank[f"Y{m}"][:, :], ACT.Relu, bias=dtb[:, m:m + 1])\
                        .then_inc(drain_sem(f"dt{m}"), 1)
                assert own.n == SOFT_STEPS

            def decays(b, n):
                g, m = divmod(n, MI)
                if n < MI:
                    wait(act, dt_ready, MI * b + n + 1)
                if n >= 2:
                    wait(act, scanned, SCANS * b + n - 1)
                for i in range(NG):
                    s = NG * g + i
                    ins = act.activation(da[:, n % 2, i, 1:], dt[:, m, 1:], ACT.Exp, scale=a_sc[:, m, s:s + 1])
                ins.then_inc(da_ready, 1)

            def square(b, c):
                taken(act, f"O{c}", b)
                act.activation(junk[:, :], flat(attn[:, :, :]), ACT.Square, accum_out=ssq[:, c:c + 1]).then_inc(squared, 1)

            def change(b, new):
                if new is not None:
                    for k in range(KC):
                        take(new, f"ctx{k}", ctxT[:, k, :])
                    for m in range(MI):
                        take(new, f"in{m}", xin[:, m, TAPS - 1:])
                    take(new, "xT0", flat(xT[:, :, :]))
                if b is not None:
                    for m in range(MI):
                        wait(act, x1_ready, NT * b + m + 1)
                        if m == 0:
                            wait(act, dbu_ready, SCANS * (b + 1))
                        act.activation(sz[:, m, :], x1[:, m, :], ACT.Silu).then_inc(sz_ready, 1)
                if new is not None:
                    take(new, "q0", flat(qk[:, 0:HEADS, :]))
                    for m in range(MI):
                        wait(act, convolved, MI * new + m + 1)
                        act.activation(u[:, m, :], acc[:, m, :], ACT.Silu, bias=cb[:, m:m + 1]).then_inc(u_ready, 1)
                    take(new, "k0", flat(qk[:, HEADS:, :]))
                    if b is not None:
                        wait(act, bc_stored, 16 * new)
                    take(new, "xdbl", xdbl[:, :])
                    take(new, "v0", v[:, :])
                    softplus_parts(new, b)
                elif b is not None:
                    for j in range(NT):
                        take(b, f"x2T{j}", x2T[:, j, :])
                if new is not None:
                    take(new, "qT0", flat(qT[:, :, :]))
                    take(new, "kT0", flat(kT[:, :, :]))
                    decays(new, 0)
                if b is not None:
                    taken(act, "logits", b)
                    act.activation(lsm, lsm, ACT.Exp).then_inc(exped, 1)

            def unit(b, c, before):
                for n in range(1, MI):
                    decays(b, MI * c + n)
                if c < NT - 1:
                    take(b, f"xT{c + 1}", flat(xT[:, :, :]))
                    take(b, f"q{c + 1}", flat(qk[:, 0:HEADS, :]))
                    decays(b, MI * (c + 1))
                    wait(act, kdec_ready, (NT - 1) * b + c + 1)
                    take(b, f"k{c + 1}", flat(qk[:, HEADS:, :]))
                    take(b, f"v{c + 1}", v[:, :])
                    take(b, f"qT{c + 1}", flat(qT[:, :, :]))
                    take(b, f"kT{c + 1}", flat(kT[:, :, :]))
                square(b, c)
                if before is not None:
                    wait(act, routed, HEAD + before + 1)
                take(b, f"aT{c}", flat(aT[:, :, :]))

            sequences(act, change, unit, lambda b: None)

        @block.gpsimd
        def _(pool):
            def root(b, k, dst, src, scale, done):
                own = Chain(pool, root_steps, ROOT_STEPS * b + k)
                pause(pool, spare[1])
                own.step(pool.tensor_scalar(dst, src, scale, EPS, ALU.mult, ALU.add))
                own.settle()
                pool.tensor_tensor(dst, dst, half[:, 0:dst.shape[1]], ALU.pow).then_inc(done, 1)

            def mixed_root(b, c):
                wait(pool, squared, NT * b + c + 1)
                root(b, 2 * c, rms[:, c:c + 1], ssq[:, c:c + 1], 1.0 / D, rms_ready)

            def norm_root(b, c):
                wait(pool, stats_ready, NT * b + c + 1)
                root(b, 2 * c + 1, rstd[:, c:c + 1], mv[:, c, 1:2], 1.0, rstd_ready)

            def inputs(b, n):
                g, m = divmod(n, MI)
                wait(pool, b_loaded[g % 2], 32 * b + 16 * (g // 2 + 1))
                if n >= 2:
                    states_summed(pool, n - 2, b)
                pool.tensor_tensor(dbu[:, n % 2, :, :], bmat[:, g % 2, :, :],
                                   dtu[:, m, :].unsqueeze(1).broadcast_to([P, NG, T]), ALU.mult).then_inc(dbu_ready, 1)

            def scatter(b, first, end):
                if first == 0:
                    wait(pool, routed, HEAD + b)
                    pause(pool, spare[1], 3)
                for n in range(first, min(end, NT * TOPK)):
                    j = n // TOPK
                    pool.indirect_dma_start(table_dram, bass.IndirectOffsetOnAxis(ap=idx_s[:, n:n + 1], axis=0),
                                            tok_i[:, j:j + 1], None).then_inc(scattered, 16)

            def scatters_over(b):
                wait(pool, scattered, 16 * NT * TOPK * (b + 1))
                wait(pool, spread, HEAD + b)
                pool.tensor_tensor(spare[1][:, 2:3], spare[1][:, 1:2], spare[1][:, 1:2], ALU.mult).then_inc(spread, 1)

            def change(b, new):
                if b is not None:
                    mixed_root(b, NT - 1)
                    norm_root(b, NT - 1)
                    wait(pool, stats2_ready, NT * (b + 1))
                    wait(pool, x1_ready, NT * (b + 1))
                    root(b, 2 * NT, rstd[:, :], mv[:, :, 1], 1.0, rstd2_ready)
                if new is not None:
                    if b is not None:
                        wait(pool, dbu_ready, SCANS * new)
                    for m in range(MI):
                        wait(pool, dt_ready, MI * new + m + 1)
                        pool.tensor_tensor(dtu[:, m, :], dt[:, m, :], u[:, m, :], ALU.mult).then_inc(dtu_ready, 1)
                        if m == 0:
                            wait(pool, dtu_ready, MI * new + 1)
                            inputs(new, 0)
                    wait(pool, dtu_ready, MI * (new + 1))

            def unit(b, c, before):
                for m in range(MI):
                    if c or m:
                        inputs(b, MI * c + m)
                    if m == 1 and c < NT - 1:
                        wait(pool, rotated, NT * b + c + 1)
                        if c:
                            full(pool, f"U{c - 1}", b)
                        pool.tensor_tensor(kdec[:, :, :], qk[:, HEADS:, :],
                                           cs[:, C_KD:C_KD + HEADS].unsqueeze(2).broadcast_to([P, HEADS, HD]),
                                           ALU.mult).then_inc(kdec_ready, 1)
                    if m == 1 and c:
                        mixed_root(b, c - 1)
                    if m == 1 and 1 <= c < NT - 1:
                        state_ready(pool, c - 1, b)
                        pool.tensor_tensor(kvs[:, :, :], kv[:, :, :],
                                           cs[:, C_RC:C_RC + GROUPS].unsqueeze(2).broadcast_to([P, GROUPS, P]),
                                           ALU.mult).then_inc(kv_scaled, 1)
                    if m == 2 and c:
                        norm_root(b, c - 1)
                    if c:
                        at = MI * (c - 1) + m
                        scatter(b, EACH * at, EACH * (at + 1))
                if c == NT - 1:
                    scatters_over(b)

            EACH = -(-NT * TOPK // (MI * (NT - 1)))
            sequences(pool, change, unit, lambda b: scatter(B, 0, NT * TOPK))
            pool.wait_ge(scattered, 16 * NT * TOPK * (B + 1))

        @block.vector
        def _(dve):
            for s in (*drained.values(), routed, spread):
                dve.sem_inc(s, HEAD)

            def convolve(b):
                own = Chain(dve, front_steps, FRONT_STEPS * b)
                for t in range(TAPS):
                    for m in range(MI):
                        src = xin[:, m, t:t + T]
                        if t == 0:
                            taken(dve, f"in{m}", b)
                            own.step(dve.tensor_scalar(acc[:, m, :], src, conv_c[:, m, 0:1], None, ALU.mult))
                            continue
                        if m == 0:
                            own.settle()
                        ins = dve.scalar_tensor_tensor(out=acc[:, m, :], in0=src, scalar=conv_c[:, m, t:t + 1],
                                                       in1=acc[:, m, :], op0=ALU.mult, op1=ALU.add)
                        if t < TAPS - 1:
                            own.step(ins)
                        else:
                            ins.then_inc(convolved, 1)
                return own

            def softplus(b, own):
                for m in range(MI):
                    e, d = ex[:, m, :], dt[:, m, :]
                    wait(dve, soft_ready, MI * b + m + 1)
                    own.step(dve.tensor_scalar(d, e, 1.0, None, ALU.add))
                    own.settle()
                    own.step(dve.scalar_tensor_tensor(out=d, in0=d, scalar=1.0, in1=e, op0=ALU.subtract, op1=ALU.subtract))
                    own.settle()
                    own.step(dve.tensor_tensor(d, ln[:, m, :], d, ALU.subtract))
                    own.settle()
                    own.step(dve.scalar_tensor_tensor(out=d, in0=d, scalar=0.0, in1=e, op0=ALU.max, op1=ALU.min))
                    own.settle()
                    taken(dve, f"dt{m}", b)
                    dve.tensor_tensor(d, lin[:, m, :], d, ALU.add).then_inc(dt_ready, 1)
                assert own.n == FRONT_STEPS, own.n

            def scan(b, n):
                g, m = divmod(n, MI)
                if n:
                    wait(dve, yc_ready, SCANS * b + n)
                else:
                    wait(dve, dt_ready, MI * (b + 1))
                wait(dve, da_ready, SCANS * b + n + 1)
                wait(dve, dbu_ready, SCANS * b + n + 1)
                dve.tensor_tensor_scan(h[:, :, :].rearrange("p s t -> p (s t)"),
                                       da[:, n % 2, :, :].rearrange("p s t -> p (s t)"),
                                       dbu[:, n % 2, :, :].rearrange("p s t -> p (s t)"),
                                       0.0, ALU.mult, ALU.add).then_inc(scanned, 1)
                wait(dve, scanned, SCANS * b + n + 1)
                if m == 0:
                    wait(dve, c_loaded[g % 2], 32 * b + 16 * (g // 2 + 1))
                dve.tensor_tensor(dbu[:, n % 2, :, :], h[:, :, :], cmat[:, g % 2, :, :], ALU.mult).then_inc(yc_ready, 1)

            def rotate(b, c, before=None):
                taken(dve, f"q{c}", b)
                taken(dve, f"k{c}", b)
                if c >= 3:
                    taken(dve, f"O{c - 2}", b)
                    state_ready(dve, c - 2, b)
                if before is not None:
                    taken(dve, f"O{NT - 1}", before)
                own = Chain(dve, turn_steps, TURN_STEPS * (NT * b + c))
                pair = [P, 2 * HEADS, 2, ROT]
                for n, (part, col) in enumerate(((0, C_ROTA), (HD // 2, C_ROTB))):
                    table = cs[:, col + c * 2 * ROT:col + (c + 1) * 2 * ROT].rearrange("p (a r) -> p a r", a=2)
                    own.step(dve.tensor_tensor(rot[:, n, :, :, :], qk[:, :, part:part + ROT].unsqueeze(2).broadcast_to(pair),
                                               table.unsqueeze(1).broadcast_to(pair), ALU.mult))
                own.settle()
                own.step(dve.tensor_tensor(qk[:, :, 0:ROT], rot[:, 0, :, 0, :], rot[:, 1, :, 0, :], ALU.add))
                dve.tensor_tensor(qk[:, :, HD // 2:HD // 2 + ROT], rot[:, 1, :, 1, :], rot[:, 0, :, 1, :], ALU.subtract)\
                    .then_inc(rotated, 1)
                assert own.n == TURN_STEPS

            def mask_scores(b, c, r):
                use = f"r{r}_{c}"
                dve.tensor_tensor(pr[:, r, :, :].rearrange("p g c -> p (g c)"), full(dve, use, b)[:, :], dmask[:, r, :],
                                  ALU.mult).then_inc(drain_sem(use), 1)

            def mixed_heads(b, c):
                if c == 0:
                    dve.tensor_copy(flat(attn[:, :, :]), full(dve, "O0", b)[:, :]).then_inc(drain_sem("O0"), 1)
                else:
                    inter = full(dve, f"I{c}", b)
                    full(dve, f"aT{c - 1}", b)
                    wait(dve, squared, NT * b + c)
                    wait(dve, rotated, NT * b + min(c + 1, NT - 1) + 1)
                    dve.tensor_tensor(tmp.rearrange("p (h d) -> p h d", h=HEADS),
                                      inter[:, :].rearrange("p (h d) -> p h d", h=HEADS),
                                      cs[:, C_QD:C_QD + HEADS].unsqueeze(2).broadcast_to([P, HEADS, HD]), ALU.mult)\
                        .then_inc(drain_sem(f"I{c}"), 1)
                    taken(dve, f"I{c}", b)
                    dve.tensor_tensor(flat(attn[:, :, :]), full(dve, f"O{c}", b)[:, :], tmp, ALU.add)\
                        .then_inc(drain_sem(f"O{c}"), 1)
                if c < NT - 1:
                    update = full(dve, f"U{c}", b)[:, :].rearrange("p (g e) -> p g e", g=GROUPS)
                    blocks = cs[:, C_BD:C_BD + P].unsqueeze(1).broadcast_to([P, GROUPS, P])
                    dst = kv[:, :, :] if c == 0 else tmp2.rearrange("p (g e) -> p g e", g=GROUPS)
                    dve.tensor_tensor(dst, update, blocks, ALU.mult).then_inc(drain_sem(f"U{c}"), 1)
                    if c:
                        wait(dve, kv_scaled, (NT - 2) * b + c)
                        taken(dve, f"U{c}", b)
                        dve.tensor_tensor(kv[:, :, :], kvs[:, :, :], dst, ALU.add).then_inc(kv_ready, 1)

            def add_attention(b, c):
                own = Chain(dve, norm_steps, NORM_STEPS * b + c)
                wait(dve, rms_ready, NT * b + c + 1)
                wait(dve, x_loaded[c % 2], 16 * (2 * b + c // 2 + 1))
                dve.scalar_tensor_tensor(out=x1[:, c, :], in0=full(dve, f"wo{c}", b)[:, :], scalar=rms[:, c:c + 1],
                                         in1=x_in[:, c % 2, :], op0=ALU.mult, op1=ALU.add).then_inc(drain_sem(f"wo{c}"), 1)
                taken(dve, f"wo{c}", b)
                own.step(dve.bn_stats(st[:, c, :], x1[:, c, :]))
                own.settle()
                pause(dve, spare[0])
                dve.bn_aggr(mv[:, c, :], st[:, c, :]).then_inc(stats_ready, 1)

            def normalise(dst, c, done):
                dve.tensor_scalar(dst[:, c, :], dst[:, c, :], mv[:, c, 0:1], rstd[:, c:c + 1], ALU.subtract, ALU.mult)\
                    .then_inc(done, 1)

            def first_norm(b, c):
                wait(dve, stats_ready, NT * b + c + 1)
                wait(dve, rstd_ready, NT * b + c + 1)
                normalise(x1, c, x1_ready)

            def skip_path(b):
                for m in range(MI):
                    dve.scalar_tensor_tensor(out=y3[:, m, :], in0=u[:, m, :], scalar=dsk[:, m:m + 1],
                                             in1=full(dve, f"y{m}", b)[:, :], op0=ALU.mult, op1=ALU.add)\
                        .then_inc(drain_sem(f"y{m}"), 1)

            def gate(b):
                for m in range(MI):
                    taken(dve, f"y{m}", b)
                    wait(dve, sz_ready, MI * b + m + 1)
                    dve.tensor_tensor(y3[:, m, :], y3[:, m, :], sz[:, m, :], ALU.mult).then_inc(y3_ready, 1)

            def second_norm(b):
                own = Chain(dve, norm_steps, NORM_STEPS * b + NT)
                wait(dve, x1_ready, NT * (b + 1))
                for j in range(NT):
                    dve.tensor_tensor(x2[:, j, :], full(dve, f"yT{j}", b)[:, :], x1[:, j, :], ALU.add)\
                        .then_inc(drain_sem(f"yT{j}"), 1)
                    taken(dve, f"yT{j}", b)
                    own.step(dve.bn_stats(st[:, j, :], x2[:, j, :]))
                own.settle()
                assert own.n == NT
                pause(dve, spare[0])
                for j in range(NT):
                    dve.bn_aggr(mv[:, j, :], st[:, j, :]).then_inc(stats2_ready, 1)
                wait(dve, stats2_ready, NT * (b + 1))
                wait(dve, rstd2_ready, b + 1)
                for j in range(NT):
                    normalise(x2, j, x2_ready)

            def each(t):
                return t.unsqueeze(2).broadcast_to([P, NT, EXPERTS])

            def shift_logits(b):
                own = Chain(dve, route_steps, ROUTE_STEPS * b)
                logits = full(dve, "logits", b)[:, 0:NT * EXPERTS].rearrange("p (j e) -> p j e", j=NT)
                own.step(dve.tensor_reduce(small[:, 0, :], logits, AX.X, ALU.max))
                own.settle()
                dve.tensor_tensor(lsm, logits, each(small[:, 0, :]), ALU.subtract).then_inc(drain_sem("logits"), 1)
                return own

            def choose(b, own):
                wait(dve, exped, b + 1)
                own.step(dve.tensor_reduce(small[:, 1, :], lsm, AX.X, ALU.add))
                own.settle()
                own.step(dve.reciprocal(small[:, 2, :], small[:, 1, :]))
                own.settle()
                own.step(dve.tensor_tensor(prob, lsm, each(small[:, 2, :]), ALU.mult))
                own.settle()
                pause(dve, spare[0])
                for j in range(NT):
                    own.step(dve.max(top[:, j, :], prob[:, j, :]))
                own.settle()
                pause(dve, spare[0])
                for j in range(NT):
                    own.step(dve.match_replace(out=mask[:, j, :], in_to_replace=top[:, j, :], in_values=prob[:, j, :],
                                               imm_value=-1.0))
                own.step(dve.tensor_reduce(small[:, 3, :], top[:, :, :], AX.X, ALU.add))
                own.settle()
                dve.tensor_scalar(mask, mask, 0.0, None, ALU.is_lt).then_inc(masked, 1)
                own.step(dve.reciprocal(small[:, 0, :], small[:, 3, :]))
                own.settle()
                own.step(dve.tensor_tensor(lsm, prob, each(small[:, 0, :]), ALU.mult))

            def find_slots(b, own):
                own.settle()
                wait(dve, masked, b + 1)
                place = full(dve, "pos", b)[:, 0:NT * EXPERTS].rearrange("p (j e) -> p j e", j=NT)
                own.step(dve.scalar_tensor_tensor(out=prob, in0=place, scalar=float(CAP), in1=mask,
                                                  op0=ALU.is_lt, op1=ALU.mult))
                dve.tensor_tensor(key, place, cs[:, C_SLOT:C_SLOT + EXPERTS].unsqueeze(1).broadcast_to([P, NT, EXPERTS]),
                                  ALU.add).then_inc(drain_sem("pos"), 1)
                own.step(dve.tensor_reduce(chosen[:, :], mask.rearrange("p j e -> p e j"), AX.X, ALU.add))
                taken(dve, "pos", b)
                own.settle()
                own.step(dve.tensor_tensor(prev[:, :], prev[:, :], chosen[:, :], ALU.add))
                own.step(dve.tensor_tensor(key, key, prob, ALU.mult))
                own.step(dve.tensor_tensor(lsm, lsm, prob, ALU.mult))
                own.settle()
                pause(dve, spare[0])
                for j in range(NT):
                    own.step(dve.max(idxf[:, 0, j, :], key[:, j, :]))

            cube = [P, NT, TOPK, EXPERTS]

            def weigh(b, own):
                own.settle()
                own.step(dve.tensor_tensor(hot, key.unsqueeze(2).broadcast_to(cube),
                                           idxf[:, 0, :, :].unsqueeze(3).broadcast_to(cube), ALU.is_equal))
                own.settle()
                own.step(dve.tensor_tensor(hot, hot, lsm.unsqueeze(2).broadcast_to(cube), ALU.mult))

            def tell_slots(b, own):
                own.step(dve.scalar_tensor_tensor(out=idxf[:, 1, :, :], in0=idxf[:, 0, :, :], scalar=0.0,
                                                  in1=spill_f[:, :].rearrange("p (j k) -> p j k", j=NT),
                                                  op0=ALU.is_equal, op1=ALU.mult))
                own.settle()
                wait(dve, spread, HEAD + b + 1)
                own.step(dve.tensor_reduce(slot_w[:, bass.ds(NT * b, NT), :], hot, AX.X, ALU.add))
                own.step(dve.tensor_scalar(slot_idx[:, bass.ds(NT * b, NT), :], idxf[:, 0, :, :], -1.0, 0.0, ALU.add, ALU.max))
                own.step(dve.tensor_copy(tok_i[:, :], tok_f[:, :]))
                own.settle()
                own.step(dve.tensor_scalar(tok_f[:, :], tok_f[:, :], float(T), None, ALU.add))
                own.step(dve.tensor_scalar(spill_f[:, :], spill_f[:, :], float(T * TOPK), None, ALU.add))
                own.settle()
                dve.scalar_tensor_tensor(out=idx_s[:, :].rearrange("p (j k) -> p j k", j=NT), in0=idxf[:, 0, :, :],
                                         scalar=-1.0, in1=idxf[:, 1, :, :], op0=ALU.add, op1=ALU.add).then_inc(routed, 1)
                assert own.n == ROUTE_STEPS, own.n

            chain = {}

            def change(b, new):
                if b is not None:
                    skip_path(b)
                    add_attention(b, NT - 1)
                    first_norm(b, NT - 1)
                if new is not None:
                    front = convolve(new)
                if b is not None:
                    gate(b)
                    second_norm(b)
                if new is not None:
                    rotate(new, 0, b)
                    softplus(new, front)
                if b is not None:
                    chain["route"] = shift_logits(b)

            def unit(b, c, before):
                scan(b, MI * c)
                if before is not None:
                    choose(before, chain["route"])
                scan(b, MI * c + 1)
                mask_scores(b, c, 0)
                if before is not None:
                    find_slots(before, chain["route"])
                if c:
                    add_attention(b, c - 1)
                scan(b, MI * c + 2)
                mask_scores(b, c, 1)
                mask_scores(b, c, 2)
                if before is not None:
                    weigh(before, chain["route"])
                    tell_slots(before, chain["route"])
                if c == NT - 1:
                    mask_scores(b, c, 3)
                scan(b, MI * c + 3)
                if c < NT - 1:
                    mask_scores(b, c, 3)
                if c < NT - 1:
                    rotate(b, c + 1)
                if c:
                    first_norm(b, c - 1)
                mixed_heads(b, c)

            def routing_end(b):
                choose(b, chain["route"])
                find_slots(b, chain["route"])
                weigh(b, chain["route"])
                tell_slots(b, chain["route"])

            sequences(dve, change, unit, routing_end)


def flat(t):
    return t.rearrange("p a b -> p (a b)")


def setup(nc, wq, wk, wv, wo, rms_w, in_w, conv_w, conv_b, xp_w, dt_w, dt_b, a_log, d_skip, router,
          consts, dmask_in, table_dram, cs, ident, half, spare, wqkv, wo_sb, in_wT, xp_wT, dt_wT, rT, dmask,
          conv_c, vecs, rms_c, a_sc, ones, xin, da, stage1, stage2, x1, prev, tok_f, spill_f, idx_s, tok_i, zero_i, bank):
    with ExitStack() as mem:
        def sem(name):
            return mem.enter_context(nc.semaphore(name))

        const_loaded = sem("const_loaded")
        raw_loaded = sem("raw_loaded")
        wo_loaded = sem("wo_loaded")
        weights_loaded = sem("weights_loaded")
        zeroed = sem("zeroed")
        table_cleared = sem("table_cleared")
        turned = sem("turned")
        copied = sem("copied")
        a_exp = sem("a_exp")
        a_ready = sem("a_ready")
        pads = sem("pads")

        raw = stage1[:, 0, :, :].rearrange("p s t -> p (s t)")
        raw_in = raw[:, 0:MI * CTX].rearrange("p (t d) -> p t d", t=MI)
        raw_dt = raw[:, MI * CTX:MI * CTX + MI * RANK].rearrange("p (t r) -> p t r", t=MI)
        raw2 = stage2[:, 0, :, :].rearrange("p s t -> p (s t)")
        raw_xp = raw2[0:RANK + 2 * STATE, 0:INNER]
        raw_r = raw2[0:EXPERTS, INNER:INNER + D]
        raw_vec = raw2[0:4 * MI, INNER + D:INNER + D + P]
        block = mem.enter_context(nc.Block())

        @block.sync
        def _(sp):
            sp.dma_start(cs[:, :], consts).then_inc(const_loaded, 16)
            sp.dma_start(raw_in, in_w.rearrange("(t p) d -> p t d", p=P)).then_inc(raw_loaded, 16)
            sp.dma_start(raw_dt, dt_w.rearrange("(t p) r -> p t r", p=P)).then_inc(raw_loaded, 16)
            sp.dma_start(raw_xp, xp_w).then_inc(raw_loaded, 16)
            sp.dma_start(raw_r, router).then_inc(raw_loaded, 16)
            sp.dma_start(a_sc[:, :, :], a_log.rearrange("(m p) s -> p m s", p=P)).then_inc(raw_loaded, 16)
            sp.dma_start(wo_sb[:, :, :], wo.rearrange("(k p) n -> p k n", p=P)).then_inc(wo_loaded, 16)
            for n, w in enumerate((wq, wk, wv)):
                sp.dma_start(wqkv[:, n, :, :], w.rearrange("(k p) n -> p k n", p=P)).then_inc(weights_loaded, 16)
            sp.dma_start(dmask[:, :, :], dmask_in).then_inc(weights_loaded, 16)
            wait(sp, zeroed, 1)
            sp.dma_start(table_dram[0:SLOTS, :].rearrange("(p n) a -> p (n a)", p=P), zero_i).then_inc(table_cleared, 16)
            sp.wait_ge(weights_loaded, 80)
            sp.wait_ge(table_cleared, 16)

        @block.scalar
        def _(act):
            for n, vec in enumerate((conv_b, dt_b, d_skip, rms_w)):
                act.dma_start(raw_vec[n * MI:(n + 1) * MI, :], vec.rearrange("(k p) -> k p", p=P)).then_inc(raw_loaded, 16)
            act.dma_start(conv_c[:, :, :], conv_w.rearrange("(m p) a t -> p m (a t)", p=P)).then_inc(weights_loaded, 16)
            act.wait_ge(raw_loaded, 16 * 9)
            act.activation(a_sc[:, :, :], a_sc[:, :, :], ACT.Exp).then_inc(a_exp, 1)
            for k, name in enumerate(("A0", "A1")):
                act.wait_ge(turned, k + 1)
                act.activation(in_wT[:, k, :], bank[name][:, :], ACT.Copy).then_inc(copied, 1)
            act.wait_ge(turned, 3)
            act.activation(xp_wT[:, :, :], bank["S0"][:, 0:MI * (RANK + 2 * STATE)].rearrange("p (m r) -> p m r", m=MI),
                           ACT.Copy).then_inc(copied, 1)
            act.wait_ge(turned, 4)
            act.activation(dt_wT[:, :], bank["S1"][0:RANK, :], ACT.Copy).then_inc(copied, 1)
            act.wait_ge(turned, 5)
            act.activation(rT[:, :, :], bank["Y0"][:, 0:KD * EXPERTS].rearrange("p (k e) -> p k e", k=KD), ACT.Copy)\
                .then_inc(copied, 1)
            act.wait_ge(turned, 6)
            act.activation(vecs[:, :], bank["Y1"][:, 0:4 * MI], ACT.Copy).then_inc(copied, 1)
            act.wait_ge(weights_loaded, 80)

        @block.tensor
        def _(pe):
            pe.wait_ge(const_loaded, 16)
            pe.wait_ge(raw_loaded, 16 * 9)
            for k, name in enumerate(("A0", "A1")):
                for t in range(MI):
                    ins = pe.transpose(bank[name][:, t * P:(t + 1) * P], raw_in[:, t, k * P:(k + 1) * P], ident)
                ins.then_inc(turned, 1)
            rows = RANK + 2 * STATE
            for m in range(MI):
                ins = pe.transpose(bank["S0"][:, m * rows:(m + 1) * rows], raw_xp[:, m * P:(m + 1) * P],
                                   ident[0:rows, 0:rows])
            ins.then_inc(turned, 1)
            for m in range(MI):
                ins = pe.transpose(bank["S1"][0:RANK, m * P:(m + 1) * P], raw_dt[:, m, :], ident)
            ins.then_inc(turned, 1)
            for k in range(KD):
                ins = pe.transpose(bank["Y0"][:, k * EXPERTS:(k + 1) * EXPERTS], raw_r[:, k * P:(k + 1) * P],
                                   ident[0:EXPERTS, 0:EXPERTS])
            ins.then_inc(turned, 1)
            pe.transpose(bank["Y1"][:, 0:4 * MI], raw_vec, ident[0:4 * MI, 0:4 * MI]).then_inc(turned, 1)

        @block.vector
        def _(dve):
            dve.memset(zero_i, 0).then_inc(zeroed, 1)
            dve.memset(half[:, :], -0.5)
            for s in spare:
                dve.memset(s[:, :], 1.0)
            dve.memset(ones[:, :], 1.0)
            dve.memset(prev[:, :], 0.0)
            dve.memset(da[:, :, :, 0:1], 0.0)
            dve.memset(xin[:, :, 0:TAPS - 1], 0.0).then_inc(pads, 1)
            dve.wait_ge(const_loaded, 16)
            dve.tensor_copy(tok_f[:, :], cs[:, C_TOK:C_TOK + NT])
            dve.tensor_copy(spill_f[:, :], cs[:, C_TRASH:C_TRASH + NT * TOPK])
            dve.tensor_copy(tok_i[:, :], cs[:, C_TOK:C_TOK + NT])
            dve.tensor_scalar(idx_s[:, :], cs[:, C_TRASH:C_TRASH + NT * TOPK], -1.0, None, ALU.add)
            dve.wait_ge(a_exp, 1)
            dve.tensor_scalar(a_sc[:, :, :], a_sc[:, :, :], -1.0, None, ALU.mult).then_inc(a_ready, 1)
            dve.wait_ge(wo_loaded, 16)
            dve.wait_ge(copied, 6)
            for k in range(KD):
                ins = dve.tensor_scalar(wo_sb[:, k, :], wo_sb[:, k, :], rms_c[:, k:k + 1], None, ALU.mult)
            ins.then_inc(a_ready, 1)
            dve.wait_ge(a_ready, 2)


def experts(nc, gate_up, down, x2_dram, table_dram, ye_dram, ident, spare):
    with ExitStack() as mem:
        def sb(name, shape, dt=F32):
            return mem.enter_context(nc.sbuf_tensor(name, shape, dt))

        def ps(name):
            return mem.enter_context(nc.psum_tensor(name, [P, 512], F32))

        def sem(name):
            return mem.enter_context(nc.semaphore(name))

        H2 = HID - P
        W1 = 2 * HID
        OWN = 2 * P
        tab_i = sb("tab_i", [P, P], I32)
        tab_f = sb("tab_f", [P, P])
        tokens = sb("tokens", [P, EXPERTS, CJ], I32)
        idx = sb("idx", [P, 2, CJ], I32)
        xe = sb("xe", [P, 2, CJ, D])
        xh = sb("xh", [P, 2, KD, CAP], F32R)
        xl = sb("xl", [P, 2, KD, CAP], F32R)
        w1 = sb("w1", [P, 2, KD, W1])
        w1h = sb("w1h", [P, 2, KD, W1], F32R)
        w1l = sb("w1l", [P, 2, KD, W1], F32R)
        w2 = sb("w2", [P, 2, 2, D])
        w2h = sb("w2h", [P, 2, 2, D], F32R)
        w2l = sb("w2l", [P, 2, 2, D], F32R)
        sg = sb("sg", [P, 2, 2 * CAP])
        hid = sb("hid", [P, 2, 2 * CAP])
        hh = sb("hh", [P, 2, 2 * CAP], F32R)
        hl = sb("hl", [P, 2, CAP], F32R)
        rest = sb("rest", [P, 2, CAP], F32R)
        ye = sb("ye", [P, 2, CJ, D])
        turn_ps = [ps(f"turn{j}") for j in range(CJ)]
        low_ps = [ps(f"low{s}") for s in range(2)]
        high_ps = [ps(f"high{s}") for s in range(2)]
        out_ps = [ps(f"out{j}") for j in range(CJ)]

        table_loaded = sem("table_loaded")
        table_float = sem("table_float")
        table_turned = sem("table_turned")
        tokens_ready = sem("tokens_ready")
        idx_ready = sem("idx_ready")
        gathered = [sem(f"gathered{s}") for s in range(2)]
        w1_loaded = [sem(f"w1_loaded{s}") for s in range(2)]
        w2_loaded = [sem(f"w2_loaded{s}") for s in range(2)]
        w1h_ready = sem("w1h_ready")
        w1l_own = sem("w1l_own")
        w1l_other = sem("w1l_other")
        w2h_ready = sem("w2h_ready")
        w2l_ready = sem("w2l_ready")
        xe_turned = sem("xe_turned")
        xh_ready = sem("xh_ready")
        xl_ready = sem("xl_ready")
        low_done = sem("low_done")
        high_done = sem("high_done")
        silu_low = sem("silu_low")
        silu_high = sem("silu_high")
        hid_ready = sem("hid_ready")
        hh_ready = sem("hh_ready")
        hl_ready = sem("hl_ready")
        out_done = sem("out_done")
        ye_ready = sem("ye_ready")
        ye_stored = [sem(f"ye_stored{s}") for s in range(2)]
        block = mem.enter_context(nc.Block())

        FIRST, LOOP, END = -2, 6, EXPERTS + 3
        PAIRS = (EXPERTS - 2 - LOOP) // 2

        def pipeline(eng, step):
            for c in range(FIRST, LOOP):
                step(0, c)
            with eng.Fori(0, PAIRS) as i:
                step(i, LOOP)
                step(i, LOOP + 1)
            for c in range(LOOP + 2 * PAIRS, END):
                step(0, c)

        def expert(i, c):
            if isinstance(i, int) and not 0 <= 2 * i + c < EXPERTS:
                return None
            return 2 * i + c, c % 2, i + c // 2

        @block.sync
        def _(sp):
            sp.dma_start(tab_i[:, :], table_dram[0:SLOTS, :].rearrange("(n p) a -> n (p a)", p=P)).then_inc(table_loaded, 16)

            def load_first(e, slot, pair):
                rows = gate_up[e].rearrange("(k p) f -> p k f", p=P)
                wait(sp, w1l_own, e - 1)
                sp.dma_start(w1[:, slot, :, 0:HID], rows[:, :, 0:HID]).then_inc(w1_loaded[slot], 16)
                sp.dma_start(w1[:, slot, :, HID:OWN], rows[:, :, HID + P:]).then_inc(w1_loaded[slot], 16)
                wait(sp, w1l_other, e - 1)
                sp.dma_start(w1[:, slot, :, OWN:], rows[:, :, HID:HID + P]).then_inc(w1_loaded[slot], 16)

            def load_second(e, slot, pair):
                wait(sp, w2l_ready, e - 1)
                sp.dma_start(w2[:, slot, 0, :], down[e, 0:P, :]).then_inc(w2_loaded[slot], 16)
                for half_of in range(2):
                    sp.dma_start(w2[half_of * H2:(half_of + 1) * H2, slot, 1, :], down[e, P:, :])\
                        .then_inc(w2_loaded[slot], 16)

            def store(e, slot, pair):
                for j in range(CJ):
                    wait(sp, ye_ready, CJ * e + j + 1)
                    sp.dma_start(ye_dram.rearrange("(e j p) d -> e j p d", e=EXPERTS, p=P)[e, j], ye[:, slot, j, :])\
                        .then_inc(ye_stored[slot], 16)

            def step(i, c):
                if e := expert(i, c + 2):
                    load_first(*e)
                if e := expert(i, c + 1):
                    load_second(*e)
                if e := expert(i, c - 3):
                    store(*e)

            pipeline(sp, step)
            for s in range(2):
                sp.wait_ge(ye_stored[s], 16 * CJ * (EXPERTS // 2))

        @block.gpsimd
        def _(pool):
            def gather(e, slot, pair):
                wait(pool, xe_turned, CJ * (e - 1))
                wait(pool, gathered[slot], 16 * CJ * pair)
                pool.tensor_copy(idx[:, slot, :], tokens[:, e, :] if isinstance(e, int)
                                 else flat(tokens[:, bass.ds(e, 1), :])).then_inc(idx_ready, 1)
                wait(pool, idx_ready, e + 1)
                pause(pool, spare[1])
                for j in range(CJ):
                    pool.indirect_dma_start(xe[:, slot, j, :], None, x2_dram,
                                            bass.IndirectOffsetOnAxis(ap=idx[:, slot, j:j + 1], axis=0))\
                        .then_inc(gathered[slot], 16)

            def first_rests(e, slot, pair):
                wait(pool, w1h_ready, e + 1)
                pool.tensor_tensor(w1l[:, slot, :, 0:OWN], w1[:, slot, :, 0:OWN], w1h[:, slot, :, 0:OWN].bitcast(F32),
                                   ALU.subtract).then_inc(w1l_own, 1)

            def step(i, c):
                if e := expert(i, c + 2):
                    gather(*e)
                if e := expert(i, c + 1):
                    first_rests(*e)

            wait(pool, tokens_ready, 1)
            pipeline(pool, step)

        @block.tensor
        def _(pe):
            def turn(e, slot, pair):
                wait(pe, gathered[slot], 16 * CJ * (pair + 1))
                for j in range(CJ):
                    wait(pe, xl_ready, CJ * (e - 1) + j + 1)
                    for k in range(KD):
                        ins = pe.transpose(turn_ps[j][:, k * P:(k + 1) * P], xe[:, slot, j, k * P:(k + 1) * P], ident)
                    ins.then_inc(xe_turned, 1)

            def first_product(e, slot, pair):
                wait(pe, xl_ready, CJ * (e + 1))
                wait(pe, w1l_own, e + 1)
                wait(pe, w1l_other, e + 1)
                wait(pe, hid_ready, 2 * (e - 1))
                for dst, at, done in ((low_ps[slot][:, 0:CAP], 0, None), (low_ps[slot][:, CAP:], OWN, low_done),
                                      (high_ps[slot][:, 0:CAP], P, high_done)):
                    for k in range(KD):
                        for n, (w, x) in enumerate(((w1h, xh), (w1h, xl), (w1l, xh))):
                            ins = pe.matmul(dst, w[:, slot, k, at:at + P], x[:, slot, k, :],
                                            start=(k == 0 and n == 0), stop=(k == KD - 1 and n == 2))
                    if done:
                        ins.then_inc(done, 1)

            def second_product(e, slot, pair):
                wait(pe, hl_ready, 2 * (e + 1))
                wait(pe, hh_ready, 3 * (e + 1))
                wait(pe, w2l_ready, e + 1)
                for j in range(CJ):
                    wait(pe, ye_ready, CJ * (e - 1) + j + 1)
                    cols = slice(j * P, (j + 1) * P)
                    terms = ((hh, w2h, 0), (hh, w2l, 0), (hl, w2h, 0), (rest, w2h, 1), (rest, w2l, 1))
                    for n, (h, w, part) in enumerate(terms):
                        ins = pe.matmul(out_ps[j][:, :], h[:, slot, cols], w[:, slot, part, :],
                                        start=(n == 0), stop=(n == len(terms) - 1))
                    ins.then_inc(out_done, 1)

            def step(i, c):
                if e := expert(i, c + 1):
                    turn(*e)
                if e := expert(i, c):
                    first_product(*e)
                if e := expert(i, c - 2):
                    second_product(*e)

            pe.wait_ge(table_float, 1)
            pe.transpose(turn_ps[0][:, 0:P], tab_f[:, :], ident).then_inc(table_turned, 1)
            pe.wait_ge(tokens_ready, 1)
            pipeline(pe, step)

        @block.scalar
        def _(act):
            def round_rows(e, slot, pair):
                for j in range(CJ):
                    wait(act, xe_turned, CJ * e + j + 1)
                    wait(act, high_done, e - 1)
                    act.activation(xh[:, slot, :, j * P:(j + 1) * P], turn_ps[j][:, :].rearrange("p (k t) -> p k t", k=KD),
                                   ACT.Copy).then_inc(xh_ready, 1)

            def round_first(e, slot, pair):
                wait(act, w1_loaded[slot], 48 * (pair + 1))
                wait(act, high_done, e - 1)
                act.activation(w1h[:, slot, :, :], w1[:, slot, :, :], ACT.Copy).then_inc(w1h_ready, 1)

            def round_second(e, slot, pair):
                wait(act, w2_loaded[slot], 48 * (pair + 1))
                wait(act, out_done, CJ * (e - 1))
                act.activation(w2h[:, slot, :, :], w2[:, slot, :, :], ACT.Copy).then_inc(w2h_ready, 1)

            def gates(e, slot, pair):
                wait(act, low_done, e + 1)
                wait(act, hid_ready, 2 * (e - 1))
                act.activation(sg[:, slot, 0:CAP], low_ps[slot][:, 0:CAP], ACT.Silu).then_inc(silu_low, 1)
                wait(act, high_done, e + 1)
                act.activation(sg[P - H2:, slot, CAP:], high_ps[slot][0:H2, 0:CAP], ACT.Silu).then_inc(silu_high, 1)

            def round_hidden(e, slot, pair):
                wait(act, out_done, CJ * (e - 1))
                wait(act, hid_ready, 2 * e + 1)
                act.activation(hh[:, slot, 0:CAP], hid[:, slot, 0:CAP], ACT.Copy).then_inc(hh_ready, 1)
                wait(act, hid_ready, 2 * e + 2)
                act.activation(hh[P - H2:, slot, CAP:], hid[P - H2:, slot, CAP:], ACT.Copy).then_inc(hh_ready, 1)
                act.activation(rest[0:H2, slot, :], hid[P - H2:, slot, CAP:], ACT.Copy).then_inc(hh_ready, 1)

            def step(i, c):
                if e := expert(i, c - 1):
                    round_hidden(*e)
                if e := expert(i, c + 1):
                    round_rows(*e)
                    round_first(*e)
                if e := expert(i, c - 1):
                    round_second(*e)
                if e := expert(i, c):
                    gates(*e)

            pipeline(act, step)

        @block.vector
        def _(dve):
            def row_rests(e, slot, pair):
                for j in range(CJ):
                    cols = slice(j * P, (j + 1) * P)
                    wait(dve, xh_ready, CJ * e + j + 1)
                    dve.tensor_tensor(xl[:, slot, :, cols], turn_ps[j][:, :].rearrange("p (k t) -> p k t", k=KD),
                                      xh[:, slot, :, cols].bitcast(F32), ALU.subtract).then_inc(xl_ready, 1)

            def first_rests(e, slot, pair):
                wait(dve, w1h_ready, e + 1)
                dve.tensor_tensor(w1l[:, slot, :, OWN:], w1[:, slot, :, OWN:], w1h[:, slot, :, OWN:].bitcast(F32),
                                  ALU.subtract).then_inc(w1l_other, 1)

            def second_rests(e, slot, pair):
                wait(dve, w2h_ready, e + 1)
                dve.tensor_tensor(w2l[:, slot, :, :], w2[:, slot, :, :], w2h[:, slot, :, :].bitcast(F32), ALU.subtract)\
                    .then_inc(w2l_ready, 1)

            def gated(e, slot, pair):
                wait(dve, hl_ready, 2 * (e - 1))
                wait(dve, hh_ready, 3 * (e - 1))
                wait(dve, silu_low, e + 1)
                dve.tensor_tensor(hid[:, slot, 0:CAP], low_ps[slot][:, CAP:], sg[:, slot, 0:CAP], ALU.mult)\
                    .then_inc(hid_ready, 1)
                wait(dve, silu_high, e + 1)
                dve.tensor_tensor(hid[P - H2:, slot, CAP:], high_ps[slot][P - H2:, 0:CAP], sg[P - H2:, slot, CAP:], ALU.mult)\
                    .then_inc(hid_ready, 1)

            def hidden_rests(e, slot, pair):
                wait(dve, hh_ready, 3 * e + 1)
                dve.tensor_tensor(hl[:, slot, :], hid[:, slot, 0:CAP], hh[:, slot, 0:CAP].bitcast(F32), ALU.subtract)\
                    .then_inc(hl_ready, 1)
                wait(dve, hh_ready, 3 * e + 2)
                dve.tensor_tensor(rest[P - H2:, slot, :], hid[P - H2:, slot, CAP:], hh[P - H2:, slot, CAP:].bitcast(F32),
                                  ALU.subtract).then_inc(hl_ready, 1)

            def take_out(e, slot, pair):
                wait(dve, ye_stored[slot], 16 * CJ * pair)
                for j in range(CJ):
                    wait(dve, out_done, CJ * e + j + 1)
                    dve.tensor_copy(ye[:, slot, j, :], out_ps[j][:, :]).then_inc(ye_ready, 1)

            def step(i, c):
                if e := expert(i, c - 3):
                    take_out(*e)
                if e := expert(i, c - 1):
                    hidden_rests(*e)
                if e := expert(i, c + 1):
                    row_rests(*e)
                    first_rests(*e)
                if e := expert(i, c - 1):
                    second_rests(*e)
                if e := expert(i, c):
                    gated(*e)

            dve.wait_ge(table_loaded, 16)
            dve.tensor_copy(tab_f[:, :], tab_i[:, :]).then_inc(table_float, 1)
            dve.wait_ge(table_turned, 1)
            dve.tensor_copy(tokens[:, :, :].rearrange("p e j -> p (e j)"), turn_ps[0][:, 0:P]).then_inc(tokens_ready, 1)
            pipeline(dve, step)


def combine(nc, x2_dram, ye_dram, out, slot_idx, slot_w, half, spare):
    with ExitStack() as mem:
        def sb(name, shape, dt=F32):
            return mem.enter_context(nc.sbuf_tensor(name, shape, dt))

        def sem(name):
            return mem.enter_context(nc.semaphore(name))

        rows = sb("rows", [P, 2, TOPK, D])
        xr = sb("xr", [P, 2, D])
        even = sb("even", [P, 2, D])
        odd = sb("odd", [P, 2, D])
        stt = sb("stt", [P, 2, 6])
        mvc = sb("mvc", [P, 2, 2])
        root = sb("root", [P, 2])

        rows_gathered = [sem(f"rows_gathered{s}") for s in range(2)]
        xr_loaded = [sem(f"xr_loaded{s}") for s in range(2)]
        summed = sem("summed")
        var_ready = sem("var_ready")
        shifted = sem("var_shifted")
        root_ready = sem("root_ready")
        final = sem("final")
        out_stored = [sem(f"out_stored{s}") for s in range(2)]
        sum_steps = sem("sum_steps")
        PER = TOPK + 1
        block = mem.enter_context(nc.Block())

        @block.sync
        def _(sp):
            for t in range(TILES):
                s = t % 2
                if t >= 2:
                    sp.wait_ge(summed, t - 1)
                sp.dma_start(xr[:, s, :], x2_dram[t * P:(t + 1) * P, :]).then_inc(xr_loaded[s], 16)
                if t:
                    sp.wait_ge(final, t)
                    sp.dma_start(out.rearrange("b (t p) d -> (b t) p d", p=P)[t - 1], even[:, 1 - s, :])\
                        .then_inc(out_stored[1 - s], 16)
            sp.wait_ge(final, TILES)
            sp.dma_start(out.rearrange("b (t p) d -> (b t) p d", p=P)[TILES - 1], even[:, 1, :]).then_inc(out_stored[1], 16)
            for s in range(2):
                sp.wait_ge(out_stored[s], 16 * (TILES // 2))

        @block.gpsimd
        def _(pool):
            def root_of(t):
                s = t % 2
                pool.wait_ge(var_ready, t + 1)
                pool.tensor_scalar(root[:, s:s + 1], mvc[:, s, 1:2], 1.0, EPS, ALU.mult, ALU.add).then_inc(shifted, 1)
                pool.wait_ge(shifted, t + 1)
                pool.tensor_tensor(root[:, s:s + 1], root[:, s:s + 1], half[:, 0:1], ALU.pow).then_inc(root_ready, 1)

            for t in range(TILES):
                if t >= 2:
                    pool.wait_ge(summed, t - 1)
                for k in range(TOPK):
                    pool.indirect_dma_start(rows[:, t % 2, k, :], None, ye_dram,
                                            bass.IndirectOffsetOnAxis(ap=slot_idx[:, t, k:k + 1], axis=0))\
                        .then_inc(rows_gathered[t % 2], 16)
                if t >= 2:
                    root_of(t - 2)
            root_of(TILES - 2)
            root_of(TILES - 1)

        @block.vector
        def _(dve):
            def last_norm(t):
                s = t % 2
                dve.wait_ge(root_ready, t + 1)
                dve.tensor_scalar(even[:, s, :], even[:, s, :], mvc[:, s, 0:1], root[:, s:s + 1], ALU.subtract, ALU.mult)\
                    .then_inc(final, 1)

            for t in range(TILES):
                s = t % 2
                own = Chain(dve, sum_steps, PER * t)
                dve.wait_ge(xr_loaded[s], 16 * (t // 2 + 1))
                dve.wait_ge(rows_gathered[s], 16 * TOPK * (t // 2 + 1))
                if t >= 2:
                    dve.wait_ge(out_stored[s], 16 * (t // 2))
                for k in range(TOPK):
                    w = slot_w[:, t, k:k + 1]
                    if k == 1:
                        own.step(dve.tensor_scalar(odd[:, s, :], rows[:, s, 1, :], w, None, ALU.mult))
                        continue
                    part = odd if k % 2 else even
                    if k >= 2:
                        dve.wait_ge(sum_steps, PER * t + k - 1)
                    own.step(dve.scalar_tensor_tensor(out=part[:, s, :], in0=rows[:, s, k, :], scalar=w,
                                                      in1=xr[:, s, :] if k == 0 else part[:, s, :],
                                                      op0=ALU.mult, op1=ALU.add))
                own.settle()
                dve.tensor_tensor(even[:, s, :], even[:, s, :], odd[:, s, :], ALU.add).then_inc(summed, 1)
                dve.wait_ge(summed, t + 1)
                own.step(dve.bn_stats(stt[:, s, :], even[:, s, :]))
                own.settle()
                dve.bn_aggr(mvc[:, s, :], stt[:, s, :]).then_inc(var_ready, 1)
                if t:
                    last_norm(t - 1)
            last_norm(TILES - 1)


def constants():
    c = np.zeros((P, C_END), np.float32)
    p = np.arange(P)
    c[:, C_ID:C_ID + P] = np.eye(P)
    c[:, C_TRI:C_TRI + P] = p[:, None] < p[None, :]
    c[:, C_BD:C_BD + P] = p[:, None] // HD == p[None, :] // HD
    freq = np.float32(1 / 1024) ** np.linspace(0, 1, ROT, dtype=np.float32)
    t = np.arange(T, dtype=np.float32)
    theta = (t[:, None] * freq[None, :]).astype(np.float64).reshape(NT, P, ROT)
    cos, sin = np.cos(theta), np.sin(theta)
    for col, pair in ((C_ROTA, (cos, sin)), (C_ROTB, (sin, cos))):
        c[:, col:col + NT * 2 * ROT] = np.stack(pair, 2).transpose(1, 0, 2, 3).reshape(P, -1)
    start = 2.0 ** (-2.0 ** (-(np.log2(HEADS) - 3)))
    slopes = np.array([start * start ** i for i in range(HEADS)], np.float32)
    r = np.exp(-slopes).astype(np.float32).astype(np.float64)
    c[:, C_QD:C_QD + HEADS] = r[None, :] ** (p[:, None] + 1.0)
    c[:, C_KD:C_KD + HEADS] = r[None, :] ** (P - 1.0 - p[:, None])
    for g in range(GROUPS):
        c[:, C_RC + g] = r[g * HPG + p // HD] ** float(P)
    c[:, C_SLOT:C_SLOT + EXPERTS] = np.arange(EXPERTS) * CAP + 1
    c[:, C_TRASH:C_TRASH + NT * TOPK] = SLOTS + 1 + p[:, None] + P * np.arange(NT * TOPK)[None, :]
    c[:, C_TOK:C_TOK + NT] = p[:, None] + P * np.arange(NT)[None, :]
    diff = p[None, :] - p[:, None]
    dm = np.where(diff >= 0, r[:, None, None] ** np.maximum(diff, 0)[None], 0.0)
    dm = dm.reshape(GROUPS, HPG, P, P).transpose(2, 1, 0, 3).reshape(P, HPG, GROUPS * P)
    return c, dm.astype(np.float32)


_INS = ["x", "ctx_1024", "L0_attn_Wq", "L0_attn_Wk", "L0_attn_Wv", "L0_attn_Wo", "L0_attn_rms_w", "L0_xattn_in_proj_w",
        "L0_xattn_conv_w", "L0_xattn_conv_b", "L0_xattn_x_proj_w", "L0_xattn_dt_proj_w", "L0_xattn_dt_proj_b",
        "L0_xattn_A_log", "L0_xattn_D", "L0_ffn_router_weight", "L0_ffn_gate_up_proj", "L0_ffn_down_proj"]


def kernel(**inputs):
    import concourse.bacc as bacc
    from concourse.bass_utils import run_bass_kernel_spmd

    nc = bacc.Bacc("TRN2", target_bir_lowering=False, num_devices=1)
    arrays, args = {}, []
    table, decay = constants()
    for name, a in [(n, inputs[n]) for n in _INS] + [("table", table), ("decay", decay)]:
        a = np.ascontiguousarray(a)
        arrays[f"in_{name}"] = a
        args.append(nc.dram_tensor(f"in_{name}", a.shape, F32, kind="ExternalInput").ap())
    args.append(nc.dram_tensor("out", (B, T, D), F32, kind="ExternalOutput").ap())
    build(nc, *args)
    return run_bass_kernel_spmd(nc, [arrays], core_ids=[0]).results[0]["out"]
```
